# Optimizing a Trainium2 kernel written in Bass

```python
import numpy as np
import jax
import jax.numpy as jnp

def _softmax(x, axis=-1):
    return jax.nn.softmax(x, axis=axis)

def _gelu(x):
    return jax.nn.gelu(x, approximate=True)

def _silu(x):
    return jax.nn.silu(x)

def _sigmoid(x):
    return jax.nn.sigmoid(x)

def _layernorm(x, axis=-1, eps=1e-05):
    m = jnp.mean(x, axis=axis, keepdims=True)
    v = jnp.var(x, axis=axis, keepdims=True)
    return (x - m) / jnp.sqrt(v + eps)

def _scatter_add(tgt, idx, src, axis=0):
    return tgt.at[idx].add(src)

def _segment_sum(src, seg, n):
    return jax.ops.segment_sum(src, seg, n)
kernel_name = 'mk_vit_tower_cls_d1_tok_img1024_r4_600986'

def setup_inputs(seed: int=0):
    np.random.seed(seed)
    _w = jnp.asarray

    def _rec_inputs():
        import jax
        import jax.numpy as jnp
        _rk = jax.random.key(seed)
        x = -7.10856e-05 + 0.999911 * jax.random.normal(jax.random.fold_in(_rk, 1), (16, 512, 256, 4), jnp.float32)
        cls_tok = 0.02 * jax.random.normal(jax.random.fold_in(_rk, 5), (1, 1, 256), jnp.float32)
        return (x, cls_tok)
    x, cls_tok = _rec_inputs()

    def _L0_tok_setup():
        import jax, jax.numpy as jnp
        import numpy as np
        B, S, D, E = (8, 512, 256, 4)
        DE = 512
        key = jax.random.key(seed)
        k1, k2, k3, k4 = jax.random.split(key, 4)
        scale = 1.0 / np.sqrt(D)
        return {'expert_id': 0, 'freq_features': jax.random.normal(k1, (B, S, D, E), dtype=jnp.float32), 'W0': jax.random.normal(k2, (DE, D), dtype=jnp.float32) * scale, 'W1': jax.random.normal(k3, (DE, D), dtype=jnp.float32) * scale, 'Wo': jax.random.normal(k4, (D, DE), dtype=jnp.float32) * (1.0 / np.sqrt(DE))}
    _L0_tok_all = _L0_tok_setup()
    _L0_tok_in = {k: v for k, v in _L0_tok_all.items() if k in ('W0', 'W1', 'Wo')}
    del _L0_tok_all

    def _L0_attn_setup():
        import jax, jax.numpy as jnp
        import numpy as np
        B, S, H, NH = (2, 512, 256, 16)
        HD = H // NH
        SCALE = HD ** (-0.5)
        EPS = 1e-05

        def _weight_quant(w):
            scale = 1.0 / jnp.clip(jnp.mean(jnp.abs(w)), 1e-05)
            wq = jnp.clip(jnp.round(w * scale), -1.0, 1.0) / scale
            return w + jax.lax.stop_gradient(wq - w)

        def _act_quant(x):
            scale = 127.0 / jnp.clip(jnp.max(jnp.abs(x), axis=-1, keepdims=True), 1e-05)
            y = jnp.clip(jnp.round(x * scale), -128.0, 127.0) / scale
            return x + jax.lax.stop_gradient(y - x)

        def _bitlinear(x, w):
            mu = jnp.mean(x, axis=(1, 2), keepdims=True)
            var = jnp.var(x, axis=(1, 2), keepdims=True)
            x_norm = (x - mu) * jax.lax.rsqrt(var + EPS)
            return _act_quant(x_norm) @ _weight_quant(w).T
        key = jax.random.key(seed)
        kx, k1, k2, k3, k4 = jax.random.split(key, 5)
        x = jax.random.normal(kx, (B, S, H), dtype=jnp.float32)
        init = 0.02
        w_q = jax.random.normal(k1, (H, H), dtype=jnp.float32) * init
        w_k = jax.random.normal(k2, (H, H), dtype=jnp.float32) * init
        w_v = jax.random.normal(k3, (H, H), dtype=jnp.float32) * init
        w_o = jax.random.normal(k4, (H, H), dtype=jnp.float32) * init
        return {'x': x, 'w_q': w_q, 'w_k': w_k, 'w_v': w_v, 'w_o': w_o}
    _L0_attn_all = _L0_attn_setup()
    _L0_attn_in = {k: v for k, v in _L0_attn_all.items() if k in ('w_q', 'w_k', 'w_v', 'w_o')}
    del _L0_attn_all

    def _L0_ffn_setup():
        import jax, jax.numpy as jnp
        import numpy as np
        FF_DIM = 512
        TOP_K = 2
        key = jax.random.key(seed)
        k1, k2, k3, k4 = jax.random.split(key, 4)
        B, S, D, E, F = (2, 512, 256, 8, FF_DIM)
        std = 0.006
        return {'x': jax.random.normal(k1, (B, S, D), dtype=jnp.float32), 'gate_w': jax.random.normal(k2, (D, E), dtype=jnp.float32) * 0.02, 'gate_up_w': jax.random.normal(k3, (E, D, 2 * F), dtype=jnp.float32) * std, 'down_w': jax.random.normal(k4, (E, F, D), dtype=jnp.float32) * std}
    _L0_ffn_all = _L0_ffn_setup()
    _L0_ffn_in = {k: v for k, v in _L0_ffn_all.items() if k in ('gate_w', 'gate_up_w', 'down_w')}
    del _L0_ffn_all
    return {'x': x, 'cls_tok': cls_tok, 'L0_tok_W0': _L0_tok_in['W0'], 'L0_tok_W1': _L0_tok_in['W1'], 'L0_tok_Wo': _L0_tok_in['Wo'], 'L0_attn_w_q': _L0_attn_in['w_q'], 'L0_attn_w_k': _L0_attn_in['w_k'], 'L0_attn_w_v': _L0_attn_in['w_v'], 'L0_attn_w_o': _L0_attn_in['w_o'], 'L0_ffn_gate_w': _L0_ffn_in['gate_w'], 'L0_ffn_gate_up_w': _L0_ffn_in['gate_up_w'], 'L0_ffn_down_w': _L0_ffn_in['down_w']}

def reference(x, cls_tok, L0_tok_W0, L0_tok_W1, L0_tok_Wo, L0_attn_w_q, L0_attn_w_k, L0_attn_w_v, L0_attn_w_o, L0_ffn_gate_w, L0_ffn_gate_up_w, L0_ffn_down_w):
    import jax
    import jax.numpy as jnp

    def _L0_tok_ref(expert_id, freq_features, W0, W1, Wo):
        import jax, jax.numpy as jnp
        import numpy as np
        B, S, D, E = (8, 512, 256, 4)
        DE = 512
        x = freq_features[:, :, :, expert_id]
        gate = jax.nn.relu(jnp.einsum('bsd,ed->bse', x, W0))
        up = jnp.einsum('bsd,ed->bse', x, W1)
        hidden = gate * up
        out = jnp.einsum('bse,de->bsd', hidden, Wo)
        return out

    def _L0_attn_ref(x, w_q, w_k, w_v, w_o):
        import jax, jax.numpy as jnp
        import numpy as np
        B, S, H, NH = (2, 512, 256, 16)
        HD = H // NH
        SCALE = HD ** (-0.5)
        EPS = 1e-05

        def _weight_quant(w):
            scale = 1.0 / jnp.clip(jnp.mean(jnp.abs(w)), 1e-05)
            wq = jnp.clip(jnp.round(w * scale), -1.0, 1.0) / scale
            return w + jax.lax.stop_gradient(wq - w)

        def _act_quant(x):
            scale = 127.0 / jnp.clip(jnp.max(jnp.abs(x), axis=-1, keepdims=True), 1e-05)
            y = jnp.clip(jnp.round(x * scale), -128.0, 127.0) / scale
            return x + jax.lax.stop_gradient(y - x)

        def _bitlinear(x, w):
            mu = jnp.mean(x, axis=(1, 2), keepdims=True)
            var = jnp.var(x, axis=(1, 2), keepdims=True)
            x_norm = (x - mu) * jax.lax.rsqrt(var + EPS)
            return _act_quant(x_norm) @ _weight_quant(w).T
        bsz, seq_len, hidden = x.shape
        q = _bitlinear(x, w_q).reshape(bsz, seq_len, NH, HD).transpose(0, 2, 1, 3)
        k = _bitlinear(x, w_k).reshape(bsz, seq_len, NH, HD).transpose(0, 2, 1, 3)
        v = _bitlinear(x, w_v).reshape(bsz, seq_len, NH, HD).transpose(0, 2, 1, 3)
        scores = jnp.einsum('bhqd,bhkd->bhqk', q, k) * SCALE
        attn = jax.nn.softmax(scores, axis=-1)
        out = jnp.einsum('bhqk,bhkd->bhqd', attn, v)
        out = out.transpose(0, 2, 1, 3).reshape(bsz, seq_len, hidden)
        return _bitlinear(out, w_o)

    def _L0_ffn_ref(x, gate_w, gate_up_w, down_w):
        import jax, jax.numpy as jnp
        import numpy as np
        FF_DIM = 512
        TOP_K = 2
        B, S, D = x.shape
        E = gate_up_w.shape[0]
        F = down_w.shape[1]
        x_flat = x.reshape(B * S, D)
        router_logits = x_flat @ gate_w
        router_probs = jax.nn.softmax(router_logits, axis=-1)
        top_k_probs, top_k_idx = jax.lax.top_k(router_probs, TOP_K)
        top_k_probs = top_k_probs / jnp.sum(top_k_probs, axis=-1, keepdims=True)
        gate_up = jnp.einsum('nd,edh->enh', x_flat, gate_up_w)
        gate_out = gate_up[..., :F]
        up_out = gate_up[..., F:]
        hidden = jax.nn.silu(gate_out) * up_out
        expert_out = jnp.einsum('enf,efd->end', hidden, down_w)
        out_t = jnp.transpose(expert_out, (1, 0, 2))
        sel = jnp.take_along_axis(out_t, top_k_idx[:, :, None], axis=1)
        output = jnp.sum(sel * top_k_probs[:, :, None], axis=1)
        return output.reshape(B, S, D)
    h = _L0_tok_ref(0, x, L0_tok_W0, L0_tok_W1, L0_tok_Wo)
    h = jnp.concatenate([jnp.broadcast_to(cls_tok, (h.shape[0], 1, h.shape[2])), h], axis=1)
    h = h + _L0_attn_ref(_layernorm(h, axis=-1), L0_attn_w_q, L0_attn_w_k, L0_attn_w_v, L0_attn_w_o)
    h = h + _L0_ffn_ref(_layernorm(h, axis=-1), L0_ffn_gate_w, L0_ffn_gate_up_w, L0_ffn_down_w)
    return h

_drawn_inputs = setup_inputs


def setup_inputs(seed=0):
    import zlib

    import numpy as np

    out = dict(_drawn_inputs(seed))
    spreads = {}
    factors = {'cls_tok': 6.176,
     'L0_attn_w_q': 2.981,
     'L0_attn_w_k': 2.946,
     'L0_ffn_gate_w': 8.0,
     'L0_ffn_gate_up_w': 8.0,
     'L0_ffn_down_w': 8.0}
    for name, (base, spread) in spreads.items():
        noise = np.random.default_rng([zlib.crc32(name.encode()), seed]).standard_normal(out[name].shape)
        drawn = base * np.exp(spread * noise) if base else spread * noise
        out[name] = jnp.asarray(drawn.astype(out[name].dtype))
    for name, factor in factors.items():
        out[name] = (out[name] * factor).astype(out[name].dtype)
    return out
```

```python
import concourse.bass as bass
from concourse import mybir
from contextlib import ExitStack

F32 = mybir.dt.float32
BF16 = mybir.dt.bfloat16
I32 = mybir.dt.int32
ALU = mybir.AluOpType
ACT = mybir.ActivationFunctionType
AX = mybir.AxisListType

D = 256
S = 512
SEQ = S + 1
DE = 512
NH, HD = 16, 16
E, F = 8, 512
EPS = 1e-5
TB = S // 128
DC = D // 128
EC = DE // 128
FC = F // 128
NG = 4
GH = NH // NG
UNITS = TB * GH
VW = 32
PARTS = "hml"
Q_STACK = ("h", "h", "hm", "ml")
K_STACK = ("hml", "hm", "h")
QK = len("".join(Q_STACK)) * HD
MROWS = 3
MAGIC = 1.5 * 2.0 ** 23

C_ID, C_TRI = 0, 128
C_BD = 256
C_GH = C_BD + DC * NH
C_J = C_GH + NG * NH
C_JP = C_J + E
C_ROW = C_JP + E
C_CROW = C_ROW + TB
C_BASE = C_CROW + 1


def geometry(images):
    tokens = images * SEQ
    cap = -(-tokens // 128) * 128
    tiles = (2 * tokens + E * 127) // 128
    tiles = -(-tiles // Tile.UNROLL) * Tile.UNROLL
    return tokens, cap, tiles, (E - 1) * cap + tiles * 128


def constants(images):
    import numpy as np
    tokens, cap, tiles, rows = geometry(images)
    p = np.arange(128)[:, None]
    c = np.zeros((128, C_BASE + E + tiles), np.float32)
    c[:, C_ID:C_ID + 128] = np.eye(128)
    c[:, C_TRI:C_TRI + 128] = p < np.arange(128)
    h = np.arange(NH)
    for k in range(DC):
        c[:, C_BD + k * NH:C_BD + (k + 1) * NH] = h == k * (NH // DC) + p // HD
    for g in range(NG):
        c[:, C_GH + g * NH:C_GH + (g + 1) * NH] = h == g * GH + p // VW
    c[:, C_J:C_J + E] = np.arange(E)
    c[:, C_JP:C_JP + E] = np.arange(E) + E
    c[:, C_ROW:C_ROW + TB] = 1 + 128 * np.arange(TB) + p
    c[:, C_CROW] = (p * SEQ)[:, 0]
    c[:, C_BASE:C_BASE + E] = np.arange(E) * cap
    c[:, C_BASE + E:] = np.arange(tiles)
    return c


class At:

    def __init__(self, k, n=None, ok=True):
        self.k, self.n, self.ok, self.par = k, n, ok, k % 2
        self.v = k if n is None else 2 * n + k
        self.half = k // 2 if n is None else n + k // 2


def fresh(eng, at, *batches):
    if batches[0].n is None or isinstance(batches[0].n, int):
        return batches
    n = batches[0].n
    copy = eng.alloc_register(f"lap_{batches[0].k}_{at}")
    eng.reg_mov(copy, n)
    n = eng.snap(copy, min_val=n.min_val, max_val=n.max_val)
    return [At(b.k, n, b.ok) for b in batches]


def wait(eng, sem, per, b, n):
    value = b.v * per + n
    if not isinstance(value, int) or value > 0:
        eng.wait_ge(sem, value)


def bcast(ap, axis, n):
    shape = list(ap.shape)
    shape.insert(axis, n)
    return ap.unsqueeze(axis).broadcast_to(shape)


def vit_layer(nc, images, x_t, cls, w0_t, w1_t, wo_t, attn_w_t, gate_w, gate_up_w, down_w, consts, out):
    tokens, cap, tiles, list_rows = geometry(images)
    total = float(SEQ * D)
    dram = lambda name, shape, dt: nc.dram_tensor(name, shape, dt, kind="Internal").ap()
    h_dram = dram("h_dram", [images * S, D], F32)
    qk_dram = dram("qk_dram", [2, 2, NH, len(PARTS) * HD, S], BF16)
    x2_dram = dram("x2_dram", [tokens + 1, D], F32)
    list_dram = dram("list_dram", [list_rows, 2], I32)

    with ExitStack() as outer:
        sb = lambda name, shape, dt=F32: outer.enter_context(nc.sbuf_tensor(name, shape, dt))
        cst = sb("cst", [128, C_BASE + E + tiles])
        tile_row = sb("tile_row", [1, tiles], I32)
        tile_expert = sb("tile_expert", [1, tiles], I32)
        banks = [outer.enter_context(nc.psum_tensor(f"bank{k}", [128, 512], F32)) for k in range(8)]
        with ExitStack() as inner:
            token_phase(nc, inner, images, x_t, cls, w0_t, w1_t, wo_t, attn_w_t, gate_w, consts, out,
                        h_dram, qk_dram, x2_dram, list_dram, cst, tile_row, tile_expert, banks, total)
        with ExitStack() as inner:
            expert_phase(nc, inner, images, gate_up_w, down_w, out, x2_dram, list_dram,
                         cst, tile_row, tile_expert, banks)


def token_phase(nc, ctx, images, x_t, cls, w0_t, w1_t, wo_t, attn_w_t, gate_w, consts, out,
                h_dram, qk_dram, x2_dram, list_dram, cst, tile_row, tile_expert, banks, total):
    tokens, cap, tiles, list_rows = geometry(images)
    sb = lambda name, shape, dt=F32: ctx.enter_context(nc.sbuf_tensor(name, shape, dt))
    SETUP, STEPS, CLASS_TOKENS = range(3)
    sems = {}

    def s(name):
        if name not in sems:
            sems[name] = nc.alloc_semaphore(f"{name}_{stage}")
        return sems[name]

    w0 = sb("w0", [128, DC, DE])
    w1 = sb("w1", [128, DC, DE])
    wo = sb("wo", [128, EC, D])
    wq_int = sb("wq_int", [128, 4, DC, D], BF16)
    wo_cls = sb("wo_cls", [64, NG, D], BF16)
    gate_sb = sb("gate_sb", [128, DC, E])
    ones = sb("ones", [128, 128])
    ones_bf = sb("ones_bf", [128, 128], BF16)
    id_bf = sb("id_bf", [128, 128], BF16)
    tri_bf = sb("tri_bf", [128, 128], BF16)
    neg_half = sb("neg_half", [128, 8])
    w_mean = sb("w_mean", [128, 4])
    w_scale = sb("w_scale", [128, 4])
    w_fac = sb("w_fac", [128, 4])
    cls_row = sb("cls_row", [1, D])
    cls_norm = sb("cls_norm", [1, D])
    cls_stat = sb("cls_stat", [1, 6])
    cls_mv = sb("cls_mv", [1, 4])
    cls_fact = sb("cls_fact", [1, 4])
    cls_f = sb("cls_f", [128, 4])
    cls_t = sb("cls_t", [128, DC])
    identf = cst[:, C_ID:C_ID + 128]
    bd_mask = cst[:, C_BD:C_BD + DC * NH].rearrange("p (c h) -> p c h", c=DC)
    gh_mask = cst[:, C_GH:C_GH + NG * NH].rearrange("p (g h) -> p g h", g=NG)

    xt = sb("xt", [128, 2, DC, S])
    relu = sb("relu", [128, 2, S])
    hid = sb("hid", [128, EC, S])
    h_sb = sb("h_sb", [128, TB, D])
    xn = sb("xn", [128, TB, D])
    qi = sb("qi", [128, TB, D], BF16)
    xq = sb("xq", [128, DC, SEQ], BF16)
    bn1 = sb("bn1", [128, TB, 6])
    mv1 = sb("mv1", [128, TB, 2])
    ve1 = sb("ve1", [128, TB])
    rstd1 = sb("rstd1", [128, TB])
    nb1 = sb("nb1", [128, TB])
    vr1 = sb("vr1", [128, TB])
    sums1 = sb("sums1", [128, 2, TB])
    red1 = sb("red1", [128, 2])
    ms1 = sb("ms1", [128, 2])
    msq1 = sb("msq1", [128, 2])
    rs1 = sb("rs1", [128, 1])
    am1 = sb("am1", [128, TB + 1])
    am1b = sb("am1b", [128, 1])
    ax1 = sb("ax1", [128, TB + 1])
    rax1 = sb("rax1", [128, TB + 1])
    comb1 = sb("comb1", [128, TB + 1])
    aq1 = sb("aq1", [128, TB + 1])
    aqv = sb("aqv", [128, TB + 1])
    cls_q = sb("cls_q", [128, DC])
    aqb = sb("aqb", [128, S])
    fq = sb("fq", [128, DC, SEQ])
    fk = sb("fk", [128, DC, SEQ])
    rest = sb("rest", [128, DC, S])
    parts = {a + p: sb(f"part_{a}{p}", [128, DC, S], BF16) for a in "qk" for p in "hml"}
    kbd = sb("kbd", [128, DC, NH])
    qbd = sb("qbd", [128, DC, NH])
    qs = sb("qs", [QK + MROWS, NH, S], BF16)
    ks = sb("ks", [128, NH, S], BF16)
    v_sb = sb("v_sb", [128, 2, TB, NH, VW])
    vcls = sb("vcls", [128, 2, NH, VW])
    scs = sb("scs", [128, 2, (2 * TB + 1) * NH])
    cmx = sb("cmx", [128, TB * NH])
    mc = sb("mc", [128, NH])
    pci = sb("pci", [128, TB + 1, NH])
    pc = sb("pc", [128, 2, TB + 1, NH])
    mxs = sb("mxs", [128, TB, NH])
    mf = sb("mf", [128, TB, NH])
    nmp = sb("nmp", [128, TB, MROWS * GH], BF16)
    nmr = sb("nmr", [128, TB, GH])
    dsc = sb("dsc", [128, TB, NH])
    pcls = sb("pcls", [128, 2, TB, NH])
    mt_sb = sb("mt_sb", [MROWS * GH, S], BF16)
    pt = sb("pt", [128, 2, GH, S])
    pvs = sb("pvs", [128, S])
    den = sb("den", [128, TB, GH])
    rinv = sb("rinv", [128, TB, GH])
    pr = sb("pr", [128, TB, NH])
    cadd = sb("cadd", [128, TB, GH, HD])
    o_sb = sb("o_sb", [128, 2, TB, D])
    pvm = sb("pvm", [128, NG, NH])
    pv4 = sb("pv4", [128, NG])
    rc = sb("rc", [NG, GH])
    oc = sb("oc", [NG, GH, HD])
    bnc = sb("bnc", [NG, 6])
    mvc = sb("mvc", [NG, 2])
    bn2 = sb("bn2", [128, 2, 6])
    mv2 = sb("mv2", [128, 2])
    e2 = sb("e2", [128, 1])
    e2c = sb("e2c", [NG, 1])
    st2 = sb("st2", [128, 2])
    st2c = sb("st2c", [NG, 2])
    ms2 = sb("ms2", [128, 2])
    msq2 = sb("msq2", [128, 2])
    rs2 = sb("rs2", [128, 1])
    am2 = sb("am2", [128, TB + 1])
    amc = sb("amc", [NG, 1])
    ax2 = sb("ax2", [128, TB + 1])
    rax2 = sb("rax2", [128, TB + 1])
    comb2 = sb("comb2", [128, TB + 1])
    aqo = sb("aqo", [128, TB + 1])
    qi2 = sb("qi2", [128, TB, D], BF16)
    qic = sb("qic", [NG, GH * HD], BF16)
    xq2 = sb("xq2", [128, DC, S], BF16)
    xqc = sb("xqc", [64, NG], BF16)
    hw = sb("hw", [128, TB, D])
    h2c = sb("h2c", [1, D])
    bn3 = sb("bn3", [128, TB, 6])
    mv3 = sb("mv3", [128, TB, 2])
    ve3 = sb("ve3", [128, TB])
    rstd3 = sb("rstd3", [128, TB])
    nb3 = sb("nb3", [128, TB])
    x2 = sb("x2", [128, TB, D])
    x2_t = sb("x2_t", [128, DC, S])
    lg = sb("lg", [128, TB, E])
    rtmp = sb("rtmp", [128, TB, E])
    m1 = sb("m1", [128, TB])
    m2 = sb("m2", [128, TB])
    ix = sb("ix", [128, TB])
    oh = sb("oh", [128, 2, TB, E])
    picked = sb("picked", [128, TB, E], BF16)
    e21 = sb("e21", [128, TB])
    e21e = sb("e21e", [128, TB])
    wts = sb("wts", [128, 2, TB])
    pos = sb("pos", [128, TB, E])
    slot = sb("slot", [128, 2, TB])
    slot_i = sb("slot_i", [128, 2, TB], I32)
    pay = sb("pay", [128, 2, TB, 2], I32)
    run = sb("run", [128, E])
    row = sb("row", [128, TB])
    zero_row = sb("zero_row", [1, D])
    ncnt = sb("ncnt", [1, E])
    ntile = sb("ntile", [1, E])
    tend = sb("tend", [1, E])
    toff = sb("toff", [1, E])
    tstep = sb("tstep", [1, E])
    tge = sb("tge", [1, tiles])
    trow = sb("trow", [1, tiles])
    texp = sb("texp", [1, tiles])
    pads = pt[:, :, :, :].rearrange("p a g n -> p (a g n)").bitcast(I32)[:, 4 * DC * D:4 * DC * D + 2 * (list_rows // 128)] \
        .rearrange("p (r w) -> p r w", w=2)
    w_stage = pt[:, :, :, :].rearrange("p a g n -> p (a g n)")[:, 0:4 * DC * D]

    score = banks[0:2]
    scoret = banks[2:4]
    pv_bank = banks[4]
    d0, d1, d2 = banks[5:8]
    b16 = lambda bank: bank[:, :].bitcast(BF16)
    blk = lambda t: slice(t * 128, (t + 1) * 128)
    heads = lambda g: slice(g * GH, (g + 1) * GH)

    def steps(eng, body):
        def fixed(i):
            body(*[At(i + o, None, 0 <= i + o < images) for o in (1, 0, -1, -2)])
        first = 3
        pairs = max(0, (images - 2 - first) // 2)
        for i in range(-1, first):
            fixed(i)
        if pairs:
            with eng.Fori(0, pairs) as n:
                for i in range(first, first + 2):
                    body(*[At(i + o, n) for o in (1, 0, -1, -2)])
        for i in range(first + 2 * pairs, images + 2):
            fixed(i)

    def hold(eng, sem, per, b, n):
        wait(eng, sem, per, b, n)
        if b.n is not None:
            eng.sem_inc(s("held"), 1)

    def in_slot(g, P, C, W):
        st = (W, g + 2) if g < 2 else (C, g - 2)
        tg = (W, g + 1) if g < 3 else (C, 0)
        mt = (W, 3) if g == 0 else (C, g - 1)
        return st, tg, mt


    def sync_program(sp, stage):
        if stage == SETUP:
            sp.dma_start(cst[:, :], consts).then_inc(s("cst_in"), 16)
            sp.dma_start(w_stage.rearrange("p (w c n) -> p w c n", w=4, c=DC),
                         attn_w_t.rearrange("w (c p) n -> p w c n", p=128)).then_inc(s("attn_w_in"), 16)
            sp.dma_start(cls_row[:, :], cls).then_inc(s("cls_in"), 16)
            sp.dma_start(w0[:, :, :], w0_t.rearrange("(c p) n -> p c n", p=128)).then_inc(s("tok_w_in"), 16)
            sp.dma_start(w1[:, :, :], w1_t.rearrange("(c p) n -> p c n", p=128)).then_inc(s("tok_w_in"), 16)
            sp.dma_start(wo[:, :, :], wo_t.rearrange("(c p) n -> p c n", p=128)).then_inc(s("tok_w_in"), 16)
            sp.dma_start(gate_sb[:, :, :], gate_w.rearrange("(c p) n -> p c n", p=128)).then_inc(s("gate_in"), 16)

        def load_x(b, v, par):
            sp.dma_start(xt[:, par, :, :], x_t[bass.ds(v * D, D), :].rearrange("(c p) n -> p c n", p=128)) \
                .then_inc(s(f"x_in{par}"), 16)
        if stage == SETUP:
            sp.wait_ge(s("w_int"), 4)
            for g in range(NG):
                sp.dma_start(wo_cls[:, g, :], wq_int[64 * (g % 2):64 * (g % 2) + 64, 3, g // 2, :]) \
                    .then_inc(s("wo_cls_in"), 16)
            sp.wait_ge(s("pads_set"), 2)
            sp.dma_start(list_dram.rearrange("(p r) w -> p r w", p=128), pads).then_inc(s("list_init"), 16)
            sp.dma_start(x2_dram[tokens:tokens + 1, :], zero_row[:, :]).then_inc(s("list_init"), 16)

        def stack(b, g):
            hold(sp, s("pe_st"), UNITS * NG, b, UNITS * (g + 1) - UNITS * NG)
            hold(sp, s("parts_stored"), 16 * 4 * len(PARTS), b, 16 * 4 * len(PARTS))
            for a, (dst, runs) in enumerate(((qs, Q_STACK), (ks, K_STACK))):
                to = 0
                for part in runs:
                    lo, n = PARTS.index(part[0]) * HD, len(part) * HD
                    sp.dma_start(dst[to:to + n, heads(g), :],
                                 qk_dram[b.par, a, heads(g), lo:lo + n, :].rearrange("j r n -> r j n")) \
                        .then_inc(s(f"stacked{g}"), 16)
                    to += n

        def store_parts(b):
            for a in "qk":
                for n, part in enumerate(PARTS):
                    hold(sp, s(f"pool_{part}{a}" if part == "l" else f"act_{a}{part}"), 1, b, 1)
                    for f in range(DC):
                        sp.dma_start(qk_dram[b.par, "qk".index(a), f * NH // DC:(f + 1) * NH // DC, n * HD:(n + 1) * HD, :],
                                     parts[a + part][:, f, :]).then_inc(s("parts_stored"), 16)

        def maxima(b, g):
            hold(sp, s("act_mt"), NG, b, g + 1)
            sp.dma_start(qs[QK:QK + MROWS, heads(g), :], mt_sb[:, :]) \
                .then_inc(s(f"max_in{g}"), 16)

        def body(P, C, W, X):
            for g in range(NG):
                P, C, W, X = fresh(sp, g, P, C, W, X)
                st, tg, mt = in_slot(g, P, C, W)
                if mt[0].ok:
                    maxima(*mt)
                if g < 3 and C.ok:
                    stack(C, g + 1)
                if g == 0 and P.ok:
                    hold(sp, s("pe_up"), EC, P, 0)
                    nxt = P.v + 1
                    if isinstance(nxt, int) and nxt >= images:
                        pass
                    else:
                        load_x(P, nxt, 1 - P.par)
                if g == 1 and P.ok:
                    hold(sp, s("act_h"), 2, P, 2)
                    sp.dma_start(h_dram[bass.ds(P.v * S, S), :].rearrange("(t p) n -> p t n", p=128),
                                 h_sb[:, :, :]).then_inc(s("h_stored"), 16)
                if g == 2 and W.ok:
                    hold(sp, s("h_stored"), 16, W, 16)
                    hold(sp, s("h2_stored"), 16, W, 0)
                    hold(sp, s("act_x2"), TB, W, 0)
                    sp.dma_start(hw[:, :, :], h_dram[bass.ds(W.v * S, S), :].rearrange("(t p) n -> p t n", p=128)) \
                        .then_inc(s("hw_in"), 16)
                if g == 3 and P.ok:
                    store_parts(P)
                    stack(P, 0)
                if g == 3 and W.ok:
                    hold(sp, s("dve_h2c"), 1, W, 1)
                    sp.dma_start(out[bass.ds(W.v * SEQ, 1), :], h2c[:, :]).then_inc(s("h2c_stored"), 16)
                    hold(sp, s("dve_h2"), TB, W, TB)
                    sp.dma_start(out[bass.ds(W.v * SEQ + 1, S), :].rearrange("(t p) n -> p t n", p=128),
                                 hw[:, :, :]).then_inc(s("h2_stored"), 16)
                    hold(sp, s("act_x2"), TB, W, TB)
                    sp.dma_start(x2_dram[bass.ds(W.v * SEQ + 1, S), :].rearrange("(t p) n -> p t n", p=128),
                                 x2[:, :, :]).then_inc(s("x2_stored"), 16)
        if stage == STEPS:
            load_x(None, 0, 0)
            steps(sp, body)
            sp.wait_ge(s("h2c_stored"), 16 * images)
            sp.wait_ge(s("h2_stored"), 16 * images)
            sp.wait_ge(s("x2_stored"), 16 * images)
            sp.wait_ge(s("h_stored"), 16 * images)
            sp.wait_ge(s("parts_stored"), 16 * 4 * len(PARTS) * images)
        if stage == CLASS_TOKENS:
            crow = out.rearrange("(b q) n -> b q n", q=SEQ)[:, 0, :]
            sp.dma_start(hw[0:images, 0, :], crow).then_inc(s("cls_back"), 16)
            sp.wait_ge(s("act_x2_c"), 1)
            sp.dma_start(x2_dram[0:tokens, :].rearrange("(b q) n -> b q n", q=SEQ)[:, 0, :], x2[0:images, 0, :]) \
                .then_inc(s("x2c_stored"), 16)
            sp.wait_ge(s("x2c_stored"), 16)


    def tensor_program(pe, stage):
        mm, tr = nc.tensor.matmul, nc.tensor.transpose
        if stage == SETUP:
            pe.wait_ge(s("ones_set"), 2)
            pe.wait_ge(s("w_sums"), 1)
            mm(d0[:, 0:4], ones[:, :], w_mean[:, :], start=True, stop=True).then_inc(s("pe_w_sum"), 1)
            pe.wait_ge(s("cls_norm"), 1)
            pe.wait_ge(s("cls_facts"), 1)
            mm(d1[:, 0:4], ones[0:1, :], cls_fact[:, :], start=True, stop=True)
            for c in range(DC):
                last = mm(d1[:, 4 + c:5 + c], cls_norm[:, blk(c)], ones[0:1, 0:1], start=True, stop=True)
            last.then_inc(s("pe_cls"), 1)
            pe.wait_ge(s("cls_used"), 2)
            pe.wait_ge(s("w_int"), 4)
            pe.wait_ge(s("wo_cls_in"), 16 * NG)
            pe.wait_ge(s("tok_w_in"), 48)
            pe.wait_ge(s("gate_in"), 16)
            pe.wait_ge(s("bf_set"), 3)
            pe.wait_ge(s("pool_set"), 6)

        def score_unit(b, g, u):
            j, t = u // TB, u % TB
            if u == 0:
                wait(pe, s(f"stacked{g}"), 16 * len(Q_STACK + K_STACK), b, 16 * len(Q_STACK + K_STACK))
            wait(pe, s("dve_mx"), UNITS * NG, b, UNITS * g + u - 1)
            h = g * GH + j
            mm(score[u % 2][:, :], qs[0:QK, h, blk(t)], ks[0:QK, h, :], start=True, stop=True) \
                .then_inc(s("pe_a"), 1)

        def scoret_unit(b, g, u):
            t, j = u // GH, u % GH
            if u == 0:
                wait(pe, s(f"max_in{g}"), 16, b, 16)
            wait(pe, s("act_exp"), UNITS * NG, b, UNITS * g + u - 1)
            h = g * GH + j
            mm(scoret[u % 2][:, :], ks[0:QK + MROWS, h, blk(t)], qs[0:QK + MROWS, h, :],
               start=True, stop=True).then_inc(s("pe_st"), 1)

        def pv(b, g, t):
            wait(pe, s("act_exp"), UNITS * NG, b, UNITS * g + GH * (t + 1))
            if t == 0:
                wait(pe, s("act_pvs"), NG, b, g)
                wait(pe, s("act_v"), TB, b, TB)
            for j in range(GH):
                last = mm(pv_bank[VW * j:VW * (j + 1), :], v_sb[:, b.par, t, g * GH + j, :],
                          pt[:, t % 2, j, :], start=(t == 0), stop=(t == TB - 1))
            last.then_inc(s("pe_pv"), 1)

        def body(P, C, W, X):
            for g in range(NG):
                for u in range(UNITS):
                    if u % 4 == 0:
                        P, C, W, X = fresh(pe, UNITS * g + u, P, C, W, X)
                        st, tg, mt = in_slot(g, P, C, W)
                    at = UNITS * g + u
                    if C.ok:
                        score_unit(C, g, u)
                    if st[0].ok:
                        scoret_unit(*st, u)
                    if u == 3 and tg[0].ok:
                        pv(*tg, TB - 1)
                    if u % 4 == 3 and u > 3 and st[0].ok:
                        pv(*st, u // 4 - 1)
                    if P.ok and at % 4 == 0 and at < 16:
                        e = at // 4
                        if e == 0:
                            pe.wait_ge(s(f"x_in{P.par}"), P.half * 16 + 16)
                            if X.ok:
                                wait(pe, s("dve_h2"), TB, X, TB)
                        elif e == 1 and X.ok:
                            wait(pe, s("act_x2t"), DC, X, DC)
                        wait(pe, s("act_relu"), EC, P, e)
                        for c in range(DC):
                            last = mm(d0[:, :], w0[:, c, blk(e)], xt[:, P.par, c, :], start=(c == 0), stop=(c == DC - 1))
                        last.then_inc(s("pe_gate"), 1)
                        wait(pe, s("dve_hid"), EC, P, e)
                        for c in range(DC):
                            last = mm(d1[:, :], w1[:, c, blk(e)], xt[:, P.par, c, :], start=(c == 0), stop=(c == DC - 1))
                        last.then_inc(s("pe_up"), 1)
                    if u == 2 and mt[0].ok:
                        b, gg = mt
                        wait(pe, s("dve_nm"), NG, b, gg + 1)
                        if g == 0:
                            if X.ok:
                                wait(pe, s("dve_h2c"), 1, X, 1)
                                wait(pe, s("dve_o"), NG, X, NG)
                            wait(pe, s("dve_o"), NG, W, 1)
                        if g == 1 and X.ok:
                            wait(pe, s("dve_rk"), 1, X, 1)
                        if g == 1 and W.ok:
                            wait(pe, s("dve_o"), NG, W, 2)
                        if g == 2:
                            if P.ok:
                                wait(pe, s("dve_ms"), 1, P, 1)
                            if W.ok:
                                wait(pe, s("dve_o"), NG, W, 3)
                        if g == 3:
                            if P.ok:
                                wait(pe, s("dve_scs"), 1, P, 1)
                            if W.ok:
                                wait(pe, s("dve_ms2"), 1, W, 1)
                        for t in range(TB):
                            last = tr(b16(d2)[0:MROWS * GH, blk(t)], nmp[:, t, :], id_bf[:, :])
                        last.then_inc(s("pe_mt"), 1)
                    if at == 3 and X.ok:
                        wait(pe, s("act_x2"), TB, X, TB)
                        if P.ok:
                            wait(pe, s("act_relu"), EC, P, 1)
                            wait(pe, s("dve_hid"), EC, P, 1)
                        else:
                            wait(pe, s("dve_h2"), TB, X, TB)
                        for c in range(DC):
                            for t in range(TB):
                                last = tr((d0, d1)[c][:, blk(t)], x2[:, t, blk(c)], identf)
                            last.then_inc(s("pe_x2t"), 1)
                    if at == 5 and X.ok:
                        logits(X, TB, 128, "", [("act_mt", NG, W, NG)] if W.ok else [("dve_h2c", 1, X, 1)])
                    if u == 6 and tg[0].ok:
                        b, gg = tg
                        wait(pe, s("act_pvs"), NG, b, gg + 1)
                        if gg:
                            wait(pe, s("dve_o"), NG, b, gg)
                        if g == 0 and X.ok:
                            wait(pe, s("dve_lg"), 1, X, 1)
                        if g == 1 and X.ok:
                            wait(pe, s("dve_rk"), 1, X, 1)
                        if mt[0].ok:
                            wait(pe, s("act_mt"), NG, mt[0], mt[1] + 1)
                        if g == 3 and W.ok:
                            wait(pe, s("act_xqc"), 1, W, 1)
                        for t in range(TB):
                            last = tr(d2[:, blk(t)], pvs[:, blk(t)], identf)
                        last.then_inc(s("pe_tg"), 1)
                    if at == 10 and X.ok:
                        ranks(X, TB, 128, "", [("dve_o", NG, W, 2)] if W.ok else [("dve_lg", 1, X, 1)])
                    if P.ok and at in (16, 20):
                        k = (at - 16) // 4
                        wait(pe, s("dve_hid"), EC, P, EC)
                        for t in (2 * k, 2 * k + 1):
                            for e in range(EC):
                                last = mm((d0, d1)[k][:, D * (t % 2):D * (t % 2 + 1)], hid[:, e, blk(t)], wo[:, e, :],
                                          start=(e == 0), stop=(e == EC - 1))
                        last.then_inc(s("pe_h"), 1)
                    if P.ok and at == 27:
                        wait(pe, s("act_xh"), TB, P, TB)
                        wait(pe, s("dve_sst"), 1, P, 1)
                        if W.ok:
                            wait(pe, s("dve_o"), NG, W, 3)
                        if C.ok:
                            wait(pe, s("act_mt"), NG, C, 1)
                        mm(d2[:, 0:2 * TB], ones[:, :], sums1[:, :, :].rearrange("p a t -> p (a t)"),
                           start=True, stop=True).then_inc(s("pe_st1"), 1)
                    if P.ok and at == 33:
                        wait(pe, s("pool_qi"), 1, P, 1)
                        wait(pe, s("act_h"), 2, P, 2)
                        for c in range(DC):
                            for t in range(TB):
                                last = tr(b16(d0)[:, c * S + t * 128:c * S + (t + 1) * 128], qi[:, t, blk(c)], id_bf[:, :])
                        last.then_inc(s("pe_xq"), 1)
                        wait(pe, s("dve_aq"), 1, P, 1)
                        for t in range(TB):
                            last = mm(d1[:, blk(t)], aq1[:, t:t + 1].broadcast_to([128, 128]), identf, start=True, stop=True)
                        last.then_inc(s("pe_aqb"), 1)
                    if P.ok and at == 36:
                        wait(pe, s("act_xq"), 1, P, 1)
                        wait(pe, s("act_aqb"), 1, P, 1)
                        project(P, 0, "pe_q")
                    if W.ok and at == 39:
                        wait(pe, s("dve_o"), NG, W, NG)
                        wait(pe, s("act_pc"), 1, W, 1)
                        for k in range(NG):
                            for t in range(TB):
                                mm(d2[:, k * NH:(k + 1) * NH],
                                   v_sb[:, W.par, t, heads(k), :].rearrange("p h w -> p (h w)"),
                                   pc[:, W.par, t, :], start=(t == 0), stop=False)
                            last = mm(d2[:, k * NH:(k + 1) * NH],
                                      vcls[0:1, W.par, heads(k), :].rearrange("p h w -> p (h w)"),
                                      pc[0:1, W.par, TB, :], start=False, stop=True)
                        last.then_inc(s("pe_pvc"), 1)
                    if P.ok and at == 40:
                        wait(pe, s("dve_fq"), DC, P, DC)
                        project(P, 1, "pe_k")
                    if W.ok and at == 42:
                        wait(pe, s("dve_pv4"), 1, W, 1)
                        tr(d2[0:NG, 0:128], pv4[:, :], identf).then_inc(s("pe_tr"), 1)
                    if P.ok and at == 43:
                        for t in range(TB):
                            wait(pe, s("dve_fk"), DC, P, t // 2 + 1)
                            for c in range(DC):
                                last = mm((d0, d1)[t // 2][:, D * (t % 2):D * (t % 2 + 1)], xq[:, c, blk(t)],
                                          wq_int[:, 2, c, :], start=(c == 0), stop=(c == DC - 1))
                            last.then_inc(s("pe_v"), 1)
                    if P.ok and at == 44:
                        wait(pe, s("dve_qc"), 1, P, 1)
                        if W.ok:
                            wait(pe, s("dve_oc"), 1, W, 1)
                        elif C.ok:
                            wait(pe, s("act_mt"), NG, C, 2)
                        wait(pe, s("dve_ms"), 1, P, 1)
                        for c in range(DC):
                            mm(d2[:, 0:D], xq[:, c, S:SEQ].broadcast_to([128, 128]), wq_int[:, 2, c, :],
                               start=(c == 0), stop=(c == DC - 1))
                        for w in range(2):
                            for f in range(DC):
                                for c in range(DC):
                                    last = mm(d2[:, D + 2 * w + f:D + 2 * w + f + 1], wq_int[:, w, c, blk(f)],
                                              xq[:, c, S:SEQ], start=(c == 0), stop=(c == DC - 1))
                        last.then_inc(s("pe_cols"), 1)
                    if W.ok and at == 46:
                        wait(pe, s("dve_st2"), 1, W, 1)
                        if P.ok:
                            wait(pe, s("act_vc"), 1, P, 1)
                            wait(pe, s("dve_cc"), 2, P, 2)
                        mm(d2[:, 0:2], ones[:, :], st2[:, :], start=True, stop=False)
                        mm(d2[:, 0:2], ones[0:NG, :], st2c[:, :], start=False, stop=True).then_inc(s("pe_w1"), 1)
                    if P.ok and at == 48:
                        wait(pe, s("dve_bd"), 2, P, 2)
                        wait(pe, s("act_vc"), 1, P, 1)
                        if W.ok:
                            wait(pe, s("dve_ms2"), 1, W, 1)
                        for k, (a, o) in enumerate(((fq, kbd), (fk, qbd))):
                            for t in range(TB):
                                for c in range(DC):
                                    mm(d2[:, (k * TB + t) * NH:(k * TB + t + 1) * NH], a[:, c, blk(t)], o[:, c, :],
                                       start=(c == 0), stop=(c == DC - 1))
                        for c in range(DC):
                            last = mm(d2[:, 2 * TB * NH:(2 * TB + 1) * NH], fq[:, c, S:SEQ].broadcast_to([128, 128]),
                                      kbd[:, c, :], start=(c == 0), stop=(c == DC - 1))
                        last.then_inc(s("pe_t7"), 1)
                    if W.ok and at == 51:
                        wait(pe, s("pool_qi2"), 2, W, 2)
                        if P.ok:
                            wait(pe, s("act_v"), TB, P, TB)
                            wait(pe, s("dve_scs"), 1, P, 1)
                        if C.ok:
                            wait(pe, s("act_mt"), NG, C, 3)
                        for c in range(DC):
                            for t in range(TB):
                                last = tr(b16(d0)[:, c * S + t * 128:c * S + (t + 1) * 128], qi2[:, t, blk(c)], id_bf[:, :])
                        last.then_inc(s("pe_xq2"), 1)
                        tr(b16(d2)[0:64, 0:NG], qic[:, :], id_bf[0:NG, 0:NG]).then_inc(s("pe_xqc"), 1)
                    if W.ok and at == 56:
                        wait(pe, s("act_xq2"), 1, W, 1)
                        for t in range(TB):
                            for c in range(DC):
                                last = mm((d0, d1)[t // 2][:, D * (t % 2):D * (t % 2 + 1)], xq2[:, c, blk(t)],
                                          wq_int[:, 3, c, :], start=(c == 0), stop=(c == DC - 1))
                            last.then_inc(s("pe_y"), 1)
                        hold(pe, s("act_xqc"), 1, W, 1)
                        if C.ok:
                            hold(pe, s("dve_o"), NG, C, 1)
                        for k in range(NG):
                            last = mm(d2[0:1, 0:D], xqc[:, k:k + 1], wo_cls[:, k, :], start=(k == 0), stop=(k == NG - 1))
                        last.then_inc(s("pe_yc"), 1)

        def project(b, w, signal):
            for f in range(DC):
                for c in range(DC):
                    last = mm((d0, d1)[f][:, :], wq_int[:, w, c, blk(f)], xq[:, c, 0:S], start=(c == 0), stop=(c == DC - 1))
                last.then_inc(s(signal), 1)

        def logits(b, nt, np_, x, free):
            wait(pe, s("act_x2t" + x), DC, b, DC)
            for name, per, at_, n in free:
                wait(pe, s(name), per, at_, n)
            for t in range(nt):
                for c in range(DC):
                    last = mm(d2[0:np_, t * E:(t + 1) * E], x2_t[:, c, t * 128:t * 128 + np_], gate_sb[:, c, :],
                              start=(c == 0), stop=(c == DC - 1))
            last.then_inc(s("pe_lg" + x), 1)

        def ranks(b, nt, np_, x, free):
            wait(pe, s("dve_picked" + x), 1, b, 1)
            for name, per, at_, n in free:
                wait(pe, s(name), per, at_, n)
            a = picked[0:np_, :, :].rearrange("p t e -> p (t e)")
            mm(d2[0:np_, 0:nt * E], tri_bf[0:np_, 0:np_], a[:, 0:nt * E], start=True, stop=(nt == 1))
            for t in range(1, nt):
                mm(d2[0:np_, t * E:nt * E], ones_bf[0:np_, 0:np_], a[:, 0:(nt - t) * E], start=False, stop=(t == nt - 1))
            for t in range(nt):
                last = mm(d2[:, TB * E:(TB + 1) * E], ones_bf[0:np_, :], a[:, t * E:(t + 1) * E],
                          start=(t == 0), stop=(t == nt - 1))
            last.then_inc(s("pe_rk" + x), 1)

        if stage == STEPS:
            steps(pe, body)
        if stage == CLASS_TOKENS:
            one = At(0)
            pe.wait_ge(s("act_x2_c"), 1)
            for c in range(DC):
                tr((d0, d1)[c][:, 0:images], x2[0:images, 0, blk(c)], cst[0:images, C_ID:C_ID + images]) \
                    .then_inc(s("pe_x2t_c"), 1)
            logits(one, 1, images, "_c", [])
            ranks(one, 1, images, "_c", [("dve_lg_c", 1, one, 1)])


    def scalar_program(act, stage):
        f = nc.scalar.activation
        if stage == SETUP:
            act.wait_ge(s("cls_scale"), 1)
            f(cls_norm[:, :], cls_row[:, :], ACT.Identity, bias=cls_mv[:, 3:4], scale=cls_mv[:, 2:3],
              accum_out=cls_stat[:, 0:1]).then_inc(s("cls_norm"), 1)

        def exps(b, g, u):
            t, j = u // GH, u % GH
            wait(act, s("pe_st"), UNITS * NG, b, UNITS * g + u + 1)
            if j == 0:
                wait(act, s("pe_pv"), TB * NG, b, TB * g + t - 1)
            f(pt[:, t % 2, j, :], scoret[u % 2][:, :], ACT.Exp).then_inc(s("act_exp"), 1)

        def body(P, C, W, X):
            for g in range(NG):
                for u in range(UNITS):
                    if u % 4 == 0:
                        P, C, W, X = fresh(act, UNITS * g + u, P, C, W, X)
                        st, tg, mt = in_slot(g, P, C, W)
                    at = UNITS * g + u
                    if u == 4 and tg[0].ok:
                        b, gg = tg
                        wait(act, s("pe_pv"), TB * NG, b, TB * (gg + 1))
                        wait(act, s("pe_tg"), NG, b, gg)
                        f(pvs[:, :], pv_bank[:, :], ACT.Copy).then_inc(s("act_pvs"), 1)
                    if st[0].ok:
                        exps(*st, u)
                    if P.ok and at % 4 == 0 and at < 16:
                        e = at // 4
                        wait(act, s("pe_gate"), EC, P, e + 1)
                        wait(act, s("dve_hid"), EC, P, e - 1)
                        f(relu[:, e % 2, :], d0[:, :], ACT.Relu).then_inc(s("act_relu"), 1)
                    if u == 1 and mt[0].ok:
                        b, gg = mt
                        wait(act, s("dve_dsc"), NG, b, gg + 1)
                        f(pcls[:, b.par, :, heads(gg)], dsc[:, :, heads(gg)], ACT.Exp).then_inc(s("act_pcls"), 1)
                    if u == 3 and mt[0].ok:
                        b, gg = mt
                        wait(act, s("pe_mt"), NG, b, gg + 1)
                        wait(act, s(f"max_in{(gg - 1) % NG}"), 16, b, 0 if gg == 0 else 16)
                        f(mt_sb[:, :], b16(d2)[0:MROWS * GH, 0:S], ACT.Copy).then_inc(s("act_mt"), 1)
                    if at == 3 and X.ok:
                        wait(act, s("pe_lg"), 1, X, 0)
                        for c in range(DC):
                            wait(act, s("pe_x2t"), DC, X, c + 1)
                            f(x2_t[:, c, :], (d0, d1)[c][:, :], ACT.Copy).then_inc(s("act_x2t"), 1)
                    if at == 8 and X.ok:
                        wait(act, s("dve_e"), 1, X, 1)
                        f(e21e[:, :], e21[:, :], ACT.Exp).then_inc(s("act_e"), 1)
                    if P.ok and at in (17, 21):
                        k = (at - 17) // 4
                        wait(act, s("pe_h"), 2, P, k + 1)
                        wait(act, s("h_stored"), 16, P, 0)
                        wait(act, s("dve_sst"), 1, P, 0)
                        f(h_sb[:, 2 * k:2 * k + 2, :].rearrange("p t n -> p (t n)"), (d0, d1)[k][:, :], ACT.Copy) \
                            .then_inc(s("act_h"), 1)
                    if P.ok and at == 25:
                        wait(act, s("dve_nb1"), 1, P, 1)
                        wait(act, s("pool_qi"), 1, P, 0)
                        wait(act, s("pe_st1"), 1, P, 0)
                        for t in range(TB):
                            f(xn[:, t, :], h_sb[:, t, :], ACT.Identity, bias=nb1[:, t:t + 1], scale=rstd1[:, t:t + 1],
                              accum_out=sums1[:, 0, t:t + 1]).then_inc(s("act_xh"), 1)
                    if P.ok and at == 34:
                        wait(act, s("pe_xq"), 1, P, 1)
                        wait(act, s("pe_cols"), 1, P, 0)
                        f(xq[:, :, 0:S], b16(d0).rearrange("p (c n) -> p c n", c=DC), ACT.Copy).then_inc(s("act_xq"), 1)
                        wait(act, s("pe_aqb"), 1, P, 1)
                        wait(act, s("dve_fk"), DC, P, 0)
                        f(aqb[:, :], d1[:, :], ACT.Copy).then_inc(s("act_aqb"), 1)
                    if P.ok and at == 38:
                        wait(act, s("dve_fq"), DC, P, DC)
                        wait(act, s("parts_stored"), 16 * 4 * len(PARTS), P, 0)
                        f(parts["qh"][:, :, :], fq[:, :, 0:S], ACT.Copy).then_inc(s("act_qh"), 1)
                    if P.ok and at == 41:
                        wait(act, s("dve_fk"), DC, P, DC)
                        f(parts["kh"][:, :, :], fk[:, :, 0:S], ACT.Copy).then_inc(s("act_kh"), 1)
                        wait(act, s("pool_rq"), 1, P, 1)
                        f(parts["qm"][:, :, :], rest[:, :, :], ACT.Copy).then_inc(s("act_qm"), 1)
                    if P.ok and at == 43:
                        wait(act, s("dve_aqv"), 1, P, 1)
                        wait(act, s("pe_pv"), TB * NG, P, -TB * NG)
                        wait(act, s("pe_pvc"), 1, P, -1)
                        for t in range(TB):
                            wait(act, s("pe_v"), TB, P, t // 2 * 2 + 2)
                            f(v_sb[:, P.par, t, :, 1:1 + HD],
                              (d0, d1)[t // 2][:, D * (t % 2):D * (t % 2 + 1)].rearrange("p (h d) -> p h d", d=HD),
                              ACT.Copy, scale=aqv[:, t:t + 1]).then_inc(s("act_v"), 1)
                    if P.ok and at == 45:
                        wait(act, s("pe_cols"), 1, P, 1)
                        wait(act, s("dve_cc"), 2, P, 2)
                        wait(act, s("pool_add"), NG, P, -NG)
                        f(vcls[:, P.par, :, 1:1 + HD], d2[:, 0:D].rearrange("p (h d) -> p h d", d=HD),
                          ACT.Copy, scale=aqv[:, TB:TB + 1]).then_inc(s("act_vc"), 1)
                    if P.ok and at == 46:
                        wait(act, s("pool_rk"), 1, P, 1)
                        f(parts["km"][:, :, :], rest[:, :, :], ACT.Copy).then_inc(s("act_km"), 1)
                    if P.ok and at == 52:
                        wait(act, s("dve_pci"), 1, P, 1)
                        wait(act, s("pe_pvc"), 1, P, -1)
                        f(pc[:, P.par, :, :], pci[:, :, :], ACT.Exp).then_inc(s("act_pc"), 1)
                    if W.ok and at == 52:
                        wait(act, s("pe_xq2"), 1, W, 1)
                        wait(act, s("pe_y"), TB, W, 0)
                        f(xq2[:, :, :], b16(d0).rearrange("p (c n) -> p c n", c=DC), ACT.Copy).then_inc(s("act_xq2"), 1)
                        wait(act, s("pe_xqc"), 1, W, 1)
                        wait(act, s("pe_yc"), 1, W, 0)
                        f(xqc[:, :], b16(d2)[0:64, 0:NG], ACT.Copy).then_inc(s("act_xqc"), 1)
                    if W.ok and at == 63:
                        wait(act, s("dve_nb3"), 1, W, 1)
                        wait(act, s("pe_x2t"), DC, W, 0)
                        wait(act, s("x2_stored"), 16, W, 0)
                        for t in range(TB):
                            f(x2[:, t, :], hw[:, t, :], ACT.Identity, bias=nb3[:, t:t + 1], scale=rstd3[:, t:t + 1]) \
                                .then_inc(s("act_x2"), 1)
        if stage == STEPS:
            steps(act, body)
        if stage == CLASS_TOKENS:
            act.wait_ge(s("dve_nb3_c"), 1)
            f(x2[0:images, 0, :], hw[0:images, 0, :], ACT.Identity, bias=nb3[0:images, 0:1], scale=rstd3[0:images, 0:1]) \
                .then_inc(s("act_x2_c"), 1)
            for c in range(DC):
                act.wait_ge(s("pe_x2t_c"), c + 1)
                f(x2_t[:, c, 0:images], (d0, d1)[c][:, 0:images], ACT.Copy).then_inc(s("act_x2t_c"), 1)
            act.wait_ge(s("dve_e_c"), 1)
            f(e21e[0:images, 0:1], e21[0:images, 0:1], ACT.Exp).then_inc(s("act_e_c"), 1)


    def gpsimd_program(pool, stage):
        g_ = nc.gpsimd

        def rsqrt(out_, in_, n, np_, ready, done, b):
            hold(pool, s(ready), 1, b, 1)
            g_.tensor_tensor(out_, in_, neg_half[0:np_, 0:n], ALU.pow).then_inc(s(done), 1)

        one = At(0)
        if stage == SETUP:
            for n, (place, value) in enumerate(((neg_half[:, :], -0.5), (ks[QK:128, :, :], 1.0), (v_sb[:, :, :, :, :], 0.0),
                                                (vcls[:, :, :, :], 0.0), (v_sb[:, :, :, :, 0:1], 1.0), (vcls[:, :, :, 0:1], 1.0))):
                g_.memset(place, value).then_inc(s("pool_set"), 1)
                pool.wait_ge(s("pool_set"), n + 1)
            rsqrt(cls_mv[:, 2:3], cls_mv[:, 2:3], 1, 1, "cls_var", "cls_rstd", one)

        def scatter(b, nt, np_, x):
            hold(pool, s("dve_pay" + x), 1, b, 1)
            for k in range(2):
                for t in range(nt):
                    g_.indirect_dma_start(out=list_dram, out_offset=bass.IndirectOffsetOnAxis(
                        ap=slot_i[0:np_, k, t:t + 1], axis=0), in_=pay[0:np_, k, t, :], in_offset=None) \
                        .then_inc(s("scattered"), 16)

        def body(P, C, W, X):
            for g in range(NG):
                for u in range(UNITS):
                    if u % 4 == 0:
                        P, C, W, X = fresh(pool, UNITS * g + u, P, C, W, X)
                        st, tg, mt = in_slot(g, P, C, W)
                    at = UNITS * g + u
                    if u == 9 and tg[0].ok:
                        b, gg = tg
                        hold(pool, s("dve_pr"), NG, b, gg + 1)
                        hold(pool, s("act_vc"), 1, b, 1)
                        hold(pool, s("pool_add"), NG, b, gg)
                        g_.tensor_tensor(cadd[:, :, :, :], bcast(vcls[:, b.par, heads(gg), 1:1 + HD], 1, TB),
                                         bcast(pr[:, :, heads(gg)], 3, HD), ALU.mult).then_inc(s("pool_mul"), 1)
                        hold(pool, s("pool_mul"), NG, b, gg + 1)
                        o = o_sb[:, b.par, :, :].rearrange("p t (h d) -> p t h d", d=HD)[:, :, heads(gg), :]
                        g_.tensor_tensor(o, o, cadd[:, :, :, :], ALU.add).then_inc(s("pool_add"), 1)
                    if X.ok and at == 14:
                        scatter(X, TB, 128, "")
                    if P.ok and at == 23:
                        rsqrt(rstd1[:, :], ve1[:, :], TB, 128, "dve_ve1", "pool_r1", P)
                    if P.ok and at == 28:
                        rsqrt(rs1[:, :], msq1[:, 1:2], 1, 128, "dve_ve", "pool_rs", P)
                    if P.ok and at == 31:
                        hold(pool, s("dve_q1"), TB, P, TB)
                        hold(pool, s("pe_xq"), 1, P, 0)
                        g_.tensor_scalar(qi[:, :, :], xn[:, :, :], -MAGIC, 1.0, ALU.add, ALU.mult).then_inc(s("pool_qi"), 1)
                    if P.ok and at == 39:
                        hold(pool, s("act_qh"), 1, P, 1)
                        g_.tensor_tensor(rest[:, :, :], fq[:, :, 0:S], parts["qh"][:, :, :], ALU.subtract) \
                            .then_inc(s("pool_rq"), 1)
                    if P.ok and at == 42:
                        hold(pool, s("act_qm"), 1, P, 1)
                        g_.tensor_tensor(parts["ql"][:, :, :], rest[:, :, :], parts["qm"][:, :, :], ALU.subtract) \
                            .then_inc(s("pool_lq"), 1)
                        hold(pool, s("act_kh"), 1, P, 1)
                        hold(pool, s("pool_lq"), 1, P, 1)
                        g_.tensor_tensor(rest[:, :, :], fk[:, :, 0:S], parts["kh"][:, :, :], ALU.subtract) \
                            .then_inc(s("pool_rk"), 1)
                    if W.ok and at == 46:
                        rsqrt(rs2[:, :], msq2[:, 1:2], 1, 128, "dve_ve2", "pool_rs2", W)
                        hold(pool, s("dve_amc"), 1, W, 1)
                        g_.partition_all_reduce(am2[0:NG, TB:TB + 1], amc[:, :], NG, bass.bass_isa.ReduceOp.absmax).then_inc(s("pool_amc"), 1)
                    if P.ok and at == 47:
                        hold(pool, s("act_km"), 1, P, 1)
                        g_.tensor_tensor(parts["kl"][:, :, :], rest[:, :, :], parts["km"][:, :, :], ALU.subtract) \
                            .then_inc(s("pool_lk"), 1)
                    if P.ok and at == 50:
                        hold(pool, s("dve_scs"), 1, P, 1)
                        g_.partition_all_reduce(cmx[:, :], scs[:, P.par, TB * NH:2 * TB * NH], 128,
                                                bass.bass_isa.ReduceOp.max).then_inc(s("pool_par"), 1)
                    if W.ok and at == 50:
                        hold(pool, s("dve_q2"), TB + 1, W, TB + 1)
                        hold(pool, s("pe_xqc"), 1, W, 0)
                        g_.tensor_scalar(qi2[:, :, :], o_sb[:, W.par, :, :], -MAGIC, 1.0, ALU.add, ALU.mult) \
                            .then_inc(s("pool_qi2"), 1)
                        g_.tensor_scalar(qic[:, :], oc[:, :, :].rearrange("p j d -> p (j d)"), -MAGIC, 1.0,
                                         ALU.add, ALU.mult).then_inc(s("pool_qi2"), 1)
                    if W.ok and at == 60:
                        rsqrt(rstd3[:, :], ve3[:, :], TB, 128, "dve_ve3", "pool_r3", W)
        if stage == SETUP:
            pool.wait_ge(s("list_init"), 32)
        if stage == STEPS:
            steps(pool, body)
            pool.wait_ge(s("scattered"), 16 * 2 * TB * images)
        if stage == CLASS_TOKENS:
            rsqrt(rstd3[0:images, 0:1], ve3[0:images, 0:1], 1, images, "dve_ve3_c", "pool_r3_c", one)
            scatter(one, 1, images, "_c")
            pool.wait_ge(s("scattered"), 16 * 2)


    def vector_program(dve, stage):
        v = nc.vector

        class Link:

            def __init__(self, name, per, b, start=0):
                self.sem, self.per, self.b, self.n = s(name), per, b, start

            def go(self, ins):
                ins.then_inc(self.sem, 1)
                self.n += 1

            def __call__(self, ins):
                self.go(ins)
                self.wait()

            def wait(self):
                wait(dve, self.sem, self.per, self.b, self.n)

            def hold(self):
                hold(dve, self.sem, self.per, self.b, self.n)

            def end(self, n):
                assert self.n == n, (self.sem, self.n, n)

        def signal(ins, name, per, b, n):
            ins.then_inc(s(name), 1)
            wait(dve, s(name), per, b, n)

        one = At(0)
        if stage == SETUP:
            v.memset(ones[:, :], 1.0).then_inc(s("ones_set"), 1)
            v.memset(am2[:, :], 1.0).then_inc(s("ones_set"), 1)
            v.memset(ones_bf[:, :], 1.0).then_inc(s("bf_set"), 1)
            v.memset(pads[:, :, 0:1], tokens).then_inc(s("pads_set"), 1)
            v.memset(pads[:, :, 1:2], 0).then_inc(s("pads_set"), 1)
            v.memset(zero_row[:, :], 0.0).then_inc(s("pads_set"), 1)
            dve.wait_ge(s("cst_in"), 16)
            v.tensor_copy(id_bf[:, :], identf).then_inc(s("bf_set"), 1)
            v.tensor_copy(tri_bf[:, :], cst[:, C_TRI:C_TRI + 128]).then_inc(s("bf_set"), 1)
            v.tensor_copy(run[:, :], cst[:, C_BASE:C_BASE + E]).then_inc(s("dve_init"), 1)
            v.tensor_copy(row[:, :], cst[:, C_ROW:C_ROW + TB]).then_inc(s("dve_init"), 1)
            dve.wait_ge(s("cls_in"), 16)
            init = Link("dve_chain0", 0, one)
            init(v.bn_stats(cls_stat[:, :], cls_row[:, :]))
            init(v.bn_aggr(cls_mv[:, 0:2], cls_stat[:, :]))
            v.tensor_scalar(cls_mv[:, 2:3], cls_mv[:, 1:2], EPS, None, ALU.add).then_inc(s("cls_var"), 1)
            dve.wait_ge(s("attn_w_in"), 16)
            v.tensor_reduce(out=w_mean[:, :], in_=w_stage.rearrange("p (w n) -> p w n", w=4), axis=AX.X, op=ALU.add,
                            apply_absolute_value=True).then_inc(s("w_sums"), 1)
            dve.wait_ge(s("cls_rstd"), 1)
            v.scalar_tensor_tensor(cls_mv[:, 3:4], cls_mv[:, 0:1], -1.0, cls_mv[:, 2:3], ALU.mult, ALU.mult) \
                .then_inc(s("cls_scale"), 1)
            dve.wait_ge(s("pe_w_sum"), 1)
            init(v.tensor_scalar(w_mean[:, :], d0[:, 0:4], 1.0 / (D * D), 1e-5, ALU.mult, ALU.max))
            init(v.reciprocal(w_scale[:, :], w_mean[:, :]))
            init(v.tensor_copy(w_fac[:, 1:4], w_mean[:, 1:4]))
            init(v.tensor_scalar(w_fac[:, 0:1], w_mean[:, 0:1], float(HD) ** -0.5, None, ALU.mult))
            for w in range(4):
                part = w_stage[:, w * DC * D:(w + 1) * DC * D]
                init(v.tensor_scalar(part, part, w_scale[:, w:w + 1], MAGIC, ALU.mult, ALU.add))
                init(v.tensor_scalar(part, part, -MAGIC, 1.0, ALU.add, ALU.min))
                v.tensor_scalar(wq_int[:, w, :, :].rearrange("p c n -> p (c n)"), part, -1.0, None, ALU.max) \
                    .then_inc(s("w_int"), 1)
            dve.wait_ge(s("cls_norm"), 1)
            init(v.tensor_tensor(cls_fact[:, 1:2], cls_mv[:, 1:2], cls_mv[:, 2:3], ALU.mult))
            init(v.scalar_tensor_tensor(cls_fact[:, 1:2], cls_fact[:, 1:2], D / total, cls_mv[:, 2:3], ALU.mult, ALU.mult))
            init(v.tensor_scalar(cls_fact[:, 0:1], cls_stat[:, 0:1], 1.0 / total, None, ALU.mult))
            init(v.tensor_reduce(out=cls_fact[:, 2:3], in_=cls_norm[:, :], axis=AX.X, op=ALU.max))
            v.tensor_reduce(out=cls_fact[:, 3:4], in_=cls_norm[:, :], axis=AX.X, op=ALU.min).then_inc(s("cls_facts"), 1)
            dve.wait_ge(s("pe_cls"), 1)
            v.tensor_copy(cls_f[:, :], d1[:, 0:4]).then_inc(s("cls_used"), 1)
            v.tensor_copy(cls_t[:, :], d1[:, 4:4 + DC]).then_inc(s("cls_used"), 1)
            dve.wait_ge(s("cls_used"), 2)
            dve.wait_ge(s("ones_set"), 2)
            dve.wait_ge(s("dve_init"), 2)

        def head_max(b, g, u):
            j, t = u // TB, u % TB
            wait(dve, s("pe_a"), UNITS * NG, b, UNITS * g + u + 1)
            v.reduce_max(mxs[:, t, g * GH + j:g * GH + j + 1], score[u % 2][:, :], AX.X).then_inc(s("dve_mx"), 1)

        def negate_maxima(b, g):
            wait(dve, s("dve_mx"), UNITS * NG, b, UNITS * (g + 1))
            ch = Link("dve_chain_m", NG * 4, b, 4 * g)
            hs = heads(g)
            scl = scs[:, b.par, 0:TB * NH].rearrange("p (t h) -> p t h", t=TB)[:, :, hs]
            ch(v.tensor_tensor(mf[:, :, hs], mxs[:, :, hs], scl, ALU.max))
            wait(dve, s("pe_mt"), NG, b, g)
            n = lambda k: nmp[:, :, k * GH:(k + 1) * GH]
            ch(v.tensor_scalar(n(0), mf[:, :, hs], -1.0, None, ALU.mult))
            ch(v.scalar_tensor_tensor(nmr[:, :, :], mf[:, :, hs], -1.0, n(0), ALU.mult, ALU.subtract))
            ch(v.tensor_copy(n(1), nmr[:, :, :]))
            v.tensor_tensor(n(2), nmr[:, :, :], n(1), ALU.subtract).then_inc(s("dve_nm"), 1)
            wait(dve, s("act_pcls"), NG, b, g + 1 - NG)
            v.tensor_tensor(dsc[:, :, hs], scl, mf[:, :, hs], ALU.subtract).then_inc(s("dve_dsc"), 1)
            ch.end(4 * (g + 1))

        def normalise(b, g):
            wait(dve, s("pe_tg"), NG, b, g + 1)
            wait(dve, s("act_pcls"), NG, b, g + 1)
            wait(dve, s("pool_add"), NG, b, g + 1 - NG)
            wait(dve, s("pool_qi2"), 2, b, -2)
            ch = Link("dve_chain_g", NG * 2, b, 2 * g)
            got = d2[:, :].rearrange("p (t j w) -> p t j w", t=TB, w=VW)
            pk = pcls[:, b.par, :, heads(g)]
            ch(v.tensor_tensor(den[:, :, :], got[:, :, :, 0], pk, ALU.add))
            ch(v.reciprocal(rinv[:, :, :], den[:, :, :]))
            o = o_sb[:, b.par, :, :].rearrange("p t (h d) -> p t h d", d=HD)[:, :, heads(g), :]
            v.tensor_tensor(o, got[:, :, :, 1:1 + HD], bcast(rinv[:, :, :], 3, HD), ALU.mult).then_inc(s("dve_o"), 1)
            v.tensor_tensor(pr[:, :, heads(g)], pk, rinv[:, :, :], ALU.mult).then_inc(s("dve_pr"), 1)
            ch.end(2 * (g + 1))

        def scales(ch, am, ax, rax, comb, aq, rs):
            ch(v.tensor_scalar(ax[:, :], am[:, :], rs[:, :], 1e-5, ALU.mult, ALU.max))
            ch(v.reciprocal(rax[:, :], ax[:, :]))
            ch(v.tensor_scalar(comb[:, :], rax[:, :], 127.0, rs[:, :], ALU.mult, ALU.mult))

        def norm_tokens(b, x, nt, np_, src, bn, mv, ve, chain):
            ch = Link(chain, 2 * nt, b)
            for t in range(nt):
                ch.go(v.bn_stats(bn[0:np_, t, :], src[0:np_, t, :]))
            ch.hold()
            for t in range(nt):
                ch.go(v.bn_aggr(mv[0:np_, t, :], bn[0:np_, t, :]))
            ch.wait()
            ch.end(2 * nt)

        def router(b, x, nt, np_):
            P = slice(0, np_)
            wait(dve, s("pe_lg" + x), 1, b, 1)
            signal(v.tensor_copy(lg[P, 0:nt, :], d2[P, 0:nt * E].rearrange("p (t e) -> p t e", e=E)),
                   "dve_lg" + x, 1, b, 1)
            ch = Link("dve_chain_r" + x, 10, b)
            js, jps = (bcast(cst[P, k:k + E], 1, nt) for k in (C_J, C_JP))
            m, tmp = (m1, m2), rtmp[P, 0:nt, :]
            for k in range(2):
                ch(v.tensor_reduce(out=m[k][P, 0:nt], in_=lg[P, 0:nt, :], axis=AX.X, op=ALU.max))
                if k == 1:
                    wait(dve, s("act_e" + x), 1, b, 0)
                    v.tensor_tensor(e21[P, 0:nt], m2[P, 0:nt], m1[P, 0:nt], ALU.subtract).then_inc(s("dve_e" + x), 1)
                ch(v.tensor_tensor(tmp, lg[P, 0:nt, :], bcast(m[k][P, 0:nt], 2, E), ALU.is_equal))
                ch(v.scalar_tensor_tensor(tmp, tmp, -float(E), jps, ALU.mult, ALU.add))
                ch(v.tensor_reduce(out=ix[P, 0:nt], in_=tmp, axis=AX.X, op=ALU.min))
                ch(v.tensor_tensor(oh[P, k, 0:nt, :], js, bcast(ix[P, 0:nt], 2, E), ALU.is_equal))
                if k == 0:
                    signal(v.scalar_tensor_tensor(lg[P, 0:nt, :], oh[P, 0, 0:nt, :], -3e38, lg[P, 0:nt, :],
                                                  ALU.mult, ALU.add), "dve_masked" + x, 1, b, 1)
            wait(dve, s("pe_rk" + x), 1, b, 0)
            v.tensor_tensor(picked[P, 0:nt, :], oh[P, 0, 0:nt, :], oh[P, 1, 0:nt, :], ALU.add) \
                .then_inc(s("dve_picked" + x), 1)
            ch.end(10)

        def payload(b, x, nt, np_, rows):
            P = slice(0, np_)
            ch = Link("dve_chain_s" + x, 6, b)
            wait(dve, s("act_e" + x), 1, b, 1)
            ch(v.tensor_scalar(wts[P, 0, 0:nt], e21e[P, 0:nt], 1.0, None, ALU.add))
            ch(v.reciprocal(wts[P, 0, 0:nt], wts[P, 0, 0:nt]))
            ch(v.tensor_tensor(wts[P, 1, 0:nt], e21e[P, 0:nt], wts[P, 0, 0:nt], ALU.mult))
            wait(dve, s("pe_rk" + x), 1, b, 1)
            ch(v.tensor_tensor(pos[P, 0:nt, :], d2[P, 0:nt * E].rearrange("p (t e) -> p t e", e=E),
                               bcast(run[P, :], 1, nt), ALU.add))
            signal(v.tensor_tensor(run[:, :], run[:, :], d2[:, TB * E:(TB + 1) * E], ALU.add), "dve_rk" + x, 1, b, 1)
            ch(v.tensor_tensor(oh[P, :, 0:nt, :], oh[P, :, 0:nt, :], bcast(pos[P, 0:nt, :], 1, 2), ALU.mult))
            ch(v.tensor_reduce(out=slot[P, :, 0:nt], in_=oh[P, :, 0:nt, :], axis=AX.X, op=ALU.add))
            wait(dve, s("scattered"), 16 * 2 * TB, b, 0)
            signal(v.tensor_copy(slot_i[P, :, 0:nt], slot[P, :, 0:nt]), "dve_sl" + x, 1, b, 1)
            signal(v.tensor_copy(pay[P, :, 0:nt, 0], bcast(rows, 1, 2)), "dve_row" + x, 1, b, 1)
            v.tensor_copy(pay[P, :, 0:nt, 1].bitcast(F32), wts[P, :, 0:nt]).then_inc(s("dve_pay" + x), 1)
            ch.end(6)

        def body(P, C, W, X):
            for g in range(NG):
                for u in range(UNITS):
                    if u % 4 == 0:
                        P, C, W, X = fresh(dve, UNITS * g + u, P, C, W, X)
                        st, tg, mt = in_slot(g, P, C, W)
                    at = UNITS * g + u
                    if C.ok:
                        head_max(C, g, u)
                    if u == 7 and tg[0].ok:
                        normalise(*tg)
                    if P.ok and at % 4 == 1 and at < 16:
                        e = at // 4
                        wait(dve, s("pe_up"), EC, P, e + 1)
                        wait(dve, s("act_relu"), EC, P, e + 1)
                        if e == 0:
                            wait(dve, s("pe_h"), 2, P, 0)
                        v.tensor_tensor(hid[:, e, :], d1[:, :], relu[:, e % 2, :], ALU.mult).then_inc(s("dve_hid"), 1)
                    if at == 6 and X.ok:
                        router(X, "", TB, 128)
                    if at == 11 and X.ok:
                        payload(X, "", TB, 128, row[:, :])
                        wait(dve, s("dve_pay"), 1, X, 1)
                        signal(v.tensor_scalar(row[:, :], row[:, :], float(SEQ), None, ALU.add), "dve_rows", 1, X, 1)
                    if P.ok and at == 22:
                        wait(dve, s("act_h"), 2, P, 2)
                        norm_tokens(P, "", TB, 128, h_sb, bn1, mv1, ve1, "dve_chain_n1")
                        v.tensor_scalar(ve1[:, :], mv1[:, :, 1], EPS, None, ALU.add).then_inc(s("dve_ve1"), 1)
                    if P.ok and at == 24:
                        wait(dve, s("pool_r1"), 1, P, 1)
                        v.scalar_tensor_tensor(nb1[:, :], mv1[:, :, 0], -1.0, rstd1[:, :], ALU.mult, ALU.mult) \
                            .then_inc(s("dve_nb1"), 1)
                        signal(v.tensor_tensor(vr1[:, :], mv1[:, :, 1], rstd1[:, :], ALU.mult), "dve_vr1", 1, P, 1)
                        wait(dve, s("pe_st1"), 1, P, 0)
                        v.scalar_tensor_tensor(sums1[:, 1, :], vr1[:, :], float(D), rstd1[:, :], ALU.mult, ALU.mult) \
                            .then_inc(s("dve_sst"), 1)
                    if P.ok and at == 28:
                        wait(dve, s("pe_st1"), 1, P, 1)
                        signal(v.tensor_reduce(out=red1[:, :], in_=d2[:, 0:2 * TB].rearrange("p (a t) -> p a t", a=2),
                                               axis=AX.X, op=ALU.add), "dve_ms", 1, P, 1)
                        ch = Link("dve_chain_p", 8, P)
                        ch(v.scalar_tensor_tensor(ms1[:, :], red1[:, :], 1.0 / total, cls_f[:, 0:2], ALU.mult, ALU.add))
                        ch(v.tensor_tensor(msq1[:, 0:1], ms1[:, 0:1], ms1[:, 0:1], ALU.mult))
                        v.scalar_tensor_tensor(msq1[:, 1:2], ms1[:, 1:2], EPS, msq1[:, 0:1], ALU.add, ALU.subtract) \
                            .then_inc(s("dve_ve"), 1)
                        wait(dve, s("act_xh"), TB, P, TB)
                        ch.go(v.tensor_scalar(xn[:, :, :], xn[:, :, :], ms1[:, 0:1], None, ALU.subtract))
                        ch(v.tensor_tensor(am1b[:, :], cls_f[:, 2:3], ms1[:, 0:1], ALU.subtract))
                        signal(v.tensor_reduce(out=am1[:, 0:TB], in_=xn[:, :, :], axis=AX.X, op=ALU.max,
                                               apply_absolute_value=True), "dve_am", 1, P, 1)
                        ch(v.scalar_tensor_tensor(am1[:, TB:TB + 1], ms1[:, 0:1], cls_f[:, 3:4], am1b[:, :],
                                                  ALU.subtract, ALU.max))
                        wait(dve, s("pool_rs"), 1, P, 1)
                        scales(ch, am1, ax1, rax1, comb1, aq1, rs1)
                        ch.end(8)
                        wait(dve, s("pe_aqb"), 1, P, 0)
                        signal(v.tensor_scalar(aq1[:, :], ax1[:, :], 1.0 / 127.0, None, ALU.mult), "dve_aq", 1, P, 1)
                        wait(dve, s("act_vc"), 1, P, 0)
                        v.tensor_scalar(aqv[:, :], aq1[:, :], w_fac[:, 2:3], None, ALU.mult).then_inc(s("dve_aqv"), 1)
                        for t in range(TB):
                            v.tensor_scalar(xn[:, t, :], xn[:, t, :], comb1[:, t:t + 1], MAGIC, ALU.mult, ALU.add) \
                                .then_inc(s("dve_q1"), 1)
                        ch = Link("dve_chain_c", 2, P)
                        ch(v.tensor_scalar(cls_q[:, :], cls_t[:, :], ms1[:, 0:1], None, ALU.subtract))
                        ch(v.tensor_scalar(cls_q[:, :], cls_q[:, :], comb1[:, TB:TB + 1], MAGIC, ALU.mult, ALU.add))
                        wait(dve, s("pe_cols"), 1, P, 0)
                        v.tensor_scalar(xq[:, :, S:SEQ].rearrange("p c o -> p (c o)"), cls_q[:, :], -MAGIC, None, ALU.add) \
                            .then_inc(s("dve_qc"), 1)
                    for k, (a, dst, first) in enumerate((("q", fq, 37), ("k", fk, 40))):
                        if P.ok and at == first:
                            wait(dve, s(f"act_{a}h"), 1, P, 0)
                            wait(dve, s(f"pool_r{a}"), 1, P, 0)
                            wait(dve, s("pe_t7"), 1, P, 0)
                            wait(dve, s("act_aqb"), 1, P, 1)
                            for fc in range(DC):
                                wait(dve, s(f"pe_{a}"), DC, P, fc + 1)
                                v.scalar_tensor_tensor(dst[:, fc, 0:S], (d0, d1)[fc][:, :], w_fac[:, k:k + 1],
                                                       aqb[:, :], ALU.mult, ALU.mult).then_inc(s(f"dve_f{a}"), 1)
                    if W.ok and at == 40:
                        wait(dve, s("pe_pvc"), 1, W, 1)
                        signal(v.tensor_tensor(pvm[:, :, :], d2[:, 0:NG * NH].rearrange("p (g h) -> p g h", g=NG),
                                               gh_mask, ALU.mult), "dve_pvc", 1, W, 1)
                        v.tensor_reduce(out=pv4[:, :], in_=pvm[:, :, :], axis=AX.X, op=ALU.add).then_inc(s("dve_pv4"), 1)
                    if W.ok and at == 43:
                        wait(dve, s("pe_tr"), 1, W, 1)
                        ch = Link("dve_chain_w", 11, W)
                        got = d2[0:NG, 0:128].rearrange("p (j w) -> p j w", w=VW)
                        ch(v.reciprocal(rc[:, :], got[:, :, 0]))
                        wait(dve, s("pool_qi2"), 2, W, 0)
                        signal(v.tensor_tensor(oc[:, :, :], got[:, :, 1:1 + HD], bcast(rc[:, :], 2, HD), ALU.mult),
                               "dve_oc", 1, W, 1)
                        ch.go(v.bn_stats(bnc[:, :], oc[:, :, :].rearrange("p j d -> p (j d)")))
                        wait(dve, s("pool_add"), NG, W, NG)
                        flat = o_sb[:, W.par, :, :].rearrange("p t n -> p (t n)")
                        for k in range(2):
                            ch.go(v.bn_stats(bn2[:, k, :], flat[:, k * 512:(k + 1) * 512]))
                        ch.hold()
                        ch.go(v.bn_aggr(mvc[:, :], bnc[:, :]))
                        ch(v.bn_aggr(mv2[:, :], bn2[:, :, :].rearrange("p k n -> p (k n)")))
                        ch.go(v.scalar_tensor_tensor(e2[:, :], mv2[:, 0:1], mv2[:, 0:1], mv2[:, 1:2], ALU.mult, ALU.add))
                        ch(v.scalar_tensor_tensor(e2c[:, :], mvc[:, 0:1], mvc[:, 0:1], mvc[:, 1:2], ALU.mult, ALU.add))
                        wait(dve, s("pe_w1"), 1, W, 0)
                        per, perc = TB * D / total, GH * HD / total
                        ch.go(v.tensor_scalar(st2[:, 0:1], mv2[:, 0:1], per, None, ALU.mult))
                        ch.go(v.tensor_scalar(st2[:, 1:2], e2[:, :], per, None, ALU.mult))
                        ch.go(v.tensor_scalar(st2c[:, 0:1], mvc[:, 0:1], perc, None, ALU.mult))
                        ch.wait()
                        v.tensor_scalar(st2c[:, 1:2], e2c[:, :], perc, None, ALU.mult).then_inc(s("dve_st2"), 1)
                        ch.end(11)
                    if P.ok and at == 45:
                        wait(dve, s("pe_cols"), 1, P, 1)
                        for k, dst in enumerate((fq, fk)):
                            v.tensor_scalar(dst[:, :, S:SEQ].rearrange("p c o -> p (c o)"), d2[:, D + 2 * k:D + 2 * k + 2],
                                            aq1[:, TB:TB + 1], w_fac[:, k:k + 1], ALU.mult, ALU.mult) \
                                .then_inc(s("dve_cc"), 1)
                        wait(dve, s("dve_cc"), 2, P, 2)
                        for dst, src in ((kbd, fk), (qbd, fq)):
                            v.tensor_tensor(dst[:, :, :], bd_mask, src[:, :, S:SEQ].broadcast_to([128, DC, NH]), ALU.mult) \
                                .then_inc(s("dve_bd"), 1)
                    if W.ok and at == 47:
                        wait(dve, s("pe_w1"), 1, W, 1)
                        signal(v.tensor_copy(ms2[:, :], d2[:, 0:2]), "dve_ms2", 1, W, 1)
                        ch = Link("dve_chain_v", 7, W)
                        ch(v.tensor_tensor(msq2[:, 0:1], ms2[:, 0:1], ms2[:, 0:1], ALU.mult))
                        v.scalar_tensor_tensor(msq2[:, 1:2], ms2[:, 1:2], EPS, msq2[:, 0:1], ALU.add, ALU.subtract) \
                            .then_inc(s("dve_ve2"), 1)
                        o = o_sb[:, W.par, :, :]
                        cflat = oc[:, :, :].rearrange("p j d -> p (j d)")
                        ch.go(v.tensor_scalar(o, o, ms2[:, 0:1], None, ALU.subtract))
                        ch(v.tensor_scalar(cflat, cflat, ms2[0:NG, 0:1], None, ALU.subtract))
                        wait(dve, s("pool_amc"), 1, W, 0)
                        v.tensor_reduce(out=amc[:, :], in_=cflat, axis=AX.X, op=ALU.max, apply_absolute_value=True) \
                            .then_inc(s("dve_amc"), 1)
                        ch(v.tensor_reduce(out=am2[:, 0:TB], in_=o, axis=AX.X, op=ALU.max, apply_absolute_value=True))
                        wait(dve, s("pool_rs2"), 1, W, 1)
                        wait(dve, s("pool_amc"), 1, W, 1)
                        scales(ch, am2, ax2, rax2, comb2, aqo, rs2)
                        ch.end(7)
                        signal(v.tensor_scalar(aqo[:, :], ax2[:, :], 1.0 / 127.0, w_fac[:, 3:4], ALU.mult, ALU.mult),
                               "dve_aqo", 1, W, 1)
                        for t in range(TB):
                            v.tensor_scalar(o[:, t, :], o[:, t, :], comb2[:, t:t + 1], MAGIC, ALU.mult, ALU.add) \
                                .then_inc(s("dve_q2"), 1)
                        v.tensor_scalar(cflat, cflat, comb2[0:NG, TB:TB + 1], MAGIC, ALU.mult, ALU.add) \
                            .then_inc(s("dve_q2"), 1)
                    if P.ok and at == 49:
                        wait(dve, s("pe_t7"), 1, P, 1)
                        signal(v.tensor_copy(scs[:, P.par, :], d2[:, 0:(2 * TB + 1) * NH]), "dve_scs", 1, P, 1)
                    if P.ok and at == 51:
                        wait(dve, s("pool_par"), 1, P, 1)
                        both = scs[:, P.par, 2 * TB * NH:(2 * TB + 1) * NH]
                        ch = Link("dve_chain_q", 2, P)
                        ch(v.tensor_reduce(out=mc[:, :], in_=cmx[:, :].rearrange("p (t h) -> p h t", t=TB), axis=AX.X, op=ALU.max))
                        ch(v.tensor_tensor(mc[:, :], mc[:, :], both, ALU.max))
                        wait(dve, s("act_pc"), 1, P, 0)
                        v.tensor_tensor(pci[:, :, :], scs[:, P.par, TB * NH:(2 * TB + 1) * NH].rearrange("p (t h) -> p t h", h=NH),
                                        bcast(mc[:, :], 1, TB + 1), ALU.subtract).then_inc(s("dve_pci"), 1)
                        ch.end(2)
                    if W.ok and at == 57:
                        wait(dve, s("hw_in"), 16, W, 16)
                        for t in range(TB):
                            wait(dve, s("pe_y"), TB, W, t // 2 * 2 + 2)
                            v.scalar_tensor_tensor(hw[:, t, :], (d0, d1)[t // 2][:, D * (t % 2):D * (t % 2 + 1)],
                                                   aqo[:, t:t + 1], hw[:, t, :], ALU.mult, ALU.add) \
                                .then_inc(s("dve_h2"), 1)
                        wait(dve, s("pe_yc"), 1, W, 1)
                        wait(dve, s("h2c_stored"), 16, W, 0)
                        v.scalar_tensor_tensor(h2c[:, :], d2[0:1, 0:D], aqo[0:1, TB:TB + 1], cls_row[:, :], ALU.mult, ALU.add) \
                            .then_inc(s("dve_h2c"), 1)
                        wait(dve, s("dve_h2"), TB, W, TB)
                        norm_tokens(W, "", TB, 128, hw, bn3, mv3, ve3, "dve_chain_n3")
                        v.tensor_scalar(ve3[:, :], mv3[:, :, 1], EPS, None, ALU.add).then_inc(s("dve_ve3"), 1)
                    if W.ok and at == 61:
                        wait(dve, s("pool_r3"), 1, W, 1)
                        wait(dve, s("act_x2"), TB, W, 0)
                        v.scalar_tensor_tensor(nb3[:, :], mv3[:, :, 0], -1.0, rstd3[:, :], ALU.mult, ALU.mult) \
                            .then_inc(s("dve_nb3"), 1)
                    if u == UNITS - 1 and C.ok:
                        negate_maxima(C, g)
        if stage == STEPS:
            steps(dve, body)
        if stage == CLASS_TOKENS:
            n = images
            dve.wait_ge(s("cls_back"), 16)
            norm_tokens(one, "_c", 1, n, hw, bn3, mv3, ve3, "dve_chain_n3_c")
            v.tensor_scalar(ve3[0:n, 0:1], mv3[0:n, 0:1, 1], EPS, None, ALU.add).then_inc(s("dve_ve3_c"), 1)
            dve.wait_ge(s("pool_r3_c"), 1)
            v.scalar_tensor_tensor(nb3[0:n, 0:1], mv3[0:n, 0:1, 0], -1.0, rstd3[0:n, 0:1], ALU.mult, ALU.mult) \
                .then_inc(s("dve_nb3_c"), 1)
            router(one, "_c", 1, n)
            payload(one, "_c", 1, n, cst[0:n, C_CROW:C_CROW + 1])
            ch = Link("dve_chain_t", 0, one)
            c0 = cst[0:1, C_BASE:C_BASE + E]
            ch(v.tensor_tensor(ncnt[:, :], run[0:1, :], c0, ALU.subtract))
            ch(v.tensor_scalar(ntile[:, :], ncnt[:, :], 1.0 / 128, 127.0 / 256, ALU.mult, ALU.add))
            ch(v.tensor_scalar(ntile[:, :], ntile[:, :], MAGIC, -MAGIC, ALU.add, ALU.add))
            ch(v.tensor_copy(tend[:, :], ntile[:, :]))
            for e in range(1, E):
                ch(v.tensor_tensor(tend[:, e:e + 1], tend[:, e - 1:e], ntile[:, e:e + 1], ALU.add))
            ch(v.tensor_tensor(toff[:, :], tend[:, :], ntile[:, :], ALU.subtract))
            ch(v.scalar_tensor_tensor(toff[:, :], toff[:, :], -128.0, c0, ALU.mult, ALU.add))
            ch(v.tensor_tensor(tstep[:, 1:E], toff[:, 1:E], toff[:, 0:E - 1], ALU.subtract))
            idx = cst[0:1, C_BASE + E:C_BASE + E + tiles]
            ch(v.tensor_scalar(trow[:, :], idx, 128.0, toff[:, 0:1], ALU.mult, ALU.add))
            ch(v.tensor_scalar(texp[:, :], idx, 0.0, None, ALU.mult))
            for e in range(1, E):
                ch(v.tensor_scalar(tge[:, :], idx, tend[:, e - 1:e], None, ALU.is_ge))
                ch(v.tensor_tensor(texp[:, :], texp[:, :], tge[:, :], ALU.add))
                ch(v.scalar_tensor_tensor(trow[:, :], tge[:, :], tstep[:, e:e + 1], trow[:, :], ALU.mult, ALU.add))
            ch(v.tensor_copy(tile_row[:, :], trow[:, :]))
            ch(v.tensor_copy(tile_expert[:, :], texp[:, :]))

    for stage in (SETUP, STEPS, CLASS_TOKENS):
        with nc.Block() as block:

            @block.sync
            def _(sp):
                sync_program(sp, stage)

            @block.tensor
            def _(pe):
                tensor_program(pe, stage)

            @block.scalar
            def _(act):
                scalar_program(act, stage)

            @block.gpsimd
            def _(pool):
                gpsimd_program(pool, stage)

            @block.vector
            def _(dve):
                vector_program(dve, stage)

        nc.clear_and_free_semaphores(list(sems.values()))
        nc.all_engine_barrier()
        sems.clear()


class Tile:

    UNROLL = 8

    def __init__(self, k, n=None):
        self.k, self.n = k, n
        self.v = k if n is None else self.UNROLL * n + k

    def next(self, by):
        return Tile(self.k + by, self.n)

    def place(self, ring):
        return self.k % ring

    def laps(self, ring):
        return self.k // ring + 1 + (0 if self.n is None else self.UNROLL // ring * self.n)


def expert_phase(nc, ctx, images, gate_up_w, down_w, out, x2_dram, list_dram,
                 cst, tile_row, tile_expert, banks):
    tokens, cap, tiles, list_rows = geometry(images)
    sb = lambda name, shape, dt=F32: ctx.enter_context(nc.sbuf_tensor(name, shape, dt))
    sem = lambda name: ctx.enter_context(nc.semaphore(name))
    W = F * 2
    LISTS, ROWS, AHEAD = 8, 4, 3
    gu = [sb(f"gu_{p}", [128, E, DC, W], BF16) for p in "hl"]
    dn = [sb(f"dn_{p}", [128, E, FC, D], BF16) for p in "hl"]
    gu_in = sb("gu_in", [128, 2, DC, W])
    dn_in = sb("dn_in", [128, 2, FC, D])
    ident = sb("ident", [128, 128])
    ids = sb("ids", [128, LISTS, 2], I32)
    xg = sb("xg", [128, ROWS, D])
    xh = sb("xh", [128, 2, DC, 128], BF16)
    xl = sb("xl", [128, 2, DC, 128], BF16)
    act_g = sb("act_g", [128, F])
    hid = sb("hid_e", [128, F])
    hh = sb("hh", [128, 2, FC, 128], BF16)
    hl = sb("hl", [128, 2, FC, 128], BF16)
    y_sb = sb("y_sb", [128, 2, D])
    w_in = [sem("w_in0"), sem("w_in1")]
    w_high, w_low = sem("w_high"), sem("w_low")
    ids_in = [sem(f"ids_in{k}") for k in range(LISTS)]
    x_in = [sem(f"xg_in{k}") for k in range(ROWS)]
    pe_xt, act_xh, dve_xl = sem("pe_xt"), sem("act_xh_e"), sem("dve_xl")
    pe_g, pe_u, act_silu, dve_hid = sem("pe_g"), sem("pe_u"), sem("act_silu"), sem("dve_hid_e")
    pe_ht, act_hh, dve_hl, pe_y, act_y = sem("pe_ht"), sem("act_hh"), sem("dve_hl"), sem("pe_y_e"), sem("act_y")
    added, id_set, held = sem("added"), sem("id_set"), sem("held")
    gate_b, up_b = banks[0:2], banks[2:4]
    xt_b, ht_b, y_b = banks[4], banks[5], banks[6]
    block = ctx.enter_context(nc.Block())
    blk = lambda t: slice(t * 128, (t + 1) * 128)

    def over_tiles(eng, body):
        unroll = Tile.UNROLL
        for k in range(unroll):
            body(Tile(k), tiles)
        if tiles > 2 * unroll:
            with eng.Fori(1, tiles // unroll - 1) as n:
                for k in range(unroll):
                    body(Tile(k, n), None)
        for k in range(max(unroll, tiles - unroll), tiles):
            body(Tile(k), tiles)

    def has(i, n):
        return i.n is not None or 0 <= i.v < n

    def upto(eng, sem_, value):
        if not isinstance(value, int) or value > 0:
            eng.wait_ge(sem_, value)

    @block.sync
    def _(sp):
        for e in range(E):
            upto(sp, w_high, 2 * (e - 1))
            upto(sp, w_low, 2 * (e - 1))
            sp.dma_start(gu_in[:, e % 2, :, :], gate_up_w[e * D:(e + 1) * D, :].rearrange("(c p) n -> p c n", p=128)) \
                .then_inc(w_in[e % 2], 16)
            sp.dma_start(dn_in[:, e % 2, :, :], down_w[e * F:(e + 1) * F, :].rearrange("(c p) n -> p c n", p=128)) \
                .then_inc(w_in[e % 2], 16)

        def body(i, n):
            upto(sp, added, (i.v - LISTS + 1) * 16)
            sp.sem_inc(held, 1)
            first = sp.value_load(tile_row[0:1, bass.ds(i.v, 1)], min_val=0, max_val=list_rows - 128)
            k = i.place(LISTS)
            sp.dma_start(ids[:, k, :], list_dram[bass.ds(first, 128), :]).then_inc(ids_in[k], 16)
        over_tiles(sp, body)

    @block.gpsimd
    def _(pool):
        def rows(i):
            return bass.IndirectOffsetOnAxis(ap=ids[:, i.place(LISTS), 0:1], axis=0)

        def fetch(i):
            upto(pool, ids_in[i.place(LISTS)], i.laps(LISTS) * 16)
            upto(pool, pe_xt, i.v - ROWS + 1)
            pool.sem_inc(held, 1)
            nc.gpsimd.indirect_dma_start(out=xg[:, i.place(ROWS), :], out_offset=None, in_=x2_dram, in_offset=rows(i)) \
                .then_inc(x_in[i.place(ROWS)], 16)

        def body(i, n):
            if has(i.next(AHEAD), n):
                fetch(i.next(AHEAD))
            upto(pool, act_y, i.v + 1)
            upto(pool, added, i.v * 16)
            pool.sem_inc(held, 1)
            nc.gpsimd.indirect_dma_start(out=out, out_offset=rows(i), in_=y_sb[:, i.place(2), :], in_offset=None,
                                         bounds_check=tokens - 1, oob_is_err=False, compute_op=ALU.add) \
                .then_inc(added, 16)
        for k in range(AHEAD):
            fetch(Tile(k))
        over_tiles(pool, body)
        pool.wait_ge(added, 16 * tiles)

    @block.tensor
    def _(pe):
        mm = nc.tensor.matmul

        def transpose_x(i):
            upto(pe, x_in[i.place(ROWS)], i.laps(ROWS) * 16)
            upto(pe, act_xh, i.v)
            upto(pe, dve_xl, i.v)
            for c in range(DC):
                last = nc.tensor.transpose(xt_b[:, blk(c)], xg[:, i.place(ROWS), blk(c)], ident[:, :])
            last.then_inc(pe_xt, 1)

        def down(i):
            e = pe.value_load(tile_expert[0:1, bass.ds(i.v, 1)], min_val=0, max_val=E - 1)
            upto(pe, act_hh, i.v + 1)
            upto(pe, dve_hl, i.v + 1)
            upto(pe, act_y, i.v)
            n = 0
            for c in range(FC):
                for a, w in ((hh, dn[0]), (hh, dn[1]), (hl, dn[0])):
                    n += 1
                    last = mm(y_b[:, 0:D], a[:, i.place(2), c, :], w[:, bass.ds(e, 1), c, :],
                              start=(n == 1), stop=(n == 3 * FC))
            last.then_inc(pe_y, 1)

        def body(i, n):
            e = pe.value_load(tile_expert[0:1, bass.ds(i.v, 1)], min_val=0, max_val=E - 1)
            k = i.place(2)
            upto(pe, act_xh, i.v + 1)
            upto(pe, dve_xl, i.v + 1)
            upto(pe, dve_hid, i.v - 1)
            for bank, lo, done in ((gate_b, 0, pe_g), (up_b, F, pe_u)):
                m = 0
                for c in range(DC):
                    for a, w in ((xh, gu[0]), (xh, gu[1]), (xl, gu[0])):
                        m += 1
                        last = mm(bank[k][:, :], a[:, k, c, :], w[:, bass.ds(e, 1), c, lo:lo + F],
                                  start=(m == 1), stop=(m == 3 * DC))
                last.then_inc(done, 1)
            if has(i.next(1), n):
                transpose_x(i.next(1))
            if has(i.next(-1), n):
                down(i.next(-1))
            upto(pe, dve_hid, i.v + 1)
            upto(pe, act_hh, i.v)
            upto(pe, dve_hl, i.v)
            for c in range(FC):
                last = nc.tensor.transpose(ht_b[:, blk(c)], hid[:, blk(c)], ident[:, :])
            last.then_inc(pe_ht, 1)

        pe.wait_ge(id_set, 1)
        transpose_x(Tile(0))
        pe.wait_ge(w_high, 2 * E)
        pe.wait_ge(w_low, 2 * E)
        over_tiles(pe, body)
        down(Tile(tiles - 1))

    @block.scalar
    def _(act):
        f = nc.scalar.activation
        for e in range(E):
            act.wait_ge(w_in[e % 2], 32 * (e // 2) + 32)
            f(gu[0][:, e, :, :], gu_in[:, e % 2, :, :], ACT.Copy).then_inc(w_high, 1)
            f(dn[0][:, e, :, :], dn_in[:, e % 2, :, :], ACT.Copy).then_inc(w_high, 1)

        def high_x(i):
            upto(act, pe_xt, i.v + 1)
            upto(act, pe_u, i.v - 1)
            f(xh[:, i.place(2), :, :], xt_b[:, 0:D].rearrange("p (c n) -> p c n", c=DC), ACT.Copy).then_inc(act_xh, 1)

        def take_y(i):
            upto(act, pe_y, i.v + 1)
            upto(act, added, (i.v - 1) * 16)
            f(y_sb[:, i.place(2), :], y_b[:, 0:D], ACT.Copy, scale=ids[:, i.place(LISTS), 1:2].bitcast(F32)).then_inc(act_y, 1)

        def body(i, n):
            upto(act, pe_g, i.v + 1)
            upto(act, dve_hid, i.v)
            f(act_g[:, :], gate_b[i.place(2)][:, :], ACT.Silu).then_inc(act_silu, 1)
            if has(i.next(1), n):
                high_x(i.next(1))
            if has(i.next(-1), n):
                take_y(i.next(-1))
            upto(act, pe_ht, i.v + 1)
            upto(act, pe_y, i.v - 1)
            f(hh[:, i.place(2), :, :], ht_b[:, :].rearrange("p (c n) -> p c n", c=FC), ACT.Copy).then_inc(act_hh, 1)
        high_x(Tile(0))
        over_tiles(act, body)
        take_y(Tile(tiles - 1))

    @block.vector
    def _(dve):
        v = nc.vector
        v.tensor_copy(ident[:, :], cst[:, C_ID:C_ID + 128]).then_inc(id_set, 1)
        for e in range(E):
            for dst, src, m in ((gu, gu_in, 1), (dn, dn_in, 2)):
                dve.wait_ge(w_high, 2 * e + m)
                v.tensor_tensor(dst[1][:, e, :, :], src[:, e % 2, :, :], dst[0][:, e, :, :], ALU.subtract).then_inc(w_low, 1)

        def low_x(i):
            upto(dve, act_xh, i.v + 1)
            v.tensor_tensor(xl[:, i.place(2), :, :], xt_b[:, 0:D].rearrange("p (c n) -> p c n", c=DC),
                            xh[:, i.place(2), :, :], ALU.subtract).then_inc(dve_xl, 1)

        def body(i, n):
            upto(dve, act_silu, i.v + 1)
            upto(dve, pe_u, i.v + 1)
            upto(dve, pe_ht, i.v)
            v.tensor_tensor(hid[:, :], up_b[i.place(2)][:, :], act_g[:, :], ALU.mult).then_inc(dve_hid, 1)
            if has(i.next(1), n):
                low_x(i.next(1))
            upto(dve, act_hh, i.v + 1)
            v.tensor_tensor(hl[:, i.place(2), :, :], ht_b[:, :].rearrange("p (c n) -> p c n", c=FC),
                            hh[:, i.place(2), :, :], ALU.subtract).then_inc(dve_hl, 1)
        low_x(Tile(0))
        over_tiles(dve, body)


def kernel(x, cls_tok, L0_tok_W0, L0_tok_W1, L0_tok_Wo, L0_attn_w_q, L0_attn_w_k, L0_attn_w_v, L0_attn_w_o,
           L0_ffn_gate_w, L0_ffn_gate_up_w, L0_ffn_down_w):
    import numpy as np
    import concourse.bacc as bacc
    from concourse.bass_utils import run_bass_kernel_spmd

    images = x.shape[0]
    a = lambda t: np.ascontiguousarray(np.asarray(t))
    arrays = {
        "x_t": a(np.asarray(x)[:, :, :, 0].transpose(0, 2, 1)).reshape(images * D, S),
        "cls": a(cls_tok).reshape(1, D),
        "w0_t": a(np.asarray(L0_tok_W0).T),
        "w1_t": a(np.asarray(L0_tok_W1).T),
        "wo_t": a(np.asarray(L0_tok_Wo).T),
        "attn_w_t": a(np.stack([np.asarray(w).T for w in (L0_attn_w_q, L0_attn_w_k, L0_attn_w_v, L0_attn_w_o)])),
        "gate_w": a(L0_ffn_gate_w),
        "gate_up_w": a(L0_ffn_gate_up_w).reshape(E * D, 2 * F),
        "down_w": a(L0_ffn_down_w).reshape(E * F, D),
        "consts": constants(images),
    }
    nc = bacc.Bacc("TRN2", target_bir_lowering=False, num_devices=1)
    args = [nc.dram_tensor(n, t.shape, mybir.dt.from_np(t.dtype), kind="ExternalInput").ap() for n, t in arrays.items()]
    out = nc.dram_tensor("out", (images * SEQ, D), F32, kind="ExternalOutput").ap()
    vit_layer(nc, images, *args, out)
    r = run_bass_kernel_spmd(nc, [arrays], core_ids=[0])
    return r.results[0]["out"].reshape(images, SEQ, D)
```

```python
import concourse.bass as bass
from concourse import mybir
from contextlib import ExitStack

F32 = mybir.dt.float32
BF16 = mybir.dt.bfloat16
I32 = mybir.dt.int32
ALU = mybir.AluOpType
ACT = mybir.ActivationFunctionType
AX = mybir.AxisListType

D = 256
S = 512
SEQ = S + 1
DE = 512
NH, HD = 16, 16
E, F = 8, 512
EPS = 1e-5
TB = S // 128
DC = D // 128
EC = DE // 128
FC = F // 128
NG = 4
GH = NH // NG
UNITS = TB * GH
VW = 32
PARTS = "hml"
Q_STACK = ("h", "h", "hm", "ml")
K_STACK = ("hml", "hm", "h")
QK = len("".join(Q_STACK)) * HD
MROWS = 3
MAGIC = 1.5 * 2.0 ** 23

GATE_AT = (28, 33, 36, 40)
UP_AT = (30, 34, 38, 42)
HIDDEN_AT = (32, 35, 39, 43)
STATS_AT = (3, 7)
QK_AT = (22, 24, 26, 25)
ROUTER_AT = (6, 7, 10, 11)
RESIDUAL_AT = (57, 58)

C_ID, C_TRI = 0, 128
C_BD = 256
C_DG = C_BD + DC * VW
C_SEL = C_DG + NH * VW
C_J = C_SEL + NG * NG
C_JP = C_J + E
C_ROW = C_JP + E
C_CROW = C_ROW + TB
C_BASE = C_CROW + 1


def geometry(images):
    tokens = images * SEQ
    cap = -(-tokens // 128) * 128
    tiles = (2 * tokens + E * 127) // 128
    tiles = -(-tiles // Tile.UNROLL) * Tile.UNROLL
    return tokens, cap, tiles, (E - 1) * cap + tiles * 128


def constants(images):
    import numpy as np
    tokens, cap, tiles, rows = geometry(images)
    p = np.arange(128)[:, None]
    c = np.zeros((128, C_BASE + E + tiles), np.float32)
    c[:, C_ID:C_ID + 128] = np.eye(128)
    c[:, C_TRI:C_TRI + 128] = p < np.arange(128)
    h = np.arange(NH)
    for k in range(DC):
        c[:, C_BD + k * VW:C_BD + k * VW + NH] = h == k * (NH // DC) + p // HD
    c[:, C_DG:C_DG + NH * VW] = np.repeat(h == p % VW, VW, axis=1)
    for g in range(NG):
        c[:, C_SEL + g * NG + g] = (p % VW // GH == g)[:, 0]
    c[:, C_J:C_J + E] = np.arange(E)
    c[:, C_JP:C_JP + E] = np.arange(E) + E
    c[:, C_ROW:C_ROW + TB] = 1 + 128 * np.arange(TB) + p
    c[:, C_CROW] = (p * SEQ)[:, 0]
    c[:, C_BASE:C_BASE + E] = np.arange(E) * cap
    c[:, C_BASE + E:] = np.arange(tiles)
    return c


class At:

    def __init__(self, k, n=None, ok=True):
        self.k, self.n, self.ok, self.par = k, n, ok, k % 2
        self.v = k if n is None else 2 * n + k
        self.half = k // 2 if n is None else n + k // 2


def fresh(eng, at, *batches):
    if batches[0].n is None or isinstance(batches[0].n, int):
        return batches
    n = batches[0].n
    copy = eng.alloc_register(f"lap_{batches[0].k}_{at}")
    eng.reg_mov(copy, n)
    n = eng.snap(copy, min_val=n.min_val, max_val=n.max_val)
    return [At(b.k, n, b.ok) for b in batches]


def wait(eng, sem, per, b, n):
    value = b.v * per + n
    if not isinstance(value, int) or value > 0:
        eng.wait_ge(sem, value)


def bcast(ap, axis, n):
    shape = list(ap.shape)
    shape.insert(axis, n)
    return ap.unsqueeze(axis).broadcast_to(shape)


def vit_layer(nc, images, x_t, cls, w0_t, w1_t, wo_t, attn_w_t, gate_w, gate_up_w, down_w, consts, out):
    tokens, cap, tiles, list_rows = geometry(images)
    total = float(SEQ * D)
    dram = lambda name, shape, dt: nc.dram_tensor(name, shape, dt, kind="Internal").ap()
    h_dram = dram("h_dram", [images * S, D], F32)
    qk_dram = dram("qk_dram", [2, 2, NH, len(PARTS) * HD, S], BF16)
    x2_dram = dram("x2_dram", [tokens + 1, D], F32)
    list_dram = dram("list_dram", [list_rows, 2], I32)

    with ExitStack() as outer:
        sb = lambda name, shape, dt=F32: outer.enter_context(nc.sbuf_tensor(name, shape, dt))
        cst = sb("cst", [128, C_BASE + E + tiles])
        tile_row = sb("tile_row", [1, tiles], I32)
        tile_expert = sb("tile_expert", [1, tiles], I32)
        banks = [outer.enter_context(nc.psum_tensor(f"bank{k}", [128, 512], F32)) for k in range(8)]
        programs = token_phase(nc, outer, images, x_t, cls, w0_t, w1_t, wo_t, attn_w_t, gate_w, consts, out,
                               h_dram, qk_dram, x2_dram, list_dram, cst, tile_row, tile_expert, banks, total)
        with ExitStack() as inner:
            expert_phase(nc, inner, images, gate_up_w, down_w, out, x2_dram, list_dram,
                         cst, tile_row, tile_expert, banks, *programs)


def token_phase(nc, outer, images, x_t, cls, w0_t, w1_t, wo_t, attn_w_t, gate_w, consts, out,
                h_dram, qk_dram, x2_dram, list_dram, cst, tile_row, tile_expert, banks, total):
    tokens, cap, tiles, list_rows = geometry(images)
    keep = lambda name, shape, dt=F32: outer.enter_context(nc.sbuf_tensor(name, shape, dt))
    ctx = ExitStack()
    sb = lambda name, shape, dt=F32: ctx.enter_context(nc.sbuf_tensor(name, shape, dt))
    SETUP, STEPS, CLASS_TOKENS, TABLE = range(4)
    sems = {}

    def s(name):
        if name not in sems:
            sems[name] = nc.alloc_semaphore(f"{name}_{stage}")
        return sems[name]

    gate_sb = keep("gate_sb", [128, DC, E])
    ones_bf = keep("ones_bf", [128, 128], BF16)
    tri_bf = keep("tri_bf", [128, 128], BF16)
    neg_half = keep("neg_half", [128, 8])
    hw = keep("hw", [128, TB, D])
    bn3 = keep("bn3", [128, TB, 6])
    mv3 = keep("mv3", [128, TB, 2])
    ve3 = keep("ve3", [128, TB])
    rstd3 = keep("rstd3", [128, TB])
    nb3 = keep("nb3", [128, TB])
    x2 = keep("x2", [128, TB, D])
    x2_t = keep("x2_t", [128, DC, S])
    lg = keep("lg", [128, TB, E])
    rtmp = keep("rtmp", [128, TB, E])
    m1 = keep("m1", [128, TB])
    m2 = keep("m2", [128, TB])
    ix = keep("ix", [128, TB])
    oh = keep("oh", [128, 2, TB, E])
    picked = keep("picked", [128, TB, E], BF16)
    e21 = keep("e21", [128, TB])
    e21e = keep("e21e", [128, TB])
    wts = keep("wts", [128, 2, TB])
    pos = keep("pos", [128, TB, E])
    slot = keep("slot", [128, 2, TB])
    slot_i = keep("slot_i", [128, 2, TB], I32)
    pay = keep("pay", [128, 2, TB, 2], I32)
    run = keep("run", [128, E])
    ncnt = keep("ncnt", [1, E])
    ntile = keep("ntile", [1, E])
    tend = keep("tend", [1, E])
    toff = keep("toff", [1, E])
    tstep = keep("tstep", [1, E])
    tge = keep("tge", [1, tiles])
    trow = keep("trow", [1, tiles])
    texp = keep("texp", [1, tiles])

    w0 = sb("w0", [128, DC, DE])
    w1 = sb("w1", [128, DC, DE])
    wo = sb("wo", [128, EC, D])
    wq_int = sb("wq_int", [128, 4, DC, D], BF16)
    wo_cls = sb("wo_cls", [64, NG, D], BF16)
    ones = sb("ones", [128, 128])
    id_bf = sb("id_bf", [128, 128], BF16)
    w_mean = sb("w_mean", [128, 4])
    w_scale = sb("w_scale", [128, 4])
    w_fac = sb("w_fac", [128, 4])
    cls_row = sb("cls_row", [1, D])
    cls_norm = sb("cls_norm", [1, D])
    cls_stat = sb("cls_stat", [1, 6])
    cls_mv = sb("cls_mv", [1, 4])
    cls_fact = sb("cls_fact", [1, 4])
    cls_f = sb("cls_f", [128, 4])
    cls_t = sb("cls_t", [128, DC])
    identf = cst[:, C_ID:C_ID + 128]
    bd_mask = cst[:, C_BD:C_BD + DC * VW].rearrange("p (c h) -> p c h", c=DC)
    diagonal = cst[:, C_DG:C_DG + NH * VW]

    xt = sb("xt", [128, 2, DC, S])
    relu = sb("relu", [128, 2, S])
    hid = sb("hid", [128, EC, S])
    h_sb = sb("h_sb", [128, TB, D])
    xn = sb("xn", [128, TB, D])
    qi = sb("qi", [128, TB, D], BF16)
    xq = sb("xq", [128, DC, SEQ], BF16)
    bn1 = sb("bn1", [128, TB, 6])
    mv1 = sb("mv1", [128, TB, 2])
    ve1 = sb("ve1", [128, TB])
    rstd1 = sb("rstd1", [128, TB])
    nb1 = sb("nb1", [128, TB])
    vr1 = sb("vr1", [128, TB])
    sums1 = sb("sums1", [128, 2, TB])
    red1 = sb("red1", [128, 2])
    ms1 = sb("ms1", [128, 2])
    msq1 = sb("msq1", [128, 2])
    rs1 = sb("rs1", [128, 1])
    am1 = sb("am1", [128, TB + 1])
    am1b = sb("am1b", [128, 1])
    ax1 = sb("ax1", [128, TB + 1])
    rax1 = sb("rax1", [128, TB + 1])
    comb1 = sb("comb1", [128, TB + 1])
    aq1 = sb("aq1", [128, TB + 1])
    aqv = sb("aqv", [128, TB + 1])
    cls_q = sb("cls_q", [128, DC])
    aqb = sb("aqb", [128, S])
    fq = sb("fq", [128, DC, SEQ])
    fk = sb("fk", [128, DC, SEQ])
    rest = sb("rest", [128, DC, S])
    parts = {a + p: sb(f"part_{a}{p}", [128, DC, S], BF16) for a in "qk" for p in "hml"}
    kbd = sb("kbd", [128, DC, VW])
    qbd = sb("qbd", [128, DC, VW])
    sct = sb("sct", [128, S // 2])
    qs = sb("qs", [QK + MROWS, NH, S], BF16)
    ks = sb("ks", [128, NH, S], BF16)
    v_sb = sb("v_sb", [128, 2, TB, NH, VW])
    vcls = sb("vcls", [128, 2, NH, VW])
    scs = sb("scs", [128, 2, (2 * TB + 1) * NH])
    cmx = sb("cmx", [128, TB * NH])
    mc = sb("mc", [128, NH])
    pci = sb("pci", [128, TB + 1, NH])
    pc = sb("pc", [128, 2, TB + 1, VW])
    mxs = sb("mxs", [128, TB, NH])
    mf = sb("mf", [128, TB, NH])
    nmp = sb("nmp", [128, TB, MROWS * GH], BF16)
    nmr = sb("nmr", [128, TB, GH])
    dsc = sb("dsc", [128, TB, NH])
    pcls = sb("pcls", [128, 2, TB, NH])
    mt_sb = sb("mt_sb", [MROWS * GH, S], BF16)
    pt = sb("pt", [128, 2, GH, S])
    pvs = sb("pvs", [128, S])
    den = sb("den", [128, TB, GH])
    rinv = sb("rinv", [128, TB, GH])
    pr = sb("pr", [128, TB, NH])
    cadd = sb("cadd", [128, TB, GH, HD])
    o_sb = sb("o_sb", [128, 2, TB, D])
    pvd = sb("pvd", [128, NH * VW])
    rc = sb("rc", [NG, GH])
    oc = sb("oc", [NG, GH, HD])
    bnc = sb("bnc", [NG, 6])
    mvc = sb("mvc", [NG, 2])
    bn2 = sb("bn2", [128, 2, 6])
    mv2 = sb("mv2", [128, 2])
    e2 = sb("e2", [128, 1])
    e2c = sb("e2c", [NG, 1])
    st2 = sb("st2", [128, 2])
    st2c = sb("st2c", [NG, 2])
    ms2 = sb("ms2", [128, 2])
    msq2 = sb("msq2", [128, 2])
    rs2 = sb("rs2", [128, 1])
    am2 = sb("am2", [128, TB + 1])
    amc = sb("amc", [NG, 1])
    ax2 = sb("ax2", [128, TB + 1])
    rax2 = sb("rax2", [128, TB + 1])
    comb2 = sb("comb2", [128, TB + 1])
    aqo = sb("aqo", [128, TB + 1])
    qi2 = sb("qi2", [128, TB, D], BF16)
    qic = sb("qic", [NG, GH * HD], BF16)
    xq2 = sb("xq2", [128, DC, S], BF16)
    xqc = sb("xqc", [64, NG], BF16)
    h2c = sb("h2c", [1, D])
    row = sb("row", [128, TB])
    zero_row = sb("zero_row", [1, D])
    pads = pt[:, :, :, :].rearrange("p a g n -> p (a g n)").bitcast(I32)[:, 4 * DC * D:4 * DC * D + 2 * (list_rows // 128)] \
        .rearrange("p (r w) -> p r w", w=2)
    w_stage = pt[:, :, :, :].rearrange("p a g n -> p (a g n)")[:, 0:4 * DC * D]

    score = banks[0:2]
    scoret = banks[2:4]
    pv_bank = banks[4]
    d0, d1, d2 = banks[5:8]
    b16 = lambda bank: bank[:, :].bitcast(BF16)
    blk = lambda t: slice(t * 128, (t + 1) * 128)
    heads = lambda g: slice(g * GH, (g + 1) * GH)

    def steps(eng, body):
        def fixed(i):
            body(*[At(i + o, None, 0 <= i + o < images) for o in (2, 1, 0, -1, -2)])
        first = 3
        pairs = max(0, (images - 3 - first) // 2)
        for i in range(-2, first):
            fixed(i)
        if pairs:
            with eng.Fori(0, pairs) as n:
                for i in range(first, first + 2):
                    body(*[At(i + o, n) for o in (2, 1, 0, -1, -2)])
        for i in range(first + 2 * pairs, images + 2):
            fixed(i)

    def hold(eng, sem, per, b, n):
        wait(eng, sem, per, b, n)
        if b.n is not None:
            eng.sem_inc(s("held"), 1)

    def in_slot(g, P, C, W):
        st = (W, g + 2) if g < 2 else (C, g - 2)
        tg = (W, g + 1) if g < 3 else (C, 0)
        mt = (W, 3) if g == 0 else (C, g - 1)
        return st, tg, mt


    def sync_program(sp, stage):
        if stage == SETUP:
            sp.dma_start(cst[:, :], consts).then_inc(s("cst_in"), 16)
            sp.dma_start(w_stage.rearrange("p (w c n) -> p w c n", w=4, c=DC),
                         attn_w_t.rearrange("w (c p) n -> p w c n", p=128)).then_inc(s("attn_w_in"), 16)
            sp.dma_start(cls_row[:, :], cls).then_inc(s("cls_in"), 16)
            sp.dma_start(w0[:, :, :], w0_t.rearrange("(c p) n -> p c n", p=128)).then_inc(s("tok_w_in"), 16)
            sp.dma_start(w1[:, :, :], w1_t.rearrange("(c p) n -> p c n", p=128)).then_inc(s("tok_w_in"), 16)
            sp.dma_start(wo[:, :, :], wo_t.rearrange("(c p) n -> p c n", p=128)).then_inc(s("tok_w_in"), 16)
            sp.dma_start(gate_sb[:, :, :], gate_w.rearrange("(c p) n -> p c n", p=128)).then_inc(s("gate_in"), 16)

        def load_x(v, par):
            sp.dma_start(xt[:, par, :, :], x_t[bass.ds(v * D, D), :].rearrange("(c p) n -> p c n", p=128)) \
                .then_inc(s(f"x_in{par}"), 16)
        if stage == SETUP:
            sp.wait_ge(s("w_int"), 4)
            for g in range(NG):
                sp.dma_start(wo_cls[:, g, :], wq_int[64 * (g % 2):64 * (g % 2) + 64, 3, g // 2, :]) \
                    .then_inc(s("wo_cls_in"), 16)
            sp.wait_ge(s("pads_set"), 2)
            sp.dma_start(list_dram.rearrange("(p r) w -> p r w", p=128), pads).then_inc(s("list_init"), 16)
            sp.dma_start(x2_dram[tokens:tokens + 1, :], zero_row[:, :]).then_inc(s("list_init"), 16)

        def stack(b, g):
            hold(sp, s("pe_st"), UNITS * NG, b, UNITS * (g + 1) - UNITS * NG)
            hold(sp, s("parts_stored"), 16 * 4 * len(PARTS), b, 16 * 4 * len(PARTS))
            for a, (dst, runs) in enumerate(((qs, Q_STACK), (ks, K_STACK))):
                to = 0
                for part in runs:
                    lo, n = PARTS.index(part[0]) * HD, len(part) * HD
                    sp.dma_start(dst[to:to + n, heads(g), :],
                                 qk_dram[b.par, a, heads(g), lo:lo + n, :].rearrange("j r n -> r j n")) \
                        .then_inc(s(f"stacked{g}"), 16)
                    to += n

        def store_parts(b):
            for a in "qk":
                for n, part in enumerate(PARTS):
                    hold(sp, s(f"pool_{part}{a}" if part == "l" else f"act_{a}{part}"), 1, b, 1)
                    for f in range(DC):
                        sp.dma_start(qk_dram[b.par, "qk".index(a), f * NH // DC:(f + 1) * NH // DC, n * HD:(n + 1) * HD, :],
                                     parts[a + part][:, f, :]).then_inc(s("parts_stored"), 16)

        def maxima(b, g):
            hold(sp, s("act_mt"), NG, b, g + 1)
            sp.dma_start(qs[QK:QK + MROWS, heads(g), :], mt_sb[:, :]) \
                .then_inc(s(f"max_in{g}"), 16)

        def body(T, P, C, W, X):
            for g in range(NG):
                T, P, C, W, X = fresh(sp, g, T, P, C, W, X)
                st, tg, mt = in_slot(g, P, C, W)
                if mt[0].ok:
                    maxima(*mt)
                if g < 3 and C.ok:
                    stack(C, g + 1)
                if g == 0 and T.ok:
                    hold(sp, s("pe_up"), EC, T, 0)
                    if T.n is not None or T.v + 1 < images:
                        load_x(T.v + 1, 1 - T.par)
                if g == 1 and P.ok:
                    hold(sp, s("act_h"), 2, P, 2)
                    sp.dma_start(h_dram[bass.ds(P.v * S, S), :].rearrange("(t p) n -> p t n", p=128),
                                 h_sb[:, :, :]).then_inc(s("h_stored"), 16)
                if g == 2 and P.ok:
                    store_parts(P)
                if g == 2 and W.ok:
                    hold(sp, s("h_stored"), 16, W, 16)
                    hold(sp, s("h2_stored"), 16, W, 0)
                    hold(sp, s("act_x2"), TB, W, 0)
                    sp.dma_start(hw[:, :, :], h_dram[bass.ds(W.v * S, S), :].rearrange("(t p) n -> p t n", p=128)) \
                        .then_inc(s("hw_in"), 16)
                if g == 3 and P.ok:
                    stack(P, 0)
                if g == 3 and W.ok:
                    hold(sp, s("dve_h2c"), 1, W, 1)
                    sp.dma_start(out[bass.ds(W.v * SEQ, 1), :], h2c[:, :]).then_inc(s("h2c_stored"), 16)
                    hold(sp, s("dve_h2"), TB, W, TB)
                    sp.dma_start(out[bass.ds(W.v * SEQ + 1, S), :].rearrange("(t p) n -> p t n", p=128),
                                 hw[:, :, :]).then_inc(s("h2_stored"), 16)
                    hold(sp, s("act_x2"), TB, W, TB)
                    sp.dma_start(x2_dram[bass.ds(W.v * SEQ + 1, S), :].rearrange("(t p) n -> p t n", p=128),
                                 x2[:, :, :]).then_inc(s("x2_stored"), 16)
        if stage == STEPS:
            load_x(0, 0)
            steps(sp, body)
            sp.wait_ge(s("h2c_stored"), 16 * images)
            sp.wait_ge(s("h2_stored"), 16 * images)
            sp.wait_ge(s("x2_stored"), 16 * images)
            sp.wait_ge(s("h_stored"), 16 * images)
            sp.wait_ge(s("parts_stored"), 16 * 4 * len(PARTS) * images)
        if stage == CLASS_TOKENS:
            crow = out.rearrange("(b q) n -> b q n", q=SEQ)[:, 0, :]
            sp.dma_start(hw[0:images, 0, :], crow).then_inc(s("cls_back"), 16)
            sp.wait_ge(s("act_x2_c"), 1)
            sp.dma_start(x2_dram[0:tokens, :].rearrange("(b q) n -> b q n", q=SEQ)[:, 0, :], x2[0:images, 0, :]) \
                .then_inc(s("x2c_stored"), 16)
            sp.wait_ge(s("x2c_stored"), 16)


    def tensor_program(pe, stage):
        mm, tr = nc.tensor.matmul, nc.tensor.transpose
        if stage == SETUP:
            pe.wait_ge(s("ones_set"), 2)
            pe.wait_ge(s("w_sums"), 1)
            mm(d0[:, 0:4], ones[:, :], w_mean[:, :], start=True, stop=True).then_inc(s("pe_w_sum"), 1)
            pe.wait_ge(s("cls_norm"), 1)
            pe.wait_ge(s("cls_facts"), 1)
            mm(d1[:, 0:4], ones[0:1, :], cls_fact[:, :], start=True, stop=True)
            for c in range(DC):
                last = mm(d1[:, 4 + c:5 + c], cls_norm[:, blk(c)], ones[0:1, 0:1], start=True, stop=True)
            last.then_inc(s("pe_cls"), 1)
            pe.wait_ge(s("cls_used"), 2)
            pe.wait_ge(s("w_int"), 4)
            pe.wait_ge(s("wo_cls_in"), 16 * NG)
            pe.wait_ge(s("tok_w_in"), 48)
            pe.wait_ge(s("gate_in"), 16)
            pe.wait_ge(s("bf_set"), 3)
            pe.wait_ge(s("pool_set"), 6)

        def score_unit(b, g, u):
            j, t = u // TB, u % TB
            if u == 0:
                wait(pe, s(f"stacked{g}"), 16 * len(Q_STACK + K_STACK), b, 16 * len(Q_STACK + K_STACK))
            wait(pe, s("dve_mx"), UNITS * NG, b, UNITS * g + u - 1)
            h = g * GH + j
            mm(score[u % 2][:, :], qs[0:QK, h, blk(t)], ks[0:QK, h, :], start=True, stop=True) \
                .then_inc(s("pe_a"), 1)

        def scoret_unit(b, g, u):
            t, j = u // GH, u % GH
            if u == 0:
                wait(pe, s(f"max_in{g}"), 16, b, 16)
            wait(pe, s("act_exp"), UNITS * NG, b, UNITS * g + u - 1)
            h = g * GH + j
            mm(scoret[u % 2][:, :], ks[0:QK + MROWS, h, blk(t)], qs[0:QK + MROWS, h, :],
               start=True, stop=True).then_inc(s("pe_st"), 1)

        def pv(b, g, t):
            wait(pe, s("act_exp"), UNITS * NG, b, UNITS * g + GH * (t + 1))
            if t == 0:
                wait(pe, s("act_pvs"), NG, b, g)
                wait(pe, s("act_v"), TB, b, TB)
            for j in range(GH):
                last = mm(pv_bank[VW * j:VW * (j + 1), :], v_sb[:, b.par, t, g * GH + j, :],
                          pt[:, t % 2, j, :], start=(t == 0), stop=(t == TB - 1))
            last.then_inc(s("pe_pv"), 1)

        def body(T, P, C, W, X):
            for g in range(NG):
                for u in range(UNITS):
                    if u % 4 == 0:
                        T, P, C, W, X = fresh(pe, UNITS * g + u, T, P, C, W, X)
                        st, tg, mt = in_slot(g, P, C, W)
                    at = UNITS * g + u
                    if C.ok:
                        score_unit(C, g, u)
                    if st[0].ok:
                        scoret_unit(*st, u)
                    if u == 3 and tg[0].ok:
                        pv(*tg, TB - 1)
                    if u % 4 == 3 and u > 3 and st[0].ok:
                        pv(*st, u // 4 - 1)
                    if T.ok and at in GATE_AT:
                        e = GATE_AT.index(at)
                        if e == 0:
                            pe.wait_ge(s(f"x_in{T.par}"), T.half * 16 + 16)
                            if P.ok:
                                wait(pe, s("dve_fk"), DC, P, DC)
                        wait(pe, s("act_relu"), EC, T, e)
                        for c in range(DC):
                            last = mm(d0[:, :], w0[:, c, blk(e)], xt[:, T.par, c, :], start=(c == 0), stop=(c == DC - 1))
                        last.then_inc(s("pe_gate"), 1)
                    if T.ok and at in UP_AT:
                        e = UP_AT.index(at)
                        wait(pe, s("dve_hid"), EC, T, e)
                        for c in range(DC):
                            last = mm(d1[:, :], w1[:, c, blk(e)], xt[:, T.par, c, :], start=(c == 0), stop=(c == DC - 1))
                        last.then_inc(s("pe_up"), 1)
                    if P.ok and at in (0, 4):
                        k = at // 4
                        if k == 0:
                            wait(pe, s("dve_hid"), EC, P, EC)
                            if X.ok:
                                wait(pe, s("dve_h2"), TB, X, TB)
                        elif X.ok:
                            wait(pe, s("act_x2t"), DC, X, DC)
                        for t in (2 * k, 2 * k + 1):
                            for e in range(EC):
                                last = mm((d0, d1)[k][:, D * (t % 2):D * (t % 2 + 1)], hid[:, e, blk(t)], wo[:, e, :],
                                          start=(e == 0), stop=(e == EC - 1))
                        last.then_inc(s("pe_h"), 1)
                    if u == (2 if g < 3 else 3) and mt[0].ok:
                        b, gg = mt
                        wait(pe, s("dve_nm"), NG, b, gg + 1)
                        if g == 0:
                            if X.ok:
                                wait(pe, s("dve_h2c"), 1, X, 1)
                                wait(pe, s("dve_o"), NG, X, NG)
                            wait(pe, s("dve_o"), NG, W, 1)
                        if g == 1 and P.ok:
                            wait(pe, s("dve_ms"), 1, P, 1)
                        if g == 1 and X.ok:
                            wait(pe, s("dve_rk"), 1, X, 1)
                        if g == 1 and W.ok:
                            wait(pe, s("dve_o"), NG, W, 2)
                        if g == 2:
                            if P.ok:
                                wait(pe, s("dve_ms"), 1, P, 1)
                            if W.ok:
                                wait(pe, s("dve_o"), NG, W, 3)
                        if g == 3:
                            if P.ok:
                                wait(pe, s("dve_scs"), 1, P, 1)
                            if W.ok:
                                wait(pe, s("dve_ms2"), 1, W, 1)
                        for t in range(TB):
                            last = tr(b16(d2)[0:MROWS * GH, blk(t)], nmp[:, t, :], id_bf[:, :])
                        last.then_inc(s("pe_mt"), 1)
                    if at == 3 and X.ok:
                        wait(pe, s("act_x2"), TB, X, TB)
                        wait(pe, s("dve_h2"), TB, X, TB)
                        if P.ok:
                            wait(pe, s("act_h"), 2, P, 1)
                        for c in range(DC):
                            for t in range(TB):
                                last = tr((d0, d1)[c][:, blk(t)], x2[:, t, blk(c)], identf)
                            last.then_inc(s("pe_x2t"), 1)
                    if at == 5 and X.ok:
                        logits(X, TB, 128, "", [("act_mt", NG, W, NG)] if W.ok else [("dve_h2c", 1, X, 1)])
                    if u == 6 and tg[0].ok:
                        b, gg = tg
                        wait(pe, s("act_pvs"), NG, b, gg + 1)
                        if gg:
                            wait(pe, s("dve_o"), NG, b, gg)
                        if g == 0 and X.ok:
                            wait(pe, s("dve_lg"), 1, X, 1)
                        if g == 1 and X.ok:
                            wait(pe, s("dve_rk"), 1, X, 1)
                        if mt[0].ok:
                            wait(pe, s("act_mt"), NG, mt[0], mt[1] + 1)
                        if g == 3 and W.ok:
                            wait(pe, s("act_xqc"), 1, W, 1)
                        for t in range(TB):
                            last = tr(d2[:, blk(t)], pvs[:, blk(t)], identf)
                        last.then_inc(s("pe_tg"), 1)
                    if at == 16 and X.ok:
                        ranks(X, TB, 128, "", [("dve_ms", 1, P, 1)] if P.ok else [("dve_o", NG, W, 2)] if W.ok else [("dve_lg", 1, X, 1)])
                    if P.ok and at == 12:
                        wait(pe, s("act_xh"), TB, P, TB)
                        wait(pe, s("dve_sst"), 1, P, 1)
                        if W.ok:
                            wait(pe, s("dve_o"), NG, W, 2)
                        elif C.ok:
                            wait(pe, s("dve_scs"), 1, C, 1)
                        mm(d2[:, 0:2 * TB], ones[:, :], sums1[:, :, :].rearrange("p a t -> p (a t)"),
                           start=True, stop=True).then_inc(s("pe_st1"), 1)
                    if P.ok and at == 20:
                        wait(pe, s("pool_qi"), 1, P, 1)
                        wait(pe, s("act_h"), 2, P, 2)
                        for c in range(DC):
                            for t in range(TB):
                                last = tr(b16(d0)[:, c * S + t * 128:c * S + (t + 1) * 128], qi[:, t, blk(c)], id_bf[:, :])
                        last.then_inc(s("pe_xq"), 1)
                        wait(pe, s("dve_aq"), 1, P, 1)
                        for t in range(TB):
                            last = mm(d1[:, blk(t)], aq1[:, t:t + 1].broadcast_to([128, 128]), identf, start=True, stop=True)
                        last.then_inc(s("pe_aqb"), 1)
                    if P.ok and at == 22:
                        wait(pe, s("act_xq"), 1, P, 1)
                        wait(pe, s("act_aqb"), 1, P, 1)
                        project(P, 0, "pe_q")
                    if W.ok and at == 39:
                        wait(pe, s("dve_o"), NG, W, NG)
                        wait(pe, s("act_pc"), 1, W, 1)
                        for t in range(TB):
                            last = mm(d2[VW * t:VW * (t + 1), :], pc[:, W.par, t, :],
                                      v_sb[:, W.par, t, :, :].rearrange("p h w -> p (h w)"), start=True, stop=(t > 0))
                            if t == 0:
                                mm(d2[0:VW, :], pc[0:1, W.par, TB, :], vcls[0:1, W.par, :, :].rearrange("p h w -> p (h w)"),
                                   start=False, stop=True)
                        last.then_inc(s("pe_pvc"), 1)
                    if P.ok and at == 25:
                        wait(pe, s("dve_fq"), DC, P, DC)
                        project(P, 1, "pe_k")
                    if W.ok and at == 44:
                        wait(pe, s("dve_pvd"), 1, W, 1)
                        for k in range(NG):
                            last = mm(d2[0:NG, 0:GH * VW], cst[:, C_SEL + k * NG:C_SEL + (k + 1) * NG],
                                      pvd[:, k * GH * VW:(k + 1) * GH * VW], start=(k == 0), stop=(k == NG - 1))
                        last.then_inc(s("pe_tr"), 1)
                    if P.ok and at == 46:
                        for t in range(TB):
                            if T.ok:
                                wait(pe, s("dve_hid"), EC, T, EC)
                            else:
                                wait(pe, s("dve_fk"), DC, P, t // 2 + 1)
                            for c in range(DC):
                                last = mm((d0, d1)[t // 2][:, D * (t % 2):D * (t % 2 + 1)], xq[:, c, blk(t)],
                                          wq_int[:, 2, c, :], start=(c == 0), stop=(c == DC - 1))
                            last.then_inc(s("pe_v"), 1)
                    if P.ok and at == 45:
                        wait(pe, s("dve_qc"), 1, P, 1)
                        if W.ok:
                            wait(pe, s("dve_oc"), 1, W, 1)
                        elif C.ok:
                            wait(pe, s("act_mt"), NG, C, 2)
                        wait(pe, s("dve_ms"), 1, P, 1)
                        for c in range(DC):
                            mm(d2[:, 0:D], xq[:, c, S:SEQ].broadcast_to([128, 128]), wq_int[:, 2, c, :],
                               start=(c == 0), stop=(c == DC - 1))
                        for w in range(2):
                            for f in range(DC):
                                for c in range(DC):
                                    last = mm(d2[:, D + 2 * w + f:D + 2 * w + f + 1], wq_int[:, w, c, blk(f)],
                                              xq[:, c, S:SEQ], start=(c == 0), stop=(c == DC - 1))
                        last.then_inc(s("pe_cols"), 1)
                    if W.ok and at == 47:
                        wait(pe, s("dve_st2"), 1, W, 1)
                        if P.ok:
                            wait(pe, s("act_vc"), 1, P, 1)
                            wait(pe, s("dve_cc"), 2, P, 2)
                        mm(d2[:, 0:2], ones[:, :], st2[:, :], start=True, stop=False)
                        mm(d2[:, 0:2], ones[0:NG, :], st2c[:, :], start=False, stop=True).then_inc(s("pe_w1"), 1)
                    if P.ok and at == 48:
                        wait(pe, s("dve_bd"), 2, P, 2)
                        wait(pe, s("act_vc"), 1, P, 1)
                        if W.ok:
                            wait(pe, s("dve_ms2"), 1, W, 1)
                        for k, (a, o) in enumerate(((fq, kbd), (fk, qbd))):
                            for half in range(2):
                                for c in range(DC):
                                    last = mm(d2[VW * (2 * k + half):VW * (2 * k + half + 1), 0:S // 2], o[:, c, :],
                                              a[:, c, half * S // 2:(half + 1) * S // 2], start=(c == 0), stop=(c == DC - 1))
                        last.then_inc(s("pe_ct"), 1)
                    if P.ok and at == 49:
                        wait(pe, s("act_ct"), 1, P, 1)
                        for t in range(2):
                            tr(d2[:, blk(t)], sct[:, blk(t)], identf)
                        for c in range(DC):
                            last = mm(d2[:, S // 2:S // 2 + NH], fq[:, c, S:SEQ].broadcast_to([128, 128]),
                                      kbd[:, c, 0:NH], start=(c == 0), stop=(c == DC - 1))
                        last.then_inc(s("pe_t7"), 1)
                    if W.ok and at == 53:
                        wait(pe, s("pool_qi2"), 2, W, 2)
                        if P.ok:
                            wait(pe, s("act_v"), TB, P, TB)
                            wait(pe, s("dve_scs"), 1, P, 1)
                        if C.ok:
                            wait(pe, s("act_mt"), NG, C, 3)
                        for c in range(DC):
                            for t in range(TB):
                                last = tr(b16(d0)[:, c * S + t * 128:c * S + (t + 1) * 128], qi2[:, t, blk(c)], id_bf[:, :])
                        last.then_inc(s("pe_xq2"), 1)
                        tr(b16(d2)[0:64, 0:NG], qic[:, :], id_bf[0:NG, 0:NG]).then_inc(s("pe_xqc"), 1)
                    if W.ok and at == 57:
                        wait(pe, s("act_xq2"), 1, W, 1)
                        for t in range(TB):
                            for c in range(DC):
                                last = mm((d0, d1)[t // 2][:, D * (t % 2):D * (t % 2 + 1)], xq2[:, c, blk(t)],
                                          wq_int[:, 3, c, :], start=(c == 0), stop=(c == DC - 1))
                            last.then_inc(s("pe_y"), 1)
                        hold(pe, s("act_xqc"), 1, W, 1)
                        if C.ok:
                            hold(pe, s("dve_o"), NG, C, 1)
                        for k in range(NG):
                            last = mm(d2[0:1, 0:D], xqc[:, k:k + 1], wo_cls[:, k, :], start=(k == 0), stop=(k == NG - 1))
                        last.then_inc(s("pe_yc"), 1)

        def project(b, w, signal):
            for f in range(DC):
                for c in range(DC):
                    last = mm((d0, d1)[f][:, :], wq_int[:, w, c, blk(f)], xq[:, c, 0:S], start=(c == 0), stop=(c == DC - 1))
                last.then_inc(s(signal), 1)

        def logits(b, nt, np_, x, free):
            wait(pe, s("act_x2t" + x), DC, b, DC)
            for name, per, at_, n in free:
                wait(pe, s(name), per, at_, n)
            for t in range(nt):
                for c in range(DC):
                    last = mm(d2[0:np_, t * E:(t + 1) * E], x2_t[:, c, t * 128:t * 128 + np_], gate_sb[:, c, :],
                              start=(c == 0), stop=(c == DC - 1))
            last.then_inc(s("pe_lg" + x), 1)

        def ranks(b, nt, np_, x, free):
            wait(pe, s("dve_picked" + x), 1, b, 1)
            for name, per, at_, n in free:
                wait(pe, s(name), per, at_, n)
            a = picked[0:np_, :, :].rearrange("p t e -> p (t e)")
            mm(d2[0:np_, 0:nt * E], tri_bf[0:np_, 0:np_], a[:, 0:nt * E], start=True, stop=(nt == 1))
            for t in range(1, nt):
                mm(d2[0:np_, t * E:nt * E], ones_bf[0:np_, 0:np_], a[:, 0:(nt - t) * E], start=False, stop=(t == nt - 1))
            for t in range(nt):
                last = mm(d2[:, TB * E:(TB + 1) * E], ones_bf[0:np_, :], a[:, t * E:(t + 1) * E],
                          start=(t == 0), stop=(t == nt - 1))
            last.then_inc(s("pe_rk" + x), 1)

        if stage == STEPS:
            steps(pe, body)
        if stage == CLASS_TOKENS:
            one = At(0)
            pe.wait_ge(s("act_x2_c"), 1)
            for c in range(DC):
                tr((d0, d1)[c][:, 0:images], x2[0:images, 0, blk(c)], cst[0:images, C_ID:C_ID + images]) \
                    .then_inc(s("pe_x2t_c"), 1)
            logits(one, 1, images, "_c", [])
            ranks(one, 1, images, "_c", [("dve_lg_c", 1, one, 1)])


    def scalar_program(act, stage):
        f = nc.scalar.activation
        if stage == SETUP:
            act.wait_ge(s("cls_scale"), 1)
            f(cls_norm[:, :], cls_row[:, :], ACT.Identity, bias=cls_mv[:, 3:4], scale=cls_mv[:, 2:3],
              accum_out=cls_stat[:, 0:1]).then_inc(s("cls_norm"), 1)

        def exps(b, g, u):
            t, j = u // GH, u % GH
            wait(act, s("pe_st"), UNITS * NG, b, UNITS * g + u + 1)
            if j == 0:
                wait(act, s("pe_pv"), TB * NG, b, TB * g + t - 1)
            f(pt[:, t % 2, j, :], scoret[u % 2][:, :], ACT.Exp).then_inc(s("act_exp"), 1)

        def body(T, P, C, W, X):
            for g in range(NG):
                for u in range(UNITS):
                    if u % 4 == 0:
                        T, P, C, W, X = fresh(act, UNITS * g + u, T, P, C, W, X)
                        st, tg, mt = in_slot(g, P, C, W)
                    at = UNITS * g + u
                    if u == 4 and tg[0].ok:
                        b, gg = tg
                        wait(act, s("pe_pv"), TB * NG, b, TB * (gg + 1))
                        wait(act, s("pe_tg"), NG, b, gg)
                        f(pvs[:, :], pv_bank[:, :], ACT.Copy).then_inc(s("act_pvs"), 1)
                    if st[0].ok:
                        exps(*st, u)
                    if T.ok and at in GATE_AT:
                        e = GATE_AT.index(at)
                        wait(act, s("pe_gate"), EC, T, e + 1)
                        wait(act, s("dve_hid"), EC, T, e - 1)
                        f(relu[:, e % 2, :], d0[:, :], ACT.Relu).then_inc(s("act_relu"), 1)
                    if u == 1 and mt[0].ok:
                        b, gg = mt
                        wait(act, s("dve_dsc"), NG, b, gg + 1)
                        f(pcls[:, b.par, :, heads(gg)], dsc[:, :, heads(gg)], ACT.Exp).then_inc(s("act_pcls"), 1)
                    if u == (3 if g < 3 else 4) and mt[0].ok:
                        b, gg = mt
                        wait(act, s("pe_mt"), NG, b, gg + 1)
                        wait(act, s(f"max_in{(gg - 1) % NG}"), 16, b, 0 if gg == 0 else 16)
                        f(mt_sb[:, :], b16(d2)[0:MROWS * GH, 0:S], ACT.Copy).then_inc(s("act_mt"), 1)
                    if at == 3 and X.ok:
                        wait(act, s("pe_lg"), 1, X, 0)
                        for c in range(DC):
                            wait(act, s("pe_x2t"), DC, X, c + 1)
                            f(x2_t[:, c, :], (d0, d1)[c][:, :], ACT.Copy).then_inc(s("act_x2t"), 1)
                    if at == 12 and X.ok:
                        wait(act, s("dve_e"), 1, X, 1)
                        f(e21e[:, :], e21[:, :], ACT.Exp).then_inc(s("act_e"), 1)
                    if P.ok and at in (1, 5):
                        k = at // 4
                        wait(act, s("pe_h"), 2, P, k + 1)
                        wait(act, s("h_stored"), 16, P, 0)
                        wait(act, s("dve_sst"), 1, P, 0)
                        f(h_sb[:, 2 * k:2 * k + 2, :].rearrange("p t n -> p (t n)"), (d0, d1)[k][:, :], ACT.Copy) \
                            .then_inc(s("act_h"), 1)
                    if P.ok and at == 11:
                        wait(act, s("dve_nb1"), 1, P, 1)
                        wait(act, s("pool_qi"), 1, P, 0)
                        wait(act, s("pe_st1"), 1, P, 0)
                        for t in range(TB):
                            f(xn[:, t, :], h_sb[:, t, :], ACT.Identity, bias=nb1[:, t:t + 1], scale=rstd1[:, t:t + 1],
                              accum_out=sums1[:, 0, t:t + 1]).then_inc(s("act_xh"), 1)
                    if P.ok and at == 20:
                        wait(act, s("pe_xq"), 1, P, 1)
                        wait(act, s("pe_cols"), 1, P, 0)
                        f(xq[:, :, 0:S], b16(d0).rearrange("p (c n) -> p c n", c=DC), ACT.Copy).then_inc(s("act_xq"), 1)
                        wait(act, s("pe_aqb"), 1, P, 1)
                        wait(act, s("dve_fk"), DC, P, 0)
                        f(aqb[:, :], d1[:, :], ACT.Copy).then_inc(s("act_aqb"), 1)
                    if P.ok and at == 24:
                        wait(act, s("dve_fq"), DC, P, DC)
                        wait(act, s("parts_stored"), 16 * 4 * len(PARTS), P, 0)
                        f(parts["qh"][:, :, :], fq[:, :, 0:S], ACT.Copy).then_inc(s("act_qh"), 1)
                    if P.ok and at == 27:
                        wait(act, s("dve_fk"), DC, P, DC)
                        f(parts["kh"][:, :, :], fk[:, :, 0:S], ACT.Copy).then_inc(s("act_kh"), 1)
                        wait(act, s("pool_rq"), 1, P, 1)
                        f(parts["qm"][:, :, :], rest[:, :, :], ACT.Copy).then_inc(s("act_qm"), 1)
                    if P.ok and at == 47:
                        wait(act, s("dve_aqv"), 1, P, 1)
                        wait(act, s("pe_pv"), TB * NG, P, -TB * NG)
                        wait(act, s("pe_pvc"), 1, P, -1)
                        for t in range(TB):
                            wait(act, s("pe_v"), TB, P, t // 2 * 2 + 2)
                            f(v_sb[:, P.par, t, :, 1:1 + HD],
                              (d0, d1)[t // 2][:, D * (t % 2):D * (t % 2 + 1)].rearrange("p (h d) -> p h d", d=HD),
                              ACT.Copy, scale=aqv[:, t:t + 1]).then_inc(s("act_v"), 1)
                    if P.ok and at == 46:
                        wait(act, s("pe_cols"), 1, P, 1)
                        wait(act, s("dve_cc"), 2, P, 2)
                        wait(act, s("pool_add"), NG, P, -NG)
                        f(vcls[:, P.par, :, 1:1 + HD], d2[:, 0:D].rearrange("p (h d) -> p h d", d=HD),
                          ACT.Copy, scale=aqv[:, TB:TB + 1]).then_inc(s("act_vc"), 1)
                    if P.ok and at == 34:
                        wait(act, s("pool_rk"), 1, P, 1)
                        f(parts["km"][:, :, :], rest[:, :, :], ACT.Copy).then_inc(s("act_km"), 1)
                    if P.ok and at == 48:
                        wait(act, s("pe_ct"), 1, P, 1)
                        wait(act, s("pe_t7"), 1, P, 0)
                        f(sct[:, :], d2[:, 0:S // 2], ACT.Copy).then_inc(s("act_ct"), 1)
                    if P.ok and at == 54:
                        wait(act, s("dve_pci"), 1, P, 1)
                        wait(act, s("pe_pvc"), 1, P, -1)
                        f(pc[:, P.par, :, 0:NH], pci[:, :, :], ACT.Exp).then_inc(s("act_pc"), 1)
                    if W.ok and at == 53:
                        wait(act, s("pe_xq2"), 1, W, 1)
                        wait(act, s("pe_y"), TB, W, 0)
                        f(xq2[:, :, :], b16(d0).rearrange("p (c n) -> p c n", c=DC), ACT.Copy).then_inc(s("act_xq2"), 1)
                        wait(act, s("pe_xqc"), 1, W, 1)
                        wait(act, s("pe_yc"), 1, W, 0)
                        f(xqc[:, :], b16(d2)[0:64, 0:NG], ACT.Copy).then_inc(s("act_xqc"), 1)
                    if W.ok and at == 63:
                        wait(act, s("dve_nb3"), 1, W, 1)
                        wait(act, s("pe_x2t"), DC, W, 0)
                        wait(act, s("x2_stored"), 16, W, 0)
                        for t in range(TB):
                            f(x2[:, t, :], hw[:, t, :], ACT.Identity, bias=nb3[:, t:t + 1], scale=rstd3[:, t:t + 1]) \
                                .then_inc(s("act_x2"), 1)
        if stage == STEPS:
            steps(act, body)
        if stage == CLASS_TOKENS:
            act.wait_ge(s("dve_nb3_c"), 1)
            f(x2[0:images, 0, :], hw[0:images, 0, :], ACT.Identity, bias=nb3[0:images, 0:1], scale=rstd3[0:images, 0:1]) \
                .then_inc(s("act_x2_c"), 1)
            for c in range(DC):
                act.wait_ge(s("pe_x2t_c"), c + 1)
                f(x2_t[:, c, 0:images], (d0, d1)[c][:, 0:images], ACT.Copy).then_inc(s("act_x2t_c"), 1)
            act.wait_ge(s("dve_e_c"), 1)
            f(e21e[0:images, 0:1], e21[0:images, 0:1], ACT.Exp).then_inc(s("act_e_c"), 1)


    def gpsimd_program(pool, stage):
        g_ = nc.gpsimd

        def rsqrt(out_, in_, n, np_, ready, done, b):
            hold(pool, s(ready), 1, b, 1)
            g_.tensor_tensor(out_, in_, neg_half[0:np_, 0:n], ALU.pow).then_inc(s(done), 1)

        one = At(0)
        if stage == SETUP:
            for n, (place, value) in enumerate(((neg_half[:, :], -0.5), (ks[QK:128, :, :], 1.0), (v_sb[:, :, :, :, :], 0.0),
                                                (vcls[:, :, :, :], 0.0), (v_sb[:, :, :, :, 0:1], 1.0), (vcls[:, :, :, 0:1], 1.0))):
                g_.memset(place, value).then_inc(s("pool_set"), 1)
                pool.wait_ge(s("pool_set"), n + 1)
            rsqrt(cls_mv[:, 2:3], cls_mv[:, 2:3], 1, 1, "cls_var", "cls_rstd", one)

        def scatter(b, nt, np_, x):
            hold(pool, s("dve_pay" + x), 1, b, 1)
            for k in range(2):
                for t in range(nt):
                    g_.indirect_dma_start(out=list_dram, out_offset=bass.IndirectOffsetOnAxis(
                        ap=slot_i[0:np_, k, t:t + 1], axis=0), in_=pay[0:np_, k, t, :], in_offset=None) \
                        .then_inc(s("scattered"), 16)

        def body(T, P, C, W, X):
            for g in range(NG):
                for u in range(UNITS):
                    if u % 4 == 0:
                        T, P, C, W, X = fresh(pool, UNITS * g + u, T, P, C, W, X)
                        st, tg, mt = in_slot(g, P, C, W)
                    at = UNITS * g + u
                    if u == 7 and tg[0].ok:
                        b, gg = tg
                        hold(pool, s("dve_pr"), NG, b, gg + 1)
                        hold(pool, s("act_vc"), 1, b, 1)
                        hold(pool, s("pool_add"), NG, b, gg)
                        g_.tensor_tensor(cadd[:, :, :, :], bcast(vcls[:, b.par, heads(gg), 1:1 + HD], 1, TB),
                                         bcast(pr[:, :, heads(gg)], 3, HD), ALU.mult).then_inc(s("pool_mul"), 1)
                        hold(pool, s("pool_mul"), NG, b, gg + 1)
                        o = o_sb[:, b.par, :, :].rearrange("p t (h d) -> p t h d", d=HD)[:, :, heads(gg), :]
                        g_.tensor_tensor(o, o, cadd[:, :, :, :], ALU.add).then_inc(s("pool_add"), 1)
                    if X.ok and at == 34:
                        scatter(X, TB, 128, "")
                    if P.ok and at == 8:
                        rsqrt(rstd1[:, :], ve1[:, :], TB, 128, "dve_ve1", "pool_r1", P)
                    if P.ok and at == 13:
                        rsqrt(rs1[:, :], msq1[:, 1:2], 1, 128, "dve_ve", "pool_rs", P)
                    if P.ok and at == 19:
                        hold(pool, s("dve_q1"), TB, P, TB)
                        hold(pool, s("pe_xq"), 1, P, 0)
                        g_.tensor_scalar(qi[:, :, :], xn[:, :, :], -MAGIC, 1.0, ALU.add, ALU.mult).then_inc(s("pool_qi"), 1)
                    if P.ok and at == 26:
                        hold(pool, s("act_qh"), 1, P, 1)
                        g_.tensor_tensor(rest[:, :, :], fq[:, :, 0:S], parts["qh"][:, :, :], ALU.subtract) \
                            .then_inc(s("pool_rq"), 1)
                    if P.ok and at == 28:
                        hold(pool, s("act_qm"), 1, P, 1)
                        g_.tensor_tensor(parts["ql"][:, :, :], rest[:, :, :], parts["qm"][:, :, :], ALU.subtract) \
                            .then_inc(s("pool_lq"), 1)
                        hold(pool, s("act_kh"), 1, P, 1)
                        hold(pool, s("pool_lq"), 1, P, 1)
                        g_.tensor_tensor(rest[:, :, :], fk[:, :, 0:S], parts["kh"][:, :, :], ALU.subtract) \
                            .then_inc(s("pool_rk"), 1)
                    if W.ok and at == 46:
                        rsqrt(rs2[:, :], msq2[:, 1:2], 1, 128, "dve_ve2", "pool_rs2", W)
                        hold(pool, s("dve_amc"), 1, W, 1)
                        g_.partition_all_reduce(am2[0:NG, TB:TB + 1], amc[:, :], NG, bass.bass_isa.ReduceOp.absmax) \
                            .then_inc(s("pool_amc"), 1)
                    if P.ok and at == 32:
                        hold(pool, s("act_km"), 1, P, 1)
                        g_.tensor_tensor(parts["kl"][:, :, :], rest[:, :, :], parts["km"][:, :, :], ALU.subtract) \
                            .then_inc(s("pool_lk"), 1)
                    if P.ok and at == 50:
                        hold(pool, s("dve_scs"), 1, P, 1)
                        g_.partition_all_reduce(cmx[:, :], scs[:, P.par, TB * NH:2 * TB * NH], 128,
                                                bass.bass_isa.ReduceOp.max).then_inc(s("pool_par"), 1)
                    if W.ok and at == 52:
                        hold(pool, s("dve_q2"), TB + 1, W, TB + 1)
                        hold(pool, s("pe_xqc"), 1, W, 0)
                        g_.tensor_scalar(qi2[:, :, :], o_sb[:, W.par, :, :], -MAGIC, 1.0, ALU.add, ALU.mult) \
                            .then_inc(s("pool_qi2"), 1)
                        g_.tensor_scalar(qic[:, :], oc[:, :, :].rearrange("p j d -> p (j d)"), -MAGIC, 1.0,
                                         ALU.add, ALU.mult).then_inc(s("pool_qi2"), 1)
                    if W.ok and at == 61:
                        rsqrt(rstd3[:, :], ve3[:, :], TB, 128, "dve_ve3", "pool_r3", W)
        if stage == SETUP:
            pool.wait_ge(s("list_init"), 32)
        if stage == STEPS:
            steps(pool, body)
            pool.wait_ge(s("scattered"), 16 * 2 * TB * images)
        if stage == CLASS_TOKENS:
            rsqrt(rstd3[0:images, 0:1], ve3[0:images, 0:1], 1, images, "dve_ve3_c", "pool_r3_c", one)
            scatter(one, 1, images, "_c")
            pool.wait_ge(s("scattered"), 16 * 2)


    def vector_program(dve, stage):
        v = nc.vector

        class Link:

            def __init__(self, name, per, b, start=0):
                self.sem, self.per, self.b, self.n = s(name), per, b, start

            def go(self, ins):
                ins.then_inc(self.sem, 1)
                self.n += 1

            def __call__(self, ins):
                self.go(ins)
                self.wait()

            def wait(self):
                wait(dve, self.sem, self.per, self.b, self.n)

            def hold(self):
                hold(dve, self.sem, self.per, self.b, self.n)

            def end(self, n):
                assert self.n == n, (self.sem, self.n, n)

        def signal(ins, name, per, b, n):
            ins.then_inc(s(name), 1)
            wait(dve, s(name), per, b, n)

        one = At(0)
        if stage == SETUP:
            v.memset(ones[:, :], 1.0).then_inc(s("ones_set"), 1)
            v.memset(am2[:, :], 1.0).then_inc(s("ones_set"), 1)
            v.memset(ones_bf[:, :], 1.0).then_inc(s("bf_set"), 1)
            v.memset(pads[:, :, 0:1], tokens).then_inc(s("pads_set"), 1)
            v.memset(pads[:, :, 1:2], 0).then_inc(s("pads_set"), 1)
            v.memset(zero_row[:, :], 0.0).then_inc(s("pads_set"), 1)
            dve.wait_ge(s("cst_in"), 16)
            v.tensor_copy(id_bf[:, :], identf).then_inc(s("bf_set"), 1)
            v.tensor_copy(tri_bf[:, :], cst[:, C_TRI:C_TRI + 128]).then_inc(s("bf_set"), 1)
            v.tensor_copy(run[:, :], cst[:, C_BASE:C_BASE + E]).then_inc(s("dve_init"), 1)
            v.memset(pc[:, :, :, :], 0.0).then_inc(s("dve_init"), 1)
            v.tensor_copy(row[:, :], cst[:, C_ROW:C_ROW + TB]).then_inc(s("dve_init"), 1)
            dve.wait_ge(s("cls_in"), 16)
            init = Link("dve_chain0", 0, one)
            init(v.bn_stats(cls_stat[:, :], cls_row[:, :]))
            init(v.bn_aggr(cls_mv[:, 0:2], cls_stat[:, :]))
            v.tensor_scalar(cls_mv[:, 2:3], cls_mv[:, 1:2], EPS, None, ALU.add).then_inc(s("cls_var"), 1)
            dve.wait_ge(s("attn_w_in"), 16)
            v.tensor_reduce(out=w_mean[:, :], in_=w_stage.rearrange("p (w n) -> p w n", w=4), axis=AX.X, op=ALU.add,
                            apply_absolute_value=True).then_inc(s("w_sums"), 1)
            dve.wait_ge(s("cls_rstd"), 1)
            v.scalar_tensor_tensor(cls_mv[:, 3:4], cls_mv[:, 0:1], -1.0, cls_mv[:, 2:3], ALU.mult, ALU.mult) \
                .then_inc(s("cls_scale"), 1)
            dve.wait_ge(s("pe_w_sum"), 1)
            init(v.tensor_scalar(w_mean[:, :], d0[:, 0:4], 1.0 / (D * D), 1e-5, ALU.mult, ALU.max))
            init(v.reciprocal(w_scale[:, :], w_mean[:, :]))
            init(v.tensor_copy(w_fac[:, 1:4], w_mean[:, 1:4]))
            init(v.tensor_scalar(w_fac[:, 0:1], w_mean[:, 0:1], float(HD) ** -0.5, None, ALU.mult))
            for w in range(4):
                part = w_stage[:, w * DC * D:(w + 1) * DC * D]
                init(v.tensor_scalar(part, part, w_scale[:, w:w + 1], MAGIC, ALU.mult, ALU.add))
                init(v.tensor_scalar(part, part, -MAGIC, 1.0, ALU.add, ALU.min))
                v.tensor_scalar(wq_int[:, w, :, :].rearrange("p c n -> p (c n)"), part, -1.0, None, ALU.max) \
                    .then_inc(s("w_int"), 1)
            dve.wait_ge(s("cls_norm"), 1)
            init(v.tensor_tensor(cls_fact[:, 1:2], cls_mv[:, 1:2], cls_mv[:, 2:3], ALU.mult))
            init(v.scalar_tensor_tensor(cls_fact[:, 1:2], cls_fact[:, 1:2], D / total, cls_mv[:, 2:3], ALU.mult, ALU.mult))
            init(v.tensor_scalar(cls_fact[:, 0:1], cls_stat[:, 0:1], 1.0 / total, None, ALU.mult))
            init(v.tensor_reduce(out=cls_fact[:, 2:3], in_=cls_norm[:, :], axis=AX.X, op=ALU.max))
            v.tensor_reduce(out=cls_fact[:, 3:4], in_=cls_norm[:, :], axis=AX.X, op=ALU.min).then_inc(s("cls_facts"), 1)
            dve.wait_ge(s("pe_cls"), 1)
            v.tensor_copy(cls_f[:, :], d1[:, 0:4]).then_inc(s("cls_used"), 1)
            v.tensor_copy(cls_t[:, :], d1[:, 4:4 + DC]).then_inc(s("cls_used"), 1)
            dve.wait_ge(s("cls_used"), 2)
            dve.wait_ge(s("ones_set"), 2)
            dve.wait_ge(s("dve_init"), 3)

        def head_max(b, g, u):
            j, t = u // TB, u % TB
            wait(dve, s("pe_a"), UNITS * NG, b, UNITS * g + u + 1)
            v.reduce_max(mxs[:, t, g * GH + j:g * GH + j + 1], score[u % 2][:, :], AX.X).then_inc(s("dve_mx"), 1)

        def negate_maxima(b, g):
            wait(dve, s("dve_mx"), UNITS * NG, b, UNITS * (g + 1))
            ch = Link("dve_chain_m", NG * 4, b, 4 * g)
            hs = heads(g)
            scl = scs[:, b.par, 0:TB * NH].rearrange("p (t h) -> p t h", t=TB)[:, :, hs]
            ch(v.tensor_tensor(mf[:, :, hs], mxs[:, :, hs], scl, ALU.max))
            wait(dve, s("pe_mt"), NG, b, g)
            n = lambda k: nmp[:, :, k * GH:(k + 1) * GH]
            ch(v.tensor_scalar(n(0), mf[:, :, hs], -1.0, None, ALU.mult))
            ch(v.scalar_tensor_tensor(nmr[:, :, :], mf[:, :, hs], -1.0, n(0), ALU.mult, ALU.subtract))
            ch(v.tensor_copy(n(1), nmr[:, :, :]))
            v.tensor_tensor(n(2), nmr[:, :, :], n(1), ALU.subtract).then_inc(s("dve_nm"), 1)
            wait(dve, s("act_pcls"), NG, b, g + 1 - NG)
            v.tensor_tensor(dsc[:, :, hs], scl, mf[:, :, hs], ALU.subtract).then_inc(s("dve_dsc"), 1)
            ch.end(4 * (g + 1))

        def normalise(b, g):
            wait(dve, s("pe_tg"), NG, b, g + 1)
            wait(dve, s("act_pcls"), NG, b, g + 1)
            wait(dve, s("pool_add"), NG, b, g + 1 - NG)
            wait(dve, s("pool_qi2"), 2, b, -2)
            ch = Link("dve_chain_g", NG * 2, b, 2 * g)
            got = d2[:, :].rearrange("p (t j w) -> p t j w", t=TB, w=VW)
            pk = pcls[:, b.par, :, heads(g)]
            ch(v.tensor_tensor(den[:, :, :], got[:, :, :, 0], pk, ALU.add))
            ch(v.reciprocal(rinv[:, :, :], den[:, :, :]))
            o = o_sb[:, b.par, :, :].rearrange("p t (h d) -> p t h d", d=HD)[:, :, heads(g), :]
            v.tensor_tensor(o, got[:, :, :, 1:1 + HD], bcast(rinv[:, :, :], 3, HD), ALU.mult).then_inc(s("dve_o"), 1)
            v.tensor_tensor(pr[:, :, heads(g)], pk, rinv[:, :, :], ALU.mult).then_inc(s("dve_pr"), 1)
            ch.end(2 * (g + 1))

        def scales(ch, am, ax, rax, comb, aq, rs):
            ch(v.tensor_scalar(ax[:, :], am[:, :], rs[:, :], 1e-5, ALU.mult, ALU.max))
            ch(v.reciprocal(rax[:, :], ax[:, :]))
            ch(v.tensor_scalar(comb[:, :], rax[:, :], 127.0, rs[:, :], ALU.mult, ALU.mult))

        def token_stats(b, tiles_, np_, src, bn, chain, n):
            ch = Link(chain, 2 * n, b, tiles_[0])
            for t in tiles_:
                ch.go(v.bn_stats(bn[0:np_, t, :], src[0:np_, t, :]))

        def token_moments(b, np_, bn, mv, ve, chain, n, done):
            ch = Link(chain, 2 * n, b, n)
            ch.hold()
            for t in range(n):
                ch.go(v.bn_aggr(mv[0:np_, t, :], bn[0:np_, t, :]))
            ch.wait()
            ch.end(2 * n)
            v.tensor_scalar(ve[0:np_, 0:n], mv[0:np_, 0:n, 1], EPS, None, ALU.add).then_inc(s(done), 1)

        def router(b, x, nt, np_, pieces=(0, 1, 2, 3)):
            P = slice(0, np_)
            js, jps = (bcast(cst[P, k:k + E], 1, nt) for k in (C_J, C_JP))
            m, tmp = (m1, m2), rtmp[P, 0:nt, :]
            for piece in pieces:
                k = piece // 2
                ch = Link("dve_chain_r" + x, 10, b, (0, 2, 5, 7)[piece])
                if piece == 0:
                    wait(dve, s("pe_lg" + x), 1, b, 1)
                    signal(v.tensor_copy(lg[P, 0:nt, :], d2[P, 0:nt * E].rearrange("p (t e) -> p t e", e=E)),
                           "dve_lg" + x, 1, b, 1)
                if piece == 2:
                    signal(v.scalar_tensor_tensor(lg[P, 0:nt, :], oh[P, 0, 0:nt, :], -3e38, lg[P, 0:nt, :],
                                                  ALU.mult, ALU.add), "dve_masked" + x, 1, b, 1)
                if piece in (0, 2):
                    ch(v.tensor_reduce(out=m[k][P, 0:nt], in_=lg[P, 0:nt, :], axis=AX.X, op=ALU.max))
                    if k == 1:
                        wait(dve, s("act_e" + x), 1, b, 0)
                        v.tensor_tensor(e21[P, 0:nt], m2[P, 0:nt], m1[P, 0:nt], ALU.subtract).then_inc(s("dve_e" + x), 1)
                    ch(v.tensor_tensor(tmp, lg[P, 0:nt, :], bcast(m[k][P, 0:nt], 2, E), ALU.is_equal))
                else:
                    ch(v.scalar_tensor_tensor(tmp, tmp, -float(E), jps, ALU.mult, ALU.add))
                    ch(v.tensor_reduce(out=ix[P, 0:nt], in_=tmp, axis=AX.X, op=ALU.min))
                    ch(v.tensor_tensor(oh[P, k, 0:nt, :], js, bcast(ix[P, 0:nt], 2, E), ALU.is_equal))
                if piece == 3:
                    wait(dve, s("pe_rk" + x), 1, b, 0)
                    v.tensor_tensor(picked[P, 0:nt, :], oh[P, 0, 0:nt, :], oh[P, 1, 0:nt, :], ALU.add) \
                        .then_inc(s("dve_picked" + x), 1)
                    ch.end(10)

        def weights(b, x, nt, np_):
            P = slice(0, np_)
            ch = Link("dve_chain_u" + x, 3, b)
            wait(dve, s("act_e" + x), 1, b, 1)
            ch(v.tensor_scalar(wts[P, 0, 0:nt], e21e[P, 0:nt], 1.0, None, ALU.add))
            ch(v.reciprocal(wts[P, 0, 0:nt], wts[P, 0, 0:nt]))
            ch(v.tensor_tensor(wts[P, 1, 0:nt], e21e[P, 0:nt], wts[P, 0, 0:nt], ALU.mult))

        def payload(b, x, nt, np_, rows):
            P = slice(0, np_)
            ch = Link("dve_chain_s" + x, 3, b)
            wait(dve, s("pe_rk" + x), 1, b, 1)
            ch(v.tensor_tensor(pos[P, 0:nt, :], d2[P, 0:nt * E].rearrange("p (t e) -> p t e", e=E),
                               bcast(run[P, :], 1, nt), ALU.add))
            signal(v.tensor_tensor(run[:, :], run[:, :], d2[:, TB * E:(TB + 1) * E], ALU.add), "dve_rk" + x, 1, b, 1)
            ch(v.tensor_tensor(oh[P, :, 0:nt, :], oh[P, :, 0:nt, :], bcast(pos[P, 0:nt, :], 1, 2), ALU.mult))
            ch(v.tensor_reduce(out=slot[P, :, 0:nt], in_=oh[P, :, 0:nt, :], axis=AX.X, op=ALU.add))
            wait(dve, s("scattered"), 16 * 2 * TB, b, 0)
            signal(v.tensor_copy(slot_i[P, :, 0:nt], slot[P, :, 0:nt]), "dve_sl" + x, 1, b, 1)
            signal(v.tensor_copy(pay[P, :, 0:nt, 0], bcast(rows, 1, 2)), "dve_row" + x, 1, b, 1)
            v.tensor_copy(pay[P, :, 0:nt, 1].bitcast(F32), wts[P, :, 0:nt]).then_inc(s("dve_pay" + x), 1)
            ch.end(3)

        def body(T, P, C, W, X):
            for g in range(NG):
                for u in range(UNITS):
                    if u % 4 == 0:
                        T, P, C, W, X = fresh(dve, UNITS * g + u, T, P, C, W, X)
                        st, tg, mt = in_slot(g, P, C, W)
                    at = UNITS * g + u
                    if C.ok:
                        head_max(C, g, u)
                    if u == 7 and tg[0].ok:
                        normalise(*tg)
                    if T.ok and at in HIDDEN_AT:
                        e = HIDDEN_AT.index(at)
                        wait(dve, s("pe_up"), EC, T, e + 1)
                        wait(dve, s("act_relu"), EC, T, e + 1)
                        if e == 0:
                            wait(dve, s("pe_h"), 2, T, 0)
                        v.tensor_tensor(hid[:, e, :], d1[:, :], relu[:, e % 2, :], ALU.mult).then_inc(s("dve_hid"), 1)
                    if X.ok and at in ROUTER_AT:
                        router(X, "", TB, 128, pieces=(ROUTER_AT.index(at),))
                    if at == 12 and X.ok:
                        weights(X, "", TB, 128)
                    if at == 17 and X.ok:
                        payload(X, "", TB, 128, row[:, :])
                        wait(dve, s("dve_pay"), 1, X, 1)
                        signal(v.tensor_scalar(row[:, :], row[:, :], float(SEQ), None, ALU.add), "dve_rows", 1, X, 1)
                    if P.ok and at in STATS_AT:
                        k = STATS_AT.index(at)
                        wait(dve, s("act_h"), 2, P, k + 1)
                        token_stats(P, (2 * k, 2 * k + 1), 128, h_sb, bn1, "dve_chain_n1", TB)
                    if P.ok and at == 8:
                        token_moments(P, 128, bn1, mv1, ve1, "dve_chain_n1", TB, "dve_ve1")
                    if P.ok and at == 10:
                        wait(dve, s("pool_r1"), 1, P, 1)
                        v.scalar_tensor_tensor(nb1[:, :], mv1[:, :, 0], -1.0, rstd1[:, :], ALU.mult, ALU.mult) \
                            .then_inc(s("dve_nb1"), 1)
                        signal(v.tensor_tensor(vr1[:, :], mv1[:, :, 1], rstd1[:, :], ALU.mult), "dve_vr1", 1, P, 1)
                        wait(dve, s("pe_st1"), 1, P, 0)
                        v.scalar_tensor_tensor(sums1[:, 1, :], vr1[:, :], float(D), rstd1[:, :], ALU.mult, ALU.mult) \
                            .then_inc(s("dve_sst"), 1)
                    if P.ok and at == 13:
                        wait(dve, s("pe_st1"), 1, P, 1)
                        signal(v.tensor_reduce(out=red1[:, :], in_=d2[:, 0:2 * TB].rearrange("p (a t) -> p a t", a=2),
                                               axis=AX.X, op=ALU.add), "dve_ms", 1, P, 1)
                        ch = Link("dve_chain_p", 7, P)
                        ch(v.scalar_tensor_tensor(ms1[:, :], red1[:, :], 1.0 / total, cls_f[:, 0:2], ALU.mult, ALU.add))
                        ch(v.tensor_tensor(msq1[:, 0:1], ms1[:, 0:1], ms1[:, 0:1], ALU.mult))
                        v.scalar_tensor_tensor(msq1[:, 1:2], ms1[:, 1:2], EPS, msq1[:, 0:1], ALU.add, ALU.subtract) \
                            .then_inc(s("dve_ve"), 1)
                        ch(v.tensor_tensor(am1b[:, :], cls_f[:, 2:3], ms1[:, 0:1], ALU.subtract))
                        ch(v.scalar_tensor_tensor(am1[:, TB:TB + 1], ms1[:, 0:1], cls_f[:, 3:4], am1b[:, :],
                                                  ALU.subtract, ALU.max))
                        wait(dve, s("act_xh"), TB, P, TB)
                        v.tensor_scalar(xn[:, :, :], xn[:, :, :], ms1[:, 0:1], None, ALU.subtract).then_inc(s("dve_xm"), 1)
                    if P.ok and at == 15:
                        wait(dve, s("dve_xm"), 1, P, 1)
                        signal(v.tensor_reduce(out=am1[:, 0:TB], in_=xn[:, :, :], axis=AX.X, op=ALU.max,
                                               apply_absolute_value=True), "dve_am", 1, P, 1)
                    if P.ok and at == 17:
                        wait(dve, s("pool_rs"), 1, P, 1)
                        ch = Link("dve_chain_p", 7, P, 4)
                        scales(ch, am1, ax1, rax1, comb1, aq1, rs1)
                        ch.end(7)
                    if P.ok and at == 18:
                        for t in range(TB):
                            v.tensor_scalar(xn[:, t, :], xn[:, t, :], comb1[:, t:t + 1], MAGIC, ALU.mult, ALU.add) \
                                .then_inc(s("dve_q1"), 1)
                        wait(dve, s("pe_aqb"), 1, P, 0)
                        signal(v.tensor_scalar(aq1[:, :], ax1[:, :], 1.0 / 127.0, None, ALU.mult), "dve_aq", 1, P, 1)
                    if P.ok and at == 19:
                        wait(dve, s("act_vc"), 1, P, 0)
                        v.tensor_scalar(aqv[:, :], aq1[:, :], w_fac[:, 2:3], None, ALU.mult).then_inc(s("dve_aqv"), 1)
                        ch = Link("dve_chain_c", 2, P)
                        ch(v.tensor_scalar(cls_q[:, :], cls_t[:, :], ms1[:, 0:1], None, ALU.subtract))
                        ch(v.tensor_scalar(cls_q[:, :], cls_q[:, :], comb1[:, TB:TB + 1], MAGIC, ALU.mult, ALU.add))
                        wait(dve, s("pe_cols"), 1, P, 0)
                        v.tensor_scalar(xq[:, :, S:SEQ].rearrange("p c o -> p (c o)"), cls_q[:, :], -MAGIC, None, ALU.add) \
                            .then_inc(s("dve_qc"), 1)
                    if P.ok and at in QK_AT:
                        k, fc = divmod(QK_AT.index(at), DC)
                        a, dst = "qk"[k], (fq, fk)[k]
                        if fc == 0:
                            wait(dve, s(f"act_{a}h"), 1, P, 0)
                            wait(dve, s(f"pool_r{a}"), 1, P, 0)
                            wait(dve, s("pe_t7"), 1, P, 0)
                            wait(dve, s("act_aqb"), 1, P, 1)
                        wait(dve, s(f"pe_{a}"), DC, P, fc + 1)
                        v.scalar_tensor_tensor(dst[:, fc, 0:S], (d0, d1)[fc][:, :], w_fac[:, k:k + 1],
                                               aqb[:, :], ALU.mult, ALU.mult).then_inc(s(f"dve_f{a}"), 1)
                    if W.ok and at == 40:
                        wait(dve, s("pe_pvc"), 1, W, 1)
                        wait(dve, s("pe_tr"), 1, W, 0)
                        v.tensor_tensor(pvd[:, :], d2[:, :], diagonal, ALU.mult).then_inc(s("dve_pvd"), 1)
                    if W.ok and at == 44:
                        wait(dve, s("pe_tr"), 1, W, 1)
                        ch = Link("dve_chain_w", 11, W)
                        got = d2[0:NG, 0:128].rearrange("p (j w) -> p j w", w=VW)
                        ch(v.reciprocal(rc[:, :], got[:, :, 0]))
                        wait(dve, s("pool_qi2"), 2, W, 0)
                        signal(v.tensor_tensor(oc[:, :, :], got[:, :, 1:1 + HD], bcast(rc[:, :], 2, HD), ALU.mult),
                               "dve_oc", 1, W, 1)
                        ch.go(v.bn_stats(bnc[:, :], oc[:, :, :].rearrange("p j d -> p (j d)")))
                    if W.ok and at == 44:
                        ch = Link("dve_chain_w", 11, W, 2)
                        wait(dve, s("pool_add"), NG, W, NG)
                        flat = o_sb[:, W.par, :, :].rearrange("p t n -> p (t n)")
                        for k in range(2):
                            ch.go(v.bn_stats(bn2[:, k, :], flat[:, k * 512:(k + 1) * 512]))
                    if W.ok and at == 45:
                        ch = Link("dve_chain_w", 11, W, 4)
                        ch.hold()
                        ch.go(v.bn_aggr(mvc[:, :], bnc[:, :]))
                        ch(v.bn_aggr(mv2[:, :], bn2[:, :, :].rearrange("p k n -> p (k n)")))
                        ch.go(v.scalar_tensor_tensor(e2[:, :], mv2[:, 0:1], mv2[:, 0:1], mv2[:, 1:2], ALU.mult, ALU.add))
                        ch(v.scalar_tensor_tensor(e2c[:, :], mvc[:, 0:1], mvc[:, 0:1], mvc[:, 1:2], ALU.mult, ALU.add))
                        wait(dve, s("pe_w1"), 1, W, 0)
                        per, perc = TB * D / total, GH * HD / total
                        ch.go(v.tensor_scalar(st2[:, 0:1], mv2[:, 0:1], per, None, ALU.mult))
                        ch.go(v.tensor_scalar(st2[:, 1:2], e2[:, :], per, None, ALU.mult))
                        ch.go(v.tensor_scalar(st2c[:, 0:1], mvc[:, 0:1], perc, None, ALU.mult))
                        ch.wait()
                        v.tensor_scalar(st2c[:, 1:2], e2c[:, :], perc, None, ALU.mult).then_inc(s("dve_st2"), 1)
                        ch.end(11)
                    if P.ok and at == 46:
                        wait(dve, s("pe_cols"), 1, P, 1)
                        for k, dst in enumerate((fq, fk)):
                            v.tensor_scalar(dst[:, :, S:SEQ].rearrange("p c o -> p (c o)"), d2[:, D + 2 * k:D + 2 * k + 2],
                                            aq1[:, TB:TB + 1], w_fac[:, k:k + 1], ALU.mult, ALU.mult) \
                                .then_inc(s("dve_cc"), 1)
                        wait(dve, s("dve_cc"), 2, P, 2)
                        for dst, src in ((kbd, fk), (qbd, fq)):
                            v.tensor_tensor(dst[:, :, :], bd_mask, src[:, :, S:SEQ].broadcast_to([128, DC, VW]), ALU.mult) \
                                .then_inc(s("dve_bd"), 1)
                    if W.ok and at == 47:
                        wait(dve, s("pe_w1"), 1, W, 1)
                        signal(v.tensor_copy(ms2[:, :], d2[:, 0:2]), "dve_ms2", 1, W, 1)
                        ch = Link("dve_chain_v", 6, W)
                        ch(v.tensor_tensor(msq2[:, 0:1], ms2[:, 0:1], ms2[:, 0:1], ALU.mult))
                        v.scalar_tensor_tensor(msq2[:, 1:2], ms2[:, 1:2], EPS, msq2[:, 0:1], ALU.add, ALU.subtract) \
                            .then_inc(s("dve_ve2"), 1)
                        cflat = oc[:, :, :].rearrange("p j d -> p (j d)")
                        ch(v.tensor_scalar(cflat, cflat, ms2[0:NG, 0:1], None, ALU.subtract))
                        wait(dve, s("pool_amc"), 1, W, 0)
                        v.tensor_reduce(out=amc[:, :], in_=cflat, axis=AX.X, op=ALU.max, apply_absolute_value=True) \
                            .then_inc(s("dve_amc"), 1)
                    if W.ok and at == 48:
                        o = o_sb[:, W.par, :, :]
                        v.tensor_scalar(o, o, ms2[:, 0:1], None, ALU.subtract).then_inc(s("dve_om"), 1)
                    if W.ok and at == 49:
                        ch = Link("dve_chain_v", 6, W, 2)
                        wait(dve, s("dve_om"), 1, W, 1)
                        ch(v.tensor_reduce(out=am2[:, 0:TB], in_=o_sb[:, W.par, :, :], axis=AX.X, op=ALU.max,
                                           apply_absolute_value=True))
                    if W.ok and at == 50:
                        ch = Link("dve_chain_v", 6, W, 3)
                        wait(dve, s("pool_rs2"), 1, W, 1)
                        wait(dve, s("pool_amc"), 1, W, 1)
                        scales(ch, am2, ax2, rax2, comb2, aqo, rs2)
                        ch.end(6)
                        signal(v.tensor_scalar(aqo[:, :], ax2[:, :], 1.0 / 127.0, w_fac[:, 3:4], ALU.mult, ALU.mult),
                               "dve_aqo", 1, W, 1)
                    if W.ok and at == 52:
                        o = o_sb[:, W.par, :, :]
                        for t in range(TB):
                            v.tensor_scalar(o[:, t, :], o[:, t, :], comb2[:, t:t + 1], MAGIC, ALU.mult, ALU.add) \
                                .then_inc(s("dve_q2"), 1)
                        cflat = oc[:, :, :].rearrange("p j d -> p (j d)")
                        v.tensor_scalar(cflat, cflat, comb2[0:NG, TB:TB + 1], MAGIC, ALU.mult, ALU.add) \
                            .then_inc(s("dve_q2"), 1)
                    if P.ok and at == 50:
                        wait(dve, s("pe_t7"), 1, P, 1)
                        for k in range(2):
                            v.tensor_copy(scs[:, P.par, k * TB * NH:(k + 1) * TB * NH].rearrange("p (a t h) -> p a t h", a=2, h=NH),
                                          d2[:, 0:S // 2].rearrange("p (t k a h) -> p k a t h", t=2, k=2, a=2)[:, k, :, :, 0:NH]) \
                                .then_inc(s("dve_scs2"), 1)
                        wait(dve, s("dve_scs2"), 2, P, 2)
                        signal(v.tensor_copy(scs[:, P.par, 2 * TB * NH:(2 * TB + 1) * NH], d2[:, S // 2:S // 2 + NH]),
                               "dve_scs", 1, P, 1)
                    if P.ok and at == 52:
                        wait(dve, s("pool_par"), 1, P, 1)
                        both = scs[:, P.par, 2 * TB * NH:(2 * TB + 1) * NH]
                        ch = Link("dve_chain_q", 2, P)
                        ch(v.tensor_reduce(out=mc[:, :], in_=cmx[:, :].rearrange("p (t h) -> p h t", t=TB), axis=AX.X, op=ALU.max))
                        ch(v.tensor_tensor(mc[:, :], mc[:, :], both, ALU.max))
                        wait(dve, s("act_pc"), 1, P, 0)
                        v.tensor_tensor(pci[:, :, :], scs[:, P.par, TB * NH:(2 * TB + 1) * NH].rearrange("p (t h) -> p t h", h=NH),
                                        bcast(mc[:, :], 1, TB + 1), ALU.subtract).then_inc(s("dve_pci"), 1)
                        ch.end(2)
                    if W.ok and at in RESIDUAL_AT:
                        k = RESIDUAL_AT.index(at)
                        wait(dve, s("hw_in"), 16, W, 16)
                        for t in (2 * k, 2 * k + 1):
                            wait(dve, s("pe_y"), TB, W, t // 2 * 2 + 2)
                            v.scalar_tensor_tensor(hw[:, t, :], (d0, d1)[t // 2][:, D * (t % 2):D * (t % 2 + 1)],
                                                   aqo[:, t:t + 1], hw[:, t, :], ALU.mult, ALU.add) \
                                .then_inc(s("dve_h2"), 1)
                    if W.ok and at == 59:
                        wait(dve, s("pe_yc"), 1, W, 1)
                        wait(dve, s("h2c_stored"), 16, W, 0)
                        v.scalar_tensor_tensor(h2c[:, :], d2[0:1, 0:D], aqo[0:1, TB:TB + 1], cls_row[:, :], ALU.mult, ALU.add) \
                            .then_inc(s("dve_h2c"), 1)
                        wait(dve, s("dve_h2"), TB, W, 2)
                        token_stats(W, (0,), 128, hw, bn3, "dve_chain_n3", TB)
                    if W.ok and at in (60, 61):
                        if at == 60:
                            wait(dve, s("dve_h2"), TB, W, TB)
                        token_stats(W, (1, 2) if at == 60 else (3,), 128, hw, bn3, "dve_chain_n3", TB)
                    if W.ok and at == 61:
                        token_moments(W, 128, bn3, mv3, ve3, "dve_chain_n3", TB, "dve_ve3")
                    if W.ok and at == 63:
                        wait(dve, s("pool_r3"), 1, W, 1)
                        wait(dve, s("act_x2"), TB, W, 0)
                        v.scalar_tensor_tensor(nb3[:, :], mv3[:, :, 0], -1.0, rstd3[:, :], ALU.mult, ALU.mult) \
                            .then_inc(s("dve_nb3"), 1)
                    if u == UNITS - 1 and C.ok:
                        negate_maxima(C, g)
        if stage == STEPS:
            steps(dve, body)
        if stage == CLASS_TOKENS:
            n = images
            dve.wait_ge(s("cls_back"), 16)
            token_stats(one, (0,), n, hw, bn3, "dve_chain_n3_c", 1)
            token_moments(one, n, bn3, mv3, ve3, "dve_chain_n3_c", 1, "dve_ve3_c")
            dve.wait_ge(s("pool_r3_c"), 1)
            v.scalar_tensor_tensor(nb3[0:n, 0:1], mv3[0:n, 0:1, 0], -1.0, rstd3[0:n, 0:1], ALU.mult, ALU.mult) \
                .then_inc(s("dve_nb3_c"), 1)
            router(one, "_c", 1, n)
            weights(one, "_c", 1, n)
            payload(one, "_c", 1, n, cst[0:n, C_CROW:C_CROW + 1])
        if stage == TABLE:
            ch = Link("dve_chain_t", 0, one)
            c0 = cst[0:1, C_BASE:C_BASE + E]
            ch(v.tensor_tensor(ncnt[:, :], run[0:1, :], c0, ALU.subtract))
            ch(v.tensor_scalar(ntile[:, :], ncnt[:, :], 1.0 / 128, 127.0 / 256, ALU.mult, ALU.add))
            ch(v.tensor_scalar(ntile[:, :], ntile[:, :], MAGIC, -MAGIC, ALU.add, ALU.add))
            ch(v.tensor_copy(tend[:, :], ntile[:, :]))
            for e in range(1, E):
                ch(v.tensor_tensor(tend[:, e:e + 1], tend[:, e - 1:e], ntile[:, e:e + 1], ALU.add))
            ch(v.tensor_tensor(toff[:, :], tend[:, :], ntile[:, :], ALU.subtract))
            ch(v.scalar_tensor_tensor(toff[:, :], toff[:, :], -128.0, c0, ALU.mult, ALU.add))
            ch(v.tensor_tensor(tstep[:, 1:E], toff[:, 1:E], toff[:, 0:E - 1], ALU.subtract))
            idx = cst[0:1, C_BASE + E:C_BASE + E + tiles]
            ch(v.tensor_scalar(trow[:, :], idx, 128.0, toff[:, 0:1], ALU.mult, ALU.add))
            ch(v.tensor_scalar(texp[:, :], idx, 0.0, None, ALU.mult))
            for e in range(1, E):
                ch(v.tensor_scalar(tge[:, :], idx, tend[:, e - 1:e], None, ALU.is_ge))
                ch(v.tensor_tensor(texp[:, :], texp[:, :], tge[:, :], ALU.add))
                ch(v.scalar_tensor_tensor(trow[:, :], tge[:, :], tstep[:, e:e + 1], trow[:, :], ALU.mult, ALU.add))
            v.tensor_copy(tile_row[:, :], trow[:, :]).then_inc(s("table_set"), 1)
            v.tensor_copy(tile_expert[:, :], texp[:, :]).then_inc(s("table_set"), 1)

    for stage in (SETUP, STEPS):
        with nc.Block() as block:

            @block.sync
            def _(sp):
                sync_program(sp, stage)

            @block.tensor
            def _(pe):
                tensor_program(pe, stage)

            @block.scalar
            def _(act):
                scalar_program(act, stage)

            @block.gpsimd
            def _(pool):
                gpsimd_program(pool, stage)

            @block.vector
            def _(dve):
                vector_program(dve, stage)

        nc.clear_and_free_semaphores(list(sems.values()))
        nc.all_engine_barrier()
        sems.clear()
    ctx.close()
    stage = CLASS_TOKENS
    programs = [lambda eng, program=program: program(eng, CLASS_TOKENS) for program in
                (sync_program, tensor_program, scalar_program, gpsimd_program, vector_program)]
    return s, programs, lambda eng: vector_program(eng, TABLE)


class Tile:

    UNROLL = 8

    def __init__(self, k, n=None):
        self.k, self.n = k, n
        self.v = k if n is None else self.UNROLL * n + k

    def next(self, by):
        return Tile(self.k + by, self.n)

    def place(self, ring):
        return self.k % ring

    def laps(self, ring):
        return self.k // ring + 1 + (0 if self.n is None else self.UNROLL // ring * self.n)


def expert_phase(nc, ctx, images, gate_up_w, down_w, out, x2_dram, list_dram,
                 cst, tile_row, tile_expert, banks, class_sem, class_programs, table_program):
    tokens, cap, tiles, list_rows = geometry(images)
    sb = lambda name, shape, dt=F32: ctx.enter_context(nc.sbuf_tensor(name, shape, dt))
    sem = lambda name: ctx.enter_context(nc.semaphore(name))
    W = F * 2
    STAGES = 3
    LISTS, ROWS, AHEAD = 8, 4, 3
    gu = [sb(f"gu_{p}", [128, E, DC, W], BF16) for p in "hl"]
    dn = [sb(f"dn_{p}", [128, E, FC, D], BF16) for p in "hl"]
    gu_in = sb("gu_in", [128, STAGES, DC, W])
    dn_in = sb("dn_in", [128, STAGES, FC, D])
    ident = sb("ident", [128, 128])
    ids = sb("ids", [128, LISTS, 2], I32)
    xg = sb("xg", [128, ROWS, D])
    xh = sb("xh", [128, 2, DC, 128], BF16)
    xl = sb("xl", [128, 2, DC, 128], BF16)
    act_g = sb("act_g", [128, F])
    hid = sb("hid_e", [128, F])
    hh = sb("hh", [128, 2, FC, 128], BF16)
    hl = sb("hl", [128, 2, FC, 128], BF16)
    y_sb = sb("y_sb", [128, 2, D])
    w_in = [sem(f"w_in{k}") for k in range(STAGES)]
    w_high, w_low = sem("w_high"), sem("w_low")
    ids_in = [sem(f"ids_in{k}") for k in range(LISTS)]
    x_in = [sem(f"xg_in{k}") for k in range(ROWS)]
    pe_xt, act_xh, dve_xl = sem("pe_xt"), sem("act_xh_e"), sem("dve_xl")
    pe_g, pe_u, act_silu, dve_hid = sem("pe_g"), sem("pe_u"), sem("act_silu"), sem("dve_hid_e")
    pe_ht, act_hh, dve_hl, pe_y, act_y = sem("pe_ht"), sem("act_hh"), sem("dve_hl"), sem("pe_y_e"), sem("act_y")
    added, id_set, held = sem("added"), sem("id_set"), sem("held")
    gate_b, up_b = banks[0:2], banks[2:4]
    xt_b, ht_b, y_b = banks[4], banks[5], banks[6]
    block = ctx.enter_context(nc.Block())
    blk = lambda t: slice(t * 128, (t + 1) * 128)

    def over_tiles(eng, body):
        unroll = Tile.UNROLL
        for k in range(unroll):
            body(Tile(k), tiles)
        if tiles > 2 * unroll:
            with eng.Fori(1, tiles // unroll - 1) as n:
                for k in range(unroll):
                    body(Tile(k, n), None)
        for k in range(max(unroll, tiles - unroll), tiles):
            body(Tile(k), tiles)

    class_sync, class_tensor, class_scalar, class_gpsimd, class_vector = class_programs

    def has(i, n):
        return i.n is not None or 0 <= i.v < n

    def upto(eng, sem_, value):
        if not isinstance(value, int) or value > 0:
            eng.wait_ge(sem_, value)

    @block.sync
    def _(sp):
        for e in range(E):
            if e == STAGES:
                class_sync(sp)
            upto(sp, w_high, 2 * (e - STAGES + 1))
            upto(sp, w_low, 2 * (e - STAGES + 1))
            sp.dma_start(gu_in[:, e % STAGES, :, :], gate_up_w[e * D:(e + 1) * D, :].rearrange("(c p) n -> p c n", p=128)) \
                .then_inc(w_in[e % STAGES], 16)
            sp.dma_start(dn_in[:, e % STAGES, :, :], down_w[e * F:(e + 1) * F, :].rearrange("(c p) n -> p c n", p=128)) \
                .then_inc(w_in[e % STAGES], 16)
        sp.wait_ge(class_sem("table_set"), 2)
        sp.wait_ge(class_sem("scattered"), 32)

        def body(i, n):
            upto(sp, added, (i.v - LISTS + 1) * 16)
            sp.sem_inc(held, 1)
            first = sp.value_load(tile_row[0:1, bass.ds(i.v, 1)], min_val=0, max_val=list_rows - 128)
            k = i.place(LISTS)
            sp.dma_start(ids[:, k, :], list_dram[bass.ds(first, 128), :]).then_inc(ids_in[k], 16)
        over_tiles(sp, body)

    @block.gpsimd
    def _(pool):
        def rows(i):
            return bass.IndirectOffsetOnAxis(ap=ids[:, i.place(LISTS), 0:1], axis=0)

        def fetch(i):
            upto(pool, ids_in[i.place(LISTS)], i.laps(LISTS) * 16)
            upto(pool, pe_xt, i.v - ROWS + 1)
            pool.sem_inc(held, 1)
            nc.gpsimd.indirect_dma_start(out=xg[:, i.place(ROWS), :], out_offset=None, in_=x2_dram, in_offset=rows(i)) \
                .then_inc(x_in[i.place(ROWS)], 16)

        def body(i, n):
            if has(i.next(AHEAD), n):
                fetch(i.next(AHEAD))
            upto(pool, act_y, i.v + 1)
            upto(pool, added, i.v * 16)
            pool.sem_inc(held, 1)
            nc.gpsimd.indirect_dma_start(out=out, out_offset=rows(i), in_=y_sb[:, i.place(2), :], in_offset=None,
                                         bounds_check=tokens - 1, oob_is_err=False, compute_op=ALU.add) \
                .then_inc(added, 16)
        class_gpsimd(pool)
        pool.wait_ge(class_sem("x2c_stored"), 16)
        for k in range(AHEAD):
            fetch(Tile(k))
        over_tiles(pool, body)
        pool.wait_ge(added, 16 * tiles)

    @block.tensor
    def _(pe):
        mm = nc.tensor.matmul

        def transpose_x(i):
            upto(pe, x_in[i.place(ROWS)], i.laps(ROWS) * 16)
            upto(pe, act_xh, i.v)
            upto(pe, dve_xl, i.v)
            for c in range(DC):
                last = nc.tensor.transpose(xt_b[:, blk(c)], xg[:, i.place(ROWS), blk(c)], ident[:, :])
            last.then_inc(pe_xt, 1)

        def down(i):
            e = pe.value_load(tile_expert[0:1, bass.ds(i.v, 1)], min_val=0, max_val=E - 1)
            upto(pe, act_hh, i.v + 1)
            upto(pe, dve_hl, i.v + 1)
            upto(pe, act_y, i.v)
            n = 0
            for c in range(FC):
                for a, w in ((hh, dn[0]), (hh, dn[1]), (hl, dn[0])):
                    n += 1
                    last = mm(y_b[:, 0:D], a[:, i.place(2), c, :], w[:, bass.ds(e, 1), c, :],
                              start=(n == 1), stop=(n == 3 * FC))
            last.then_inc(pe_y, 1)

        def body(i, n):
            e = pe.value_load(tile_expert[0:1, bass.ds(i.v, 1)], min_val=0, max_val=E - 1)
            k = i.place(2)
            upto(pe, act_xh, i.v + 1)
            upto(pe, dve_xl, i.v + 1)
            upto(pe, dve_hid, i.v - 1)
            for bank, lo, done in ((gate_b, 0, pe_g), (up_b, F, pe_u)):
                m = 0
                for c in range(DC):
                    for a, w in ((xh, gu[0]), (xh, gu[1]), (xl, gu[0])):
                        m += 1
                        last = mm(bank[k][:, :], a[:, k, c, :], w[:, bass.ds(e, 1), c, lo:lo + F],
                                  start=(m == 1), stop=(m == 3 * DC))
                last.then_inc(done, 1)
            if has(i.next(1), n):
                transpose_x(i.next(1))
            if has(i.next(-1), n):
                down(i.next(-1))
            upto(pe, dve_hid, i.v + 1)
            upto(pe, act_hh, i.v)
            upto(pe, dve_hl, i.v)
            for c in range(FC):
                last = nc.tensor.transpose(ht_b[:, blk(c)], hid[:, blk(c)], ident[:, :])
            last.then_inc(pe_ht, 1)

        class_tensor(pe)
        pe.wait_ge(id_set, 1)
        pe.wait_ge(class_sem("table_set"), 2)
        transpose_x(Tile(0))
        pe.wait_ge(w_high, 2 * E)
        pe.wait_ge(w_low, 2 * E)
        over_tiles(pe, body)
        down(Tile(tiles - 1))

    @block.scalar
    def _(act):
        f = nc.scalar.activation
        class_scalar(act)
        for e in range(E):
            act.wait_ge(w_in[e % STAGES], 32 * (e // STAGES) + 32)
            f(gu[0][:, e, :, :], gu_in[:, e % STAGES, :, :], ACT.Copy).then_inc(w_high, 1)
            f(dn[0][:, e, :, :], dn_in[:, e % STAGES, :, :], ACT.Copy).then_inc(w_high, 1)

        def high_x(i):
            upto(act, pe_xt, i.v + 1)
            upto(act, pe_u, i.v - 1)
            f(xh[:, i.place(2), :, :], xt_b[:, 0:D].rearrange("p (c n) -> p c n", c=DC), ACT.Copy).then_inc(act_xh, 1)

        def take_y(i):
            upto(act, pe_y, i.v + 1)
            upto(act, added, (i.v - 1) * 16)
            f(y_sb[:, i.place(2), :], y_b[:, 0:D], ACT.Copy, scale=ids[:, i.place(LISTS), 1:2].bitcast(F32)).then_inc(act_y, 1)

        def body(i, n):
            upto(act, pe_g, i.v + 1)
            upto(act, dve_hid, i.v)
            f(act_g[:, :], gate_b[i.place(2)][:, :], ACT.Silu).then_inc(act_silu, 1)
            if has(i.next(1), n):
                high_x(i.next(1))
            if has(i.next(-1), n):
                take_y(i.next(-1))
            upto(act, pe_ht, i.v + 1)
            upto(act, pe_y, i.v - 1)
            f(hh[:, i.place(2), :, :], ht_b[:, :].rearrange("p (c n) -> p c n", c=FC), ACT.Copy).then_inc(act_hh, 1)
        high_x(Tile(0))
        over_tiles(act, body)
        take_y(Tile(tiles - 1))

    @block.vector
    def _(dve):
        v = nc.vector
        v.tensor_copy(ident[:, :], cst[:, C_ID:C_ID + 128]).then_inc(id_set, 1)
        class_vector(dve)
        for e in range(E):
            if e == STAGES:
                table_program(dve)
            for dst, src, m in ((gu, gu_in, 1), (dn, dn_in, 2)):
                dve.wait_ge(w_high, 2 * e + m)
                v.tensor_tensor(dst[1][:, e, :, :], src[:, e % STAGES, :, :], dst[0][:, e, :, :], ALU.subtract).then_inc(w_low, 1)

        def low_x(i):
            upto(dve, act_xh, i.v + 1)
            v.tensor_tensor(xl[:, i.place(2), :, :], xt_b[:, 0:D].rearrange("p (c n) -> p c n", c=DC),
                            xh[:, i.place(2), :, :], ALU.subtract).then_inc(dve_xl, 1)

        def body(i, n):
            upto(dve, act_silu, i.v + 1)
            upto(dve, pe_u, i.v + 1)
            upto(dve, pe_ht, i.v)
            v.tensor_tensor(hid[:, :], up_b[i.place(2)][:, :], act_g[:, :], ALU.mult).then_inc(dve_hid, 1)
            if has(i.next(1), n):
                low_x(i.next(1))
            upto(dve, act_hh, i.v + 1)
            v.tensor_tensor(hl[:, i.place(2), :, :], ht_b[:, :].rearrange("p (c n) -> p c n", c=FC),
                            hh[:, i.place(2), :, :], ALU.subtract).then_inc(dve_hl, 1)
        low_x(Tile(0))
        over_tiles(dve, body)


def kernel(x, cls_tok, L0_tok_W0, L0_tok_W1, L0_tok_Wo, L0_attn_w_q, L0_attn_w_k, L0_attn_w_v, L0_attn_w_o,
           L0_ffn_gate_w, L0_ffn_gate_up_w, L0_ffn_down_w):
    import numpy as np
    import concourse.bacc as bacc
    from concourse.bass_utils import run_bass_kernel_spmd

    images = x.shape[0]
    a = lambda t: np.ascontiguousarray(np.asarray(t))
    arrays = {
        "x_t": a(np.asarray(x)[:, :, :, 0].transpose(0, 2, 1)).reshape(images * D, S),
        "cls": a(cls_tok).reshape(1, D),
        "w0_t": a(np.asarray(L0_tok_W0).T),
        "w1_t": a(np.asarray(L0_tok_W1).T),
        "wo_t": a(np.asarray(L0_tok_Wo).T),
        "attn_w_t": a(np.stack([np.asarray(w).T for w in (L0_attn_w_q, L0_attn_w_k, L0_attn_w_v, L0_attn_w_o)])),
        "gate_w": a(L0_ffn_gate_w),
        "gate_up_w": a(L0_ffn_gate_up_w).reshape(E * D, 2 * F),
        "down_w": a(L0_ffn_down_w).reshape(E * F, D),
        "consts": constants(images),
    }
    nc = bacc.Bacc("TRN2", target_bir_lowering=False, num_devices=1)
    args = [nc.dram_tensor(n, t.shape, mybir.dt.from_np(t.dtype), kind="ExternalInput").ap() for n, t in arrays.items()]
    out = nc.dram_tensor("out", (images * SEQ, D), F32, kind="ExternalOutput").ap()
    vit_layer(nc, images, *args, out)
    r = run_bass_kernel_spmd(nc, [arrays], core_ids=[0])
    return r.results[0]["out"].reshape(images, SEQ, D)
```
